# Optimizing a Trainium2 kernel written in Bass

```python
import numpy as np
import jax
import jax.numpy as jnp

def _softmax(x, axis=-1):
    return jax.nn.softmax(x, axis=axis)

def _gelu(x):
    return jax.nn.gelu(x, approximate=True)

def _silu(x):
    return jax.nn.silu(x)

def _sigmoid(x):
    return jax.nn.sigmoid(x)

def _layernorm(x, axis=-1, eps=1e-05):
    m = jnp.mean(x, axis=axis, keepdims=True)
    v = jnp.var(x, axis=axis, keepdims=True)
    return (x - m) / jnp.sqrt(v + eps)

def _scatter_add(tgt, idx, src, axis=0):
    return tgt.at[idx].add(src)

def _segment_sum(src, seg, n):
    return jax.ops.segment_sum(src, seg, n)
kernel_name = 'mk_seq_postln_d1_jaxref_r8_49287e'

def setup_inputs(seed: int=0):
    np.random.seed(seed)
    _w = jnp.asarray

    def _L0_attn_setup():
        import jax, jax.numpy as jnp
        import numpy as np
        E2M1_GRID = jnp.array([0.0, 0.5, 1.0, 1.5, 2.0, 3.0, 4.0, 6.0], dtype=jnp.float32)
        E2M1_MIDS = (E2M1_GRID[1:] + E2M1_GRID[:-1]) / 2.0
        FP4_MAX = 6.0
        FP8_E4M3_MAX = 448.0

        def nvfp4_quant_dequant(w):
            O, I = w.shape
            w16 = w.reshape(O, I // 128, 8, 16)
            amax128 = jnp.max(jnp.abs(w16), axis=(-2, -1))
            outer = amax128 / (FP4_MAX * FP8_E4M3_MAX)
            outer = jnp.where(outer > 0, outer, 1.0)
            amax16 = jnp.max(jnp.abs(w16), axis=-1)
            inner = amax16 / FP4_MAX / outer[..., None]
            inner = inner.astype(jnp.float8_e4m3fn).astype(jnp.float32)
            scale = outer[..., None] * inner
            safe = jnp.where(scale > 0, scale, 1.0)[..., None]
            code = w16 / safe
            a = jnp.abs(code)
            idx = jnp.searchsorted(E2M1_MIDS, a)
            q = E2M1_GRID[idx] * jnp.sign(code)
            return (q * scale[..., None]).reshape(O, I)
        key = jax.random.key(seed)
        k0, k1, k2 = jax.random.split(key, 3)
        B, S, H = (2, 256, 256)
        hidden_states = jax.random.normal(k0, (B, S, H), dtype=jnp.float32)
        w_qkv = jax.random.normal(k1, (3 * H, H), dtype=jnp.float32) * 0.023
        w_o = jax.random.normal(k2, (H, H), dtype=jnp.float32) * 0.023
        w_qkv = nvfp4_quant_dequant(w_qkv)
        w_o = nvfp4_quant_dequant(w_o)
        return {'hidden_states': hidden_states, 'w_qkv': w_qkv, 'w_o': w_o}
    _L0_attn_in = _L0_attn_setup()

    def _L0_ffn_setup():
        import jax, jax.numpy as jnp
        import numpy as np
        NUM_EXPERTS = 16
        TOP_K = 2
        HIDDEN = 256
        D_FF = 512
        BATCH, SEQ = (4, 256)

        def _moe_forward(hidden, router_w, W1, W2):
            B, S, D = hidden.shape
            x = hidden.reshape(-1, D)
            T = x.shape[0]
            logits = x @ router_w
            top_vals, top_ids = jax.lax.top_k(logits, TOP_K)
            probs = jax.nn.softmax(top_vals, axis=-1)
            combine = jnp.zeros((T, NUM_EXPERTS), dtype=x.dtype)
            combine = combine.at[jnp.arange(T)[:, None], top_ids].add(probs)
            out = jnp.zeros_like(x)
            for e in range(NUM_EXPERTS):
                h = jax.nn.silu(x @ W1[e]) @ W2[e]
                out = out + combine[:, e:e + 1] * h
            return out.reshape(B, S, D)
        key = jax.random.key(seed)
        k_h, k_r, k_w1, k_w2 = jax.random.split(key, 4)
        hidden = jax.random.normal(k_h, (BATCH, SEQ, HIDDEN), dtype=jnp.float32)
        router_w = jax.random.normal(k_r, (HIDDEN, NUM_EXPERTS), dtype=jnp.float32) * HIDDEN ** (-0.5)
        W1 = jax.random.normal(k_w1, (NUM_EXPERTS, HIDDEN, D_FF), dtype=jnp.float32) * HIDDEN ** (-0.5)
        W2 = jax.random.normal(k_w2, (NUM_EXPERTS, D_FF, HIDDEN), dtype=jnp.float32) * D_FF ** (-0.5)
        return {'hidden': hidden, 'router_w': router_w, 'W1': W1, 'W2': W2}
    _L0_ffn_in = _L0_ffn_setup()
    _d = {'L0_attn_hidden_states': _L0_attn_in['hidden_states'], 'L0_attn_w_qkv': _L0_attn_in['w_qkv'], 'L0_attn_w_o': _L0_attn_in['w_o'], 'L0_ffn_router_w': _L0_ffn_in['router_w'], 'L0_ffn_W1': _L0_ffn_in['W1'], 'L0_ffn_W2': _L0_ffn_in['W2']}
    _x0 = _d['L0_attn_hidden_states']
    _d['L0_attn_hidden_states'] = jax.random.normal(jax.random.fold_in(jax.random.key(seed), 1), (4, 512, 256), dtype=_x0.dtype)
    del _x0
    return _d

def reference(L0_attn_hidden_states, L0_attn_w_qkv, L0_attn_w_o, L0_ffn_router_w, L0_ffn_W1, L0_ffn_W2):

    def _L0_attn_ref(hidden_states, w_qkv, w_o):
        import jax, jax.numpy as jnp
        import numpy as np
        E2M1_GRID = jnp.array([0.0, 0.5, 1.0, 1.5, 2.0, 3.0, 4.0, 6.0], dtype=jnp.float32)
        E2M1_MIDS = (E2M1_GRID[1:] + E2M1_GRID[:-1]) / 2.0
        FP4_MAX = 6.0
        FP8_E4M3_MAX = 448.0

        def nvfp4_quant_dequant(w):
            O, I = w.shape
            w16 = w.reshape(O, I // 128, 8, 16)
            amax128 = jnp.max(jnp.abs(w16), axis=(-2, -1))
            outer = amax128 / (FP4_MAX * FP8_E4M3_MAX)
            outer = jnp.where(outer > 0, outer, 1.0)
            amax16 = jnp.max(jnp.abs(w16), axis=-1)
            inner = amax16 / FP4_MAX / outer[..., None]
            inner = inner.astype(jnp.float8_e4m3fn).astype(jnp.float32)
            scale = outer[..., None] * inner
            safe = jnp.where(scale > 0, scale, 1.0)[..., None]
            code = w16 / safe
            a = jnp.abs(code)
            idx = jnp.searchsorted(E2M1_MIDS, a)
            q = E2M1_GRID[idx] * jnp.sign(code)
            return (q * scale[..., None]).reshape(O, I)
        B, S, H = hidden_states.shape
        num_heads = 16
        head_dim = H // num_heads
        qkv = jnp.einsum('bsh,oh->bso', hidden_states, w_qkv)
        qkv = qkv.reshape(B, S, 3, num_heads, head_dim)
        qkv = jnp.transpose(qkv, (2, 0, 3, 1, 4))
        q, k, v = (qkv[0], qkv[1], qkv[2])
        scale = 1.0 / jnp.sqrt(jnp.float32(head_dim))
        scores = jnp.einsum('bhqd,bhkd->bhqk', q, k) * scale
        causal = jnp.tril(jnp.ones((S, S), dtype=bool))
        scores = jnp.where(causal, scores, jnp.finfo(scores.dtype).min)
        probs = jax.nn.softmax(scores, axis=-1)
        attn = jnp.einsum('bhqk,bhkd->bhqd', probs, v)
        attn = jnp.transpose(attn, (0, 2, 1, 3)).reshape(B, S, H)
        return jnp.einsum('bsh,oh->bso', attn, w_o)

    def _L0_ffn_ref(hidden, router_w, W1, W2):
        import jax, jax.numpy as jnp
        import numpy as np
        NUM_EXPERTS = 16
        TOP_K = 2
        HIDDEN = 256
        D_FF = 512
        BATCH, SEQ = (4, 256)

        def _moe_forward(hidden, router_w, W1, W2):
            B, S, D = hidden.shape
            x = hidden.reshape(-1, D)
            T = x.shape[0]
            logits = x @ router_w
            top_vals, top_ids = jax.lax.top_k(logits, TOP_K)
            probs = jax.nn.softmax(top_vals, axis=-1)
            combine = jnp.zeros((T, NUM_EXPERTS), dtype=x.dtype)
            combine = combine.at[jnp.arange(T)[:, None], top_ids].add(probs)
            out = jnp.zeros_like(x)
            for e in range(NUM_EXPERTS):
                h = jax.nn.silu(x @ W1[e]) @ W2[e]
                out = out + combine[:, e:e + 1] * h
            return out.reshape(B, S, D)
        return _moe_forward(hidden, router_w, W1, W2)
    x = L0_attn_hidden_states
    x = _layernorm(x + _L0_attn_ref(x, L0_attn_w_qkv, L0_attn_w_o), axis=-1)
    x = _layernorm(x + _L0_ffn_ref(x, L0_ffn_router_w, L0_ffn_W1, L0_ffn_W2), axis=-1)
    return x

_drawn_inputs = setup_inputs


def setup_inputs(seed=0):
    import zlib

    import numpy as np

    out = dict(_drawn_inputs(seed))
    spreads = {}
    factors = {}
    for name, (base, spread) in spreads.items():
        noise = np.random.default_rng([zlib.crc32(name.encode()), seed]).standard_normal(out[name].shape)
        drawn = base * np.exp(spread * noise) if base else spread * noise
        out[name] = jnp.asarray(drawn.astype(out[name].dtype))
    for name, factor in factors.items():
        out[name] = (out[name] * factor).astype(out[name].dtype)
    return out
```

```python
from contextlib import ExitStack

import concourse.bass as bass
from concourse import mybir

P = 128
B, S, H = 4, 512, 256
NH, HD = 16, 16
T = B * S
TT = T // P
QT = S // P
KC = H // P
E, F = 16, 512
FC = F // P
TOPK = 2
MOE_TILES = (TOPK * T + E * (P - 1)) // P
SLOT_TILES = T // P + 1
EPS = 1e-5
NEG = -1.0e30

HALF = 8
TURNS = B * NH // HALF
PAIRS = HALF // 2
UNITS = 5
TU = PAIRS * UNITS
ROWS = 4 * HD
VW = 2 * HD + 1
LAG = 3
PRING = 5
SRING = 4

F32 = mybir.dt.float32
BF16 = mybir.dt.bfloat16
I32 = mybir.dt.int32
U32 = mybir.dt.uint32
ALU = mybir.AluOpType
ACT = mybir.ActivationFunctionType
X = mybir.AxisListType.X

SECOND = [[(0, 0, 0, 0)], [(0, 1, 128, 0), (0, 3, 384, 384)], [(0, 2, 256, 0), (1, 2, 256, 256)],
          [(1, 0, 0, 0)], [(1, 1, 128, 0), (1, 3, 384, 384)]]
FIRST = [[(0, 3, 0)], [(0, 2, 0), (0, 0, 384)], [(0, 1, 0), (1, 1, 256)], [(1, 3, 0)], [(1, 2, 0), (1, 0, 384)]]
W_SLOTS = 3


def post_norm_moe_layer(nc, x, xT, wqkvT, woT, router, W1, W2, out):
    ctx = ExitStack()
    with ctx:
        def sb(name, shape, dt):
            return ctx.enter_context(nc.sbuf_tensor(name, shape, dt))

        def sem(name):
            return ctx.enter_context(nc.semaphore(name))

        q_scr = nc.dram_tensor("q_scr", [TURNS, HALF, ROWS, S], BF16, kind="Internal").ap()
        k_scr = nc.dram_tensor("k_scr", [TURNS, HALF, ROWS, S], BF16, kind="Internal").ap()
        x1_scr = nc.dram_tensor("x1_scr", [T, 2 * H], BF16, kind="Internal").ap()
        slot_scr = nc.dram_tensor("slot_scr", [E * SLOT_TILES * P, 1], I32, kind="Internal").ap()
        y_scr = nc.dram_tensor("y_scr", [MOE_TILES * P, H], F32, kind="Internal").ap()

        w1 = sb("w1", [P, E, KC * 2 * F], BF16)
        w2 = sb("w2", [P, E, FC * 2 * H], BF16)
        ax = sb("ax", [P, T // P * H], F32)
        hold_v = sb("hold_v", [P, TURNS * QT * HALF * VW * 2 // 4], F32)
        hold_q = sb("hold_q", [P, 2048], F32)
        hold_w = sb("hold_w", [P, 3 * KC * F], F32)
        wqkv = sb("wqkv", [P, 2, KC, 3 * H], BF16)
        wo = sb("wo", [P, 2, KC, H], BF16)
        rout = sb("rout", [P, KC, E], F32)
        ident = sb("ident", [P, P], F32)
        identb = sb("identb", [P, P], BF16)
        maskb = sb("maskb", [P, 2 * P], BF16)
        before = sb("before", [P, P], BF16)
        onesb = sb("onesb", [P, P], BF16)
        pvs = sb("pvs", [P, 2, 2 * QT, VW], F32)
        onum = sb("onum", [P, 2 * QT, HD], F32)
        orec = sb("orec", [P, 2 * QT], F32)
        m8 = sb("m8", [P, 2, 2 * QT], F32)
        mrow = sb("mrow", [2 * QT, 2, 2, P], BF16)

        late = w2[:, E // 2:, :].rearrange("p e c -> p (e c)")
        xTs = late[:, 0:8192].rearrange("p (a c n) -> p a c n", a=2, c=KC)
        pf = late[:, 0:2 * PRING * 512].bitcast(F32).rearrange("p (r n) -> p r n", r=PRING)
        plo = late[:, 2 * PRING * 512:3 * PRING * 512].rearrange("p (r n) -> p r n", r=PRING)
        phi = late[:, 0:2 * PRING * 512].rearrange("p (r n two) -> p r n two", r=PRING, two=2)[:, :, :, 1]
        wstg = late[:, 8192:8192 + 4096].bitcast(F32)
        wqkv_f = wstg[:, 0:1536].rearrange("p (c n) -> p c n", c=KC)
        wo_f = wstg[:, 1536:2048].rearrange("p (c n) -> p c n", c=KC)
        kstk = late[:, 8192:8192 + 4096].rearrange("p (s h n) -> p s h n", s=PAIRS, h=2)
        ev = late[:, 12288:16384].rearrange("p (m a n) -> p m a n", m=4, a=2)
        qstk = hold_q[:, :].bitcast(BF16).rearrange("p (s h n) -> p s h n", s=PAIRS, h=2)
        xTf = ax[:, :].rearrange("p (c n) -> p c n", c=KC)
        at = ax[:, :].rearrange("p (u i n) -> p u i n", u=TURNS, i=QT)
        x1 = ax[:, :].rearrange("p (t n) -> p t n", t=TT)
        vst = hold_v[:, :].bitcast(BF16).rearrange("p (u k h c) -> p u k h c", u=TURNS, k=QT, h=HALF)
        wchunk = hold_w[:, :].rearrange("p (r n) -> p r n", r=3)

        aT = hold_v[:, 0:1024].bitcast(BF16).rearrange("p (a c n) -> p a c n", a=2, c=KC)
        xres = hold_v[:, 1024:2048].rearrange("p (i n) -> p i n", i=QT)
        r1 = hold_v[:, 2048:3072].rearrange("p (i n) -> p i n", i=QT)
        x1T = hold_v[:, 3072:4096].rearrange("p (c n) -> p c n", c=KC)
        x1hl = hold_q[:, 0:1024].bitcast(BF16).rearrange("p (i n) -> p i n", i=QT)
        xg = hold_q[:, 0:512].bitcast(BF16).rearrange("p (r n) -> p r n", r=2)
        xgT = hold_q[:, 512:1024].bitcast(BF16).rearrange("p (r n) -> p r n", r=2)
        ysb = hold_q[:, 1024:1536].rearrange("p (r n) -> p r n", r=2)
        hw = wqkv[:, :, :, :].rearrange("p a c n -> p (a c n)")
        hf = hw[:, 0:2048].bitcast(F32).rearrange("p (r n) -> p r n", r=2)
        hhi = hw[:, 0:2048].rearrange("p (r n two) -> p r n two", r=2, two=2)[:, :, :, 1]
        hlo = hw[:, 2048:3072].rearrange("p (r n) -> p r n", r=2)
        yg = hold_v[:, 0:4096].rearrange("p (r i k n) -> p r i k n", r=2, i=QT, k=2)
        fin = hold_w[:, 0:2048].rearrange("p (r i n) -> p r i n", r=2, i=QT)

        st = sb("st", [P, QT, 6], F32)
        mv = sb("mv", [P, QT, 2], F32)
        ve = sb("ve", [P, QT], F32)
        rstd = sb("rstd", [P, QT], F32)
        mhalf = sb("mhalf", [P, QT], F32)
        lg = sb("lg", [P, QT, E], F32)
        top = sb("top", [P, QT, 8], F32)
        topi = sb("topi", [P, QT, 8], U32)
        topf = sb("topf", [P, QT, 2], F32)
        hot = sb("hot", [P, TT, TOPK, E], F32)
        anyb = sb("anyb", [P, QT, E], BF16)
        excl = sb("excl", [P, QT, E], BF16)
        total = sb("total", [P, E], BF16)
        pree = sb("pree", [P, QT, E], F32)
        prod = sb("prod", [P, TT, TOPK, E], F32)
        posf = sb("posf", [P, TT, TOPK], F32)
        posu = sb("posu", [P, TT, TOPK], U32)
        gate = sb("gate", [P, TT, TOPK], F32)
        gtmp = sb("gtmp", [P, 2, QT], F32)
        e_i = sb("e_i", [P, E], I32)
        e_f = sb("e_f", [P, E], F32)
        eoff = sb("eoff", [P, E], F32)
        e128 = sb("e128", [P, E], F32)
        j_i = sb("j_i", [P, MOE_TILES + 1], I32)
        j_f = sb("j_f", [P, MOE_TILES + 1], F32)
        tok = sb("tok", [P, TT], I32)
        pcol_i = sb("pcol_i", [P, 1], I32)
        pcol = sb("pcol", [P, 1], F32)
        zero_i = sb("zero_i", [P, E * SLOT_TILES], I32)
        ones_f = sb("ones_f", [P, E], F32)
        cnt = sb("cnt", [P, E], F32)
        nt = sb("nt", [P, E], F32)
        binc = sb("binc", [P, E], F32)
        base = sb("base", [P, E], F32)
        delta = sb("delta", [P, E], F32)
        big = sb("big", [P, (MOE_TILES + 1) * E], F32)
        ef = sb("ef", [P, MOE_TILES + 1], F32)
        ei = sb("ei", [P, MOE_TILES + 1], I32)
        lep = sb("lep", [P, E], F32)
        used = sb("used", [P, E], F32)
        colf = sb("colf", [P, 4], F32)
        rowu = sb("rowu", [P, 1], U32)
        slots = sb("slots", [P, P], I32)
        slotf = sb("slotf", [P, P], F32)
        gidx = sb("gidx", [P, MOE_TILES + 1], U32)
        idx1 = sb("idx1", [P, 2], U32)
        idx2 = sb("idx2", [P, 2], U32)

        ps = ctx.enter_context(nc.psum_tensor("ps", [P, 8, 512], F32))
        S1B, S2B, PVB, MB = 0, 2, 6, 7

        ld_w, ld_x, ld_r, ld_x1 = sem("ld_w"), sem("ld_x"), sem("ld_r"), sem("ld_x1")
        cst = sem("cst")
        cst_v = sem("cst_v")
        zero_out = sem("zero_out")
        w_hi, w_lo, x_hi, x_lo = sem("w_hi"), sem("w_lo"), sem("x_hi"), sem("x_lo")
        qkv_rdy, qkv_hi, qkv_lo = sem("qkv_rdy"), sem("qkv_hi"), sem("qkv_lo")
        ev_out = [sem(f"ev_out{m}") for m in range(4)]
        stk_in = [sem(f"stk_in{k}") for k in range(PAIRS)]
        mrow_in = [sem(f"mrow_in{k}") for k in range(PAIRS)]
        s1_rdy, s1_max = sem("s1_rdy"), sem("s1_max")
        mT_rdy, m_hi, m_lo = sem("mT_rdy"), sem("m_hi"), sem("m_lo")
        s2_rdy, exp_done, sel_done, lo_done, pv_done = (sem("s2_rdy"), sem("exp_done"), sem("sel_done"),
                                                         sem("lo_done"), sem("pv_done"))
        pv_cp, nrm_step, nrm_done = sem("pv_cp"), sem("nrm_step"), sem("nrm_done")
        wch_in = [sem(f"wch_in{n}") for n in range(W_SLOTS)]
        wch_hi, wch_lo = sem("wch_hi"), sem("wch_lo")
        aT_rdy, aT_hi, aT_lo, op_rdy, res_done, ln_step = (sem("aT_rdy"), sem("aT_hi"), sem("aT_lo"),
                                                           sem("op_rdy"), sem("res_done"), sem("ln_step"))
        var_rdy, rstd_rdy, x1_rdy, x1_hi, x1_lo, x1_out = (sem("var_rdy"), sem("rstd_rdy"), sem("x1_rdy"),
                                                           sem("x1_hi"), sem("x1_lo"), sem("x1_out"))
        x1T_rdy, x1T_cp, lg_rdy, rt = sem("x1T_rdy"), sem("x1T_cp"), sem("lg_rdy"), sem("rt")
        any_rdy, pre_rdy, pos_rdy, gexp_in, gexp, gate_done = (sem("any_rdy"), sem("pre_rdy"), sem("pos_rdy"),
                                                               sem("gexp_in"), sem("gexp"), sem("gate_done"))
        scat = sem("scat")
        cnt_rdy, plan, row_rdy, slot_in, slotT_in, slotT, gidx_rdy, ei_rdy = (
            sem("cnt_rdy"), sem("plan"), sem("row_rdy"), sem("slot_in"), sem("slotT_in"), sem("slotT"),
            sem("gidx_rdy"), sem("ei_rdy"))
        i_cp, go = sem("i_cp"), sem("go")
        xg_in = [sem("xg_in0"), sem("xg_in1")]
        xgT_rdy, xgT_cp, h_rdy, h_act, h_lo, y_rdy, y_cp = (sem("xgT_rdy"), sem("xgT_cp"), sem("h_rdy"), sem("h_act"),
                                                            sem("h_lo"), sem("y_rdy"), sem("y_cp"))
        y_out = [sem("y_out0"), sem("y_out1")]
        i2_cp = sem("i2_cp")
        yg_in, f_step, fvar, fstd, fin_rdy, fin_out = ([sem("yg_in0"), sem("yg_in1")], sem("f_step"), sem("fvar"), sem("fstd"),
                                                       sem("fin_rdy"), [sem("fin_out0"), sem("fin_out1")])

        def w1_views(e, buf):
            return (W1[bass.ds(e, 1)].rearrange("e (c p) n -> p (e c) n", p=P),
                    wchunk[:, buf, :].rearrange("p (c n) -> p c n", n=F),
                    [w1[:, bass.ds(e, 1), :].rearrange("p e (c a n) -> p (e c) a n", a=2, n=F)[:, :, a, :] for a in (0, 1)])

        def w2_views(e, buf):
            return (W2[bass.ds(e, 1)].rearrange("e (c p) n -> p (e c) n", p=P),
                    wchunk[:, buf, :].rearrange("p (c n) -> p c n", n=H),
                    [w2[:, bass.ds(e, 1), :].rearrange("p e (c a n) -> p (e c) a n", a=2, n=H)[:, :, a, :] for a in (0, 1)])

        A_CHUNKS = W_SLOTS * TURNS
        ALL_CHUNKS = 2 * E
        assert A_CHUNKS == E + E // 2

        block = ctx.enter_context(nc.Block())

        @block.sync
        def _(sp):
            sp.dma_start(wqkv_f, wqkvT.rearrange("(c p) n -> p c n", p=P)).then_inc(ld_w, 16)
            sp.dma_start(wo_f, woT.rearrange("(c p) n -> p c n", p=P)).then_inc(ld_w, 16)
            for b in range(B):
                sp.dma_start(xTf[:, :, b * S:(b + 1) * S],
                             xT.rearrange("(c p) n -> p c n", p=P)[:, :, b * S:(b + 1) * S]).then_inc(ld_x, 16)
            sp.dma_start(rout[:, :, :], router.rearrange("(c p) n -> p c n", p=P)).then_inc(ld_r, 16)
            sp.wait_ge(cst, 1)
            sp.dma_start(slot_scr.rearrange("(p n) o -> p (n o)", p=P), zero_i[:, :]).then_inc(zero_out, 16)

            with sp.Fori(0, B) as b:
                for m in range(4):
                    scr = q_scr if m < 2 else k_scr
                    dst = scr[bass.ds(2 * b + m % 2, 1)].rearrange("u h (g d) t -> (u h) d g t", d=HD)
                    sp.wait_ge(qkv_lo, 6 * b + m + 1)
                    for g in range(4):
                        part = g // 2 if m < 2 else g % 2
                        sp.dma_start(dst[:, :, g, :], ev[:, m, part, :]).then_inc(ev_out[m], 16)

            def load_stack(u, k):
                sp.dma_start(qstk[0:ROWS, k, :, :],
                             q_scr[u, 2 * k:2 * k + 2].rearrange("h r t -> r h t")).then_inc(stk_in[k], 16)
                sp.dma_start(kstk[0:ROWS, k, :, :],
                             k_scr[u, 2 * k:2 * k + 2].rearrange("h r t -> r h t")).then_inc(stk_in[k], 16)

            def load_stack_dyn(u, k):
                for scr, stk in ((q_scr, qstk), (k_scr, kstk)):
                    sp.dma_start(stk[0:ROWS, k, :, :], scr[bass.ds(u, 1), 2 * k:2 * k + 2].rearrange(
                        "u h r t -> r (u h) t")).then_inc(stk_in[k], 16)

            def send_maxima(pair, k):
                sp.wait_ge(m_lo, pair + 1)
                for part in range(2):
                    sp.dma_start(qstk[ROWS + part:ROWS + part + 1, k, :, :].rearrange("o h (i q) -> o (h i) q", i=QT),
                                 mrow[:, k % 2, part, :]).then_inc(mrow_in[k], 16)

            for m in range(4):
                sp.wait_ge(ev_out[m], B * 64)
            for k in range(3):
                load_stack(0, k)
            send_maxima(0, 0)

            def turn(u, last):
                for k in range(PAIRS):
                    pair = PAIRS * u + k
                    if not (last and k > 0):
                        if k > 0:
                            sp.wait_ge(s2_rdy, UNITS * pair)
                            load_stack_dyn(u + 1, k - 1)
                        else:
                            if not isinstance(u, int) or u > 0:
                                sp.wait_ge(s2_rdy, UNITS * pair)
                            load_stack_dyn(u, PAIRS - 1)
                    if not (last and k == PAIRS - 1):
                        send_maxima(pair + 1, (k + 1) % PAIRS)

            turn(0, False)
            with sp.Fori(1, TURNS - 1) as u:
                turn(u, False)
            turn(TURNS - 1, True)

            with sp.Fori(0, B) as b:
                sp.wait_ge(nrm_done, PAIRS * TURNS)
                sp.wait_ge(res_done, 2 * b)
                sp.dma_start(xres, x[bass.ds(b * S, S), :].rearrange("(i p) n -> p i n", p=P)).then_inc(ld_x1, 16)
                sp.wait_ge(x1_lo, b + 1)
                sp.dma_start(x1_scr[bass.ds(b * S, S), :].rearrange("(i p) n -> p i n", p=P), x1hl).then_inc(x1_out, 16)

            with sp.Fori(0, MOE_TILES // 2) as jj:
                for k in range(2):
                    sp.wait_ge(y_cp, 2 * jj + k + 1)
                    sp.dma_start(y_scr[bass.ds((2 * jj + k) * P, P), :], ysb[:, k, :]).then_inc(y_out[k], 16)
            sp.wait_ge(y_cp, MOE_TILES)
            sp.dma_start(y_scr[(MOE_TILES - 1) * P:, :], ysb[:, 0, :]).then_inc(y_out[0], 16)

            for b in range(B):
                sp.wait_ge(fin_rdy, b + 1)
                sp.dma_start(out[b * S:(b + 1) * S, :].rearrange("(i p) n -> p i n", p=P),
                             fin[:, b % 2, :, :]).then_inc(fin_out[b % 2], 16)
            sp.wait_ge(fin_out[0], 32)
            sp.wait_ge(fin_out[1], 32)

        @block.gpsimd
        def _(pool):
            n = [0]

            def made(ins):
                ins.then_inc(cst, 1)
                n[0] += 1
                pool.wait_ge(cst, n[0])

            made(pool.memset(zero_i[:, :], 0))
            made(pool.memset(ident[:, :], 0.0))
            made(pool.affine_select(ident[:, :], ident[:, :], [[-1, P]], ALU.not_equal, 1.0, base=0, channel_multiplier=1))
            made(pool.tensor_copy(identb[:, :], ident[:, :]))
            made(pool.memset(onesb[:, :], 1.0))
            made(pool.memset(ones_f[:, :], 1.0))
            made(pool.memset(maskb[:, :], 0.0))
            made(pool.affine_select(maskb[:, :], maskb[:, :], [[0, 2], [-1, P]], ALU.is_ge, NEG, base=0, channel_multiplier=1))
            made(pool.affine_select(before[:, :], onesb[:, :], [[1, P]], ALU.is_gt, 0.0, base=0, channel_multiplier=-1))
            made(pool.iota(e_i[:, :], [[1, E]], base=0, channel_multiplier=0))
            made(pool.iota(j_i[:, :], [[1, MOE_TILES + 1]], base=0, channel_multiplier=0))
            made(pool.iota(tok[:, :], [[P, TT]], base=0, channel_multiplier=1))
            made(pool.iota(pcol_i[:, :], [[1, 1]], base=0, channel_multiplier=1))
            made(pool.memset(mhalf[:, :], -0.5))
            made(pool.memset(total[:, :], 0.0))
            made(pool.memset(vst.rearrange("p u k h c -> p (u k h) c")[:, :, 2 * HD:VW], 1.0))
            pool.wait_ge(w_lo, 2)
            made(pool.memset(kstk[ROWS:ROWS + 2, :, :, :], 1.0))

            def diagonal(u, slot, unit):
                cols = [c for _, _, _, c in SECOND[unit]]
                pool.wait_ge(exp_done, u + 1)
                pool.sem_inc(go, 1)
                if len(cols) == 1:
                    v, pat = pf[:, slot, 0:P], [[1, P]]
                else:
                    v = pf[:, slot, :].rearrange("p (b q) -> p b q", q=P)[:, 0:cols[1] // P + 1:cols[1] // P, :]
                    pat = [[0, 2], [1, P]]
                pool.affine_select(v, v, pat, ALU.is_ge, 0.0, base=0, channel_multiplier=-1).then_inc(sel_done, 1)

            def fetch(views, buf):
                src, stage, _ = views
                pool.dma_start(stage, src).then_inc(wch_in[buf], 16)

            def split(views, buf, c, turn):
                _, stage, (high, low) = views
                pool.wait_ge(wch_in[buf], 16 * (turn + 1))
                pool.tensor_copy(high, stage).then_inc(wch_hi, 1)
                pool.wait_ge(wch_hi, c + 1)
                pool.tensor_tensor(low, stage, high, ALU.subtract).then_inc(wch_lo, 1)

            fetch(w1_views(0, 0), 0)
            fetch(w1_views(1, 1), 1)
            fetch(w2_views(0, 2), 2)

            def turn(u, last):
                for k in range(PAIRS):
                    for unit in range(UNITS):
                        diagonal(TU * u + UNITS * k + unit, (UNITS * k + unit) % PRING, unit)
                    if k < W_SLOTS:
                        c = W_SLOTS * u + k
                        views = (lambda v: w1_views(2 * v + k, k)) if k < 2 else (lambda v: w2_views(v, k))
                        split(views(u), k, c, u)
                        if not last:
                            pool.wait_ge(wch_lo, c + 1)
                            fetch(views(u + 1), k)

            with pool.Fori(0, TURNS - 1) as u:
                turn(u, False)
            turn(TURNS - 1, True)
            pool.wait_ge(pv_done, TU * TURNS)
            late_e = list(range(E // 2, E))
            pool.wait_ge(wch_lo, A_CHUNKS)
            for n in range(W_SLOTS):
                fetch(w2_views(late_e[n], n), n)
            n = 0
            for b in range(B):
                pool.wait_ge(var_rdy, b + 1)
                pool.tensor_tensor(rstd[:, :], ve[:, :], mhalf[:, :], ALU.pow).then_inc(rstd_rdy, 1)
                for _ in range(2):
                    split(w2_views(late_e[n], n % W_SLOTS), n % W_SLOTS, A_CHUNKS + n, TURNS + n // W_SLOTS)
                    if n + W_SLOTS < len(late_e):
                        pool.wait_ge(wch_lo, A_CHUNKS + n + 1)
                        fetch(w2_views(late_e[n + W_SLOTS], n % W_SLOTS), n % W_SLOTS)
                    n += 1
                pool.wait_ge(pos_rdy, b + 1)
                if b == 0:
                    pool.wait_ge(zero_out, 16)
                for i in range(QT):
                    for k in range(TOPK):
                        t = QT * b + i
                        pool.indirect_dma_start(slot_scr, bass.IndirectOffsetOnAxis(ap=posu[:, t, k:k + 1], axis=0),
                                                tok[:, t:t + 1], None).then_inc(scat, 16)
            pool.wait_ge(row_rdy, 1)
            pool.wait_ge(scat, 16 * TT * TOPK)
            pool.indirect_dma_start(slots[0:MOE_TILES + 1, :], None, slot_scr.rearrange("(r n) o -> r (n o)", n=P),
                                    bass.IndirectOffsetOnAxis(ap=rowu[0:MOE_TILES + 1, 0:1], axis=0)).then_inc(slot_in, 16)
            pool.wait_ge(gidx_rdy, 1)
            pool.wait_ge(x1_out, 16 * B)

            def gather(j, k, first):
                if not first:
                    pool.wait_ge(xgT_rdy, j - 1)
                    pool.wait_ge(xg_in[k], 16 * (j // 2) if isinstance(j, int) else 8 * (j - k))
                pool.tensor_copy(idx1[:, k:k + 1], gidx[:, bass.ds(j, 1)]).then_inc(i_cp, 1)
                pool.wait_ge(i_cp, j + 1)
                pool.sem_inc(go, 1)
                pool.indirect_dma_start(xg[:, k, :], None, x1_scr,
                                        bass.IndirectOffsetOnAxis(ap=idx1[:, k:k + 1], axis=0)).then_inc(xg_in[k], 16)

            for k in range(2):
                gather(k, k, True)
            with pool.Fori(1, MOE_TILES // 2) as jj:
                for k in range(2):
                    gather(2 * jj + k, k, False)
            gather(MOE_TILES - 1, 0, False)

            pool.wait_ge(y_out[0], 16 * (MOE_TILES // 2 + 1))
            pool.wait_ge(y_out[1], 16 * (MOE_TILES // 2))
            for t in range(TT):
                if t == 2 * QT or t == 3 * QT:
                    pool.wait_ge(f_step, 6 * QT * (t // QT - 1))
                for k in range(TOPK):
                    pool.indirect_dma_start(yg[:, t // QT % 2, t % QT, k, :], None, y_scr,
                                            bass.IndirectOffsetOnAxis(ap=posu[:, t, k:k + 1], axis=0)).then_inc(yg_in[t // QT % 2], 16)

        @block.scalar
        def _(act):
            act.wait_ge(ld_w, 32)
            act.copy(wqkv[:, 0, :, :], wqkv_f).then_inc(w_hi, 1)
            act.copy(wo[:, 0, :, :], wo_f).then_inc(w_hi, 1)
            act.wait_ge(ld_x, 16 * B)
            for b in range(B):
                act.copy(xTs[:, 0, :, b * S:(b + 1) * S], xTf[:, :, b * S:(b + 1) * S]).then_inc(x_hi, 1)
            with act.Fori(0, B) as b:
                for m in range(4):
                    act.wait_ge(qkv_rdy, 6 * b + m + 1)
                    act.wait_ge(ev_out[m], 64 * b)
                    act.copy(ev[:, m, 0, :], ps[:, m, :]).then_inc(qkv_hi, 1)
                for v in range(2):
                    act.wait_ge(qkv_rdy, 6 * b + 4 + v + 1)
                    for i in range(2):
                        ins = act.copy(vst[:, bass.ds(2 * b, 2), 2 * v + i, :, 0:HD],
                                       ps[:, 4 + v, i * H:(i + 1) * H].rearrange("p (f h d) -> p f h d", f=2, d=HD))
                    ins.then_inc(qkv_hi, 1)

            def maxima_high(pair, k, wait_sent):
                act.wait_ge(mT_rdy, pair + 1)
                if wait_sent is not None:
                    act.wait_ge(mrow_in[(k - 2) % PAIRS], wait_sent)
                act.mul(mrow[:, k % 2, 0, :], ps[0:2 * QT, MB, 0:P], -1.0).then_inc(m_hi, 1)

            def pv_copy(pair, k):
                act.wait_ge(pv_done, UNITS * (pair + 1))
                if not (isinstance(pair, int) and pair < 2):
                    act.wait_ge(nrm_done, pair - 1)
                act.copy(pvs[:, k % 2, :, :], ps[:, PVB, 0:2 * QT * VW].rearrange("p (a c) -> p a c", c=VW)).then_inc(pv_cp, 1)

            maxima_high(0, 0, None)

            def turn(u, first, last):
                for k in range(PAIRS):
                    pair = PAIRS * u + k
                    for n in range(UNITS):
                        g = TU * u + UNITS * k + n
                        act.wait_ge(s2_rdy, g + 1)
                        if not (first and g < PRING):
                            act.wait_ge(pv_done, g - PRING + 1)
                        act.activation(pf[:, (UNITS * k + n) % PRING, :], ps[:, S2B + (UNITS * k + n) % SRING, :],
                                       ACT.Exp, scale=1.0 / HD ** 0.5).then_inc(exp_done, 1)
                        if n == 1 and not (last and k == PAIRS - 1):
                            kk = (k + 1) % PAIRS
                            sent = None if first and k == 0 else 32 * (u + (1 if k > 0 else 0)) if k < PAIRS - 1 else 32 * (u + 1)
                            maxima_high(pair + 1, kk, sent)
                        if n == LAG and not (first and k == 0):
                            pv_copy(pair - 1, (k - 1) % PAIRS)

            turn(0, True, False)
            with act.Fori(1, TURNS - 1) as u:
                turn(u, False, False)
            turn(TURNS - 1, False, True)
            pv_copy(PAIRS * TURNS - 1, PAIRS - 1)

            with act.Fori(0, B) as b:
                for c in range(KC):
                    act.wait_ge(aT_rdy, KC * b + c + 1)
                    act.wait_ge(op_rdy, 2 * b)
                    act.copy(aT[:, 0, c, :], ps[:, c, :]).then_inc(aT_hi, 1)
                act.wait_ge(x1_rdy, QT * (b + 1))
                act.wait_ge(x1_out, 16 * b)
                act.copy(x1hl[:, :, 0:H], x1[:, bass.ds(QT * b, QT), :]).then_inc(x1_hi, 1)
                for c in range(KC):
                    act.wait_ge(x1T_rdy, KC * b + c + 1)
                    act.wait_ge(lg_rdy, b)
                    act.copy(x1T[:, c, :], ps[:, 4 + c, :]).then_inc(x1T_cp, 1)
                act.wait_ge(gexp_in, b + 1)
                act.wait_ge(gate_done, b)
                act.activation(gtmp[:, 1, :], gtmp[:, 0, :], ACT.Exp).then_inc(gexp, 1)

            def expert_tile(j, k, free):
                act.wait_ge(h_rdy, j + 1)
                if free:
                    act.wait_ge(y_rdy, j - 1)
                act.activation(hf[:, k, :], ps[:, 2 + k, :], ACT.Silu).then_inc(h_act, 1)

            def result(j, k, free):
                act.wait_ge(y_rdy, j + 1)
                if free:
                    act.wait_ge(y_out[k], 8 * (j - k))
                act.copy(ysb[:, k, :], ps[:, 4 + k, 0:H]).then_inc(y_cp, 1)

            expert_tile(0, 0, False)
            expert_tile(1, 1, False)
            result(0, 0, False)
            expert_tile(2, 0, True)
            result(1, 1, False)
            with act.Fori(1, MOE_TILES // 2) as jj:
                expert_tile(2 * jj + 1, 1, True)
                result(2 * jj, 0, True)
                expert_tile(2 * jj + 2, 0, True)
                result(2 * jj + 1, 1, True)
            result(MOE_TILES - 1, 0, True)

            for b in range(B):
                act.wait_ge(fvar, b + 1)
                act.sqrt(rstd[:, :], ve[:, :]).then_inc(fstd, 1)

        @block.vector
        def _(dve):
            dve.wait_ge(w_hi, 1)
            dve.tensor_tensor(wqkv[:, 1, :, :], wqkv_f, wqkv[:, 0, :, :], ALU.subtract).then_inc(w_lo, 1)
            dve.wait_ge(w_hi, 2)
            dve.tensor_tensor(wo[:, 1, :, :], wo_f, wo[:, 0, :, :], ALU.subtract).then_inc(w_lo, 1)
            for b in range(B):
                dve.wait_ge(x_hi, b + 1)
                s = slice(b * S, (b + 1) * S)
                dve.tensor_tensor(xTs[:, 1, :, s], xTf[:, :, s], xTs[:, 0, :, s], ALU.subtract).then_inc(x_lo, 1)
            dve.wait_ge(cst, 16)
            dve.tensor_copy(e_f[:, :], e_i[:, :]).then_inc(cst_v, 1)
            dve.tensor_copy(j_f[:, :], j_i[:, :]).then_inc(cst_v, 1)
            dve.tensor_copy(pcol[:, :], pcol_i[:, :]).then_inc(cst_v, 1)
            dve.wait_ge(cst_v, 3)
            dve.tensor_scalar(eoff[:, :], e_f[:, :], float(SLOT_TILES * P), None, ALU.mult).then_inc(cst_v, 1)
            dve.tensor_scalar(e128[:, :], e_f[:, :], float(P), None, ALU.mult).then_inc(cst_v, 1)
            with dve.Fori(0, B) as b:
                for m in range(4):
                    dve.wait_ge(qkv_hi, 6 * b + m + 1)
                    dve.tensor_tensor(ev[:, m, 1, :], ps[:, m, :], ev[:, m, 0, :], ALU.subtract).then_inc(qkv_lo, 1)
                for v in range(2):
                    dve.wait_ge(qkv_hi, 6 * b + 4 + v + 1)
                    for i in range(2):
                        vs = vst[:, bass.ds(2 * b, 2), 2 * v + i, :, :]
                        ins = dve.tensor_tensor(vs[:, :, :, HD:2 * HD],
                                                ps[:, 4 + v, i * H:(i + 1) * H].rearrange("p (f h d) -> p f h d", f=2, d=HD),
                                                vs[:, :, :, 0:HD], ALU.subtract)
                    ins.then_inc(qkv_lo, 1)

            def unit_max(g, k, n, wait_m8):
                dve.wait_ge(s1_rdy, g + 1)
                if n == 0 and wait_m8 is not None:
                    dve.wait_ge(mT_rdy, wait_m8)
                bank = S1B + (UNITS * k + n) % 2
                m = m8[:, k % 2, :]
                if n == 2:
                    ins = dve.tensor_reduce(m.rearrange("p (h i) -> p h i", i=QT)[:, :, 1],
                                            ps[:, bank, :].rearrange("p (h n) -> p h n", h=2), X, ALU.max)
                else:
                    for h, i, c in FIRST[n]:
                        ins = dve.tensor_reduce(m[:, h * QT + i:h * QT + i + 1], ps[:, bank, c:c + (i + 1) * P], X, ALU.max)
                ins.then_inc(s1_max, 1)

            def maxima_low(pair, k):
                dve.wait_ge(m_hi, pair + 1)
                dve.scalar_tensor_tensor(mrow[:, k % 2, 1, :], ps[0:2 * QT, MB, 0:P], -1.0, mrow[:, k % 2, 0, :],
                                         ALU.mult, ALU.subtract).then_inc(m_lo, 1)

            def low_part(g, slot):
                dve.wait_ge(sel_done, g + 1)
                dve.tensor_tensor(plo[:, slot, :], pf[:, slot, :], phi[:, slot, :], ALU.subtract).then_inc(lo_done, 1)

            def normalise(pair, u, k):
                dve.wait_ge(pv_cp, pair + 1)
                if not (isinstance(pair, int) and pair == 0):
                    dve.wait_ge(nrm_done, pair)
                v = pvs[:, k % 2, :, :]
                dve.reciprocal(orec[:, :], v[:, :, 2 * HD]).then_inc(nrm_step, 1)
                dve.tensor_tensor(onum[:, :, :], v[:, :, 0:HD], v[:, :, HD:2 * HD], ALU.add).then_inc(nrm_step, 1)
                dve.wait_ge(nrm_step, 2 * pair + 2)
                dst = at[:, bass.ds(u, 1), :, 2 * k * HD:2 * (k + 1) * HD].rearrange("p u i (h d) -> p (u i) h d", d=HD)
                dve.tensor_tensor(dst, onum[:, :, :].rearrange("p (i h) d -> p i h d", h=2),
                                  orec[:, :].rearrange("p (i h) -> p i h", h=2).unsqueeze(3).to_broadcast([P, QT, 2, HD]),
                                  ALU.mult).then_inc(nrm_done, 1)

            for n in range(UNITS):
                unit_max(n, 0, n, None)
            maxima_low(0, 0)
            for n in range(UNITS):
                unit_max(UNITS + n, 1, n, None)

            def turn(u, first, last):
                for k in range(PAIRS):
                    pair = PAIRS * u + k
                    for n in range(UNITS):
                        g = TU * u + UNITS * k + n
                        if not (last and k >= 2):
                            unit_max(g + 2 * UNITS, (k + 2) % PAIRS, n, pair + 1)
                        if n == 2 and not (last and k == PAIRS - 1):
                            maxima_low(pair + 1, (k + 1) % PAIRS)
                        low_part(g, (UNITS * k + n) % PRING)
                        if n == UNITS - 1 and not (first and k == 0):
                            normalise(pair - 1, u if k > 0 else u - 1, (k - 1) % PAIRS)

            turn(0, True, False)
            with dve.Fori(1, TURNS - 1) as u:
                turn(u, False, False)
            turn(TURNS - 1, False, True)
            normalise(PAIRS * TURNS - 1, TURNS - 1, PAIRS - 1)

            def chain(ins, b):
                k[0] += 1
                ins.then_inc(rt, 1)
                dve.wait_ge(rt, CH * b + k[0])

            CH = 15
            for b in range(B):
                k = [0]
                for c in range(KC):
                    dve.wait_ge(aT_hi, KC * b + c + 1)
                    dve.tensor_tensor(aT[:, 1, c, :], ps[:, c, :], aT[:, 0, c, :], ALU.subtract).then_inc(aT_lo, 1)
                dve.wait_ge(ld_x1, 16 * (b + 1))
                for g in range(2):
                    dve.wait_ge(op_rdy, 2 * b + g + 1)
                    dve.tensor_tensor(r1[:, 2 * g:2 * g + 2, :], ps[:, 2 + g, :].rearrange("p (i n) -> p i n", i=2),
                                      xres[:, 2 * g:2 * g + 2, :], ALU.add).then_inc(res_done, 1)
                dve.wait_ge(res_done, 2 * b + 2)
                for i in range(QT):
                    dve.bn_stats(st[:, i, :], r1[:, i, :]).then_inc(ln_step, 1)
                for i in range(QT):
                    dve.wait_ge(ln_step, 2 * QT * b + i + 1)
                    dve.bn_aggr(mv[:, i, :], st[:, i, :]).then_inc(ln_step, 1)
                dve.wait_ge(ln_step, 2 * QT * (b + 1))
                dve.tensor_scalar(ve[:, :], mv[:, :, 1], EPS, None, ALU.add).then_inc(var_rdy, 1)
                dve.wait_ge(rstd_rdy, b + 1)
                for i in range(QT):
                    dve.tensor_scalar(x1[:, bass.ds(QT * b + i, 1), :].rearrange("p o n -> p (o n)"), r1[:, i, :],
                                      mv[:, i, 0:1], rstd[:, i:i + 1], ALU.subtract, ALU.mult).then_inc(x1_rdy, 1)
                dve.wait_ge(x1_hi, b + 1)
                dve.tensor_tensor(x1hl[:, :, H:2 * H], x1[:, bass.ds(QT * b, QT), :], x1hl[:, :, 0:H],
                                  ALU.subtract).then_inc(x1_lo, 1)
                dve.wait_ge(lg_rdy, b + 1)
                chain(dve.tensor_copy(lg[:, :, :], ps[:, 6, 0:QT * E].rearrange("p (i e) -> p i e", e=E)), b)
                for i in range(QT):
                    ins = dve.max(top[:, i, :], lg[:, i, :])
                chain(ins, b)
                for i in range(QT):
                    ins = dve.max_index(topi[:, i, :], top[:, i, :], lg[:, i, :])
                chain(ins, b)
                dve.tensor_tensor(gtmp[:, 0, :], top[:, :, 1], top[:, :, 0], ALU.subtract).then_inc(gexp_in, 1)
                chain(dve.tensor_copy(topf[:, :, :], topi[:, :, 0:2]), b)
                hb = hot[:, bass.ds(QT * b, QT), :, :]
                for i in range(TOPK):
                    ins = dve.tensor_tensor(hb[:, :, i, :], e_f[:, :].unsqueeze(1).to_broadcast([P, QT, E]),
                                            topf[:, :, i:i + 1].to_broadcast([P, QT, E]), ALU.is_equal)
                chain(ins, b)
                chain(dve.tensor_tensor(anyb[:, :, :], hb[:, :, 0, :], hb[:, :, 1, :], ALU.add), b)
                chain(dve.tensor_copy(excl[:, 0, :], total[:, :]), b)
                for i in range(1, QT):
                    chain(dve.tensor_tensor(excl[:, i, :], excl[:, i - 1, :], anyb[:, i - 1, :], ALU.add), b)
                dve.tensor_tensor(total[:, :], excl[:, QT - 1, :], anyb[:, QT - 1, :], ALU.add).then_inc(any_rdy, 1)
                dve.wait_ge(pre_rdy, b + 1)
                chain(dve.tensor_tensor(pree[:, :, :], ps[:, 7, 0:QT * E].rearrange("p (i e) -> p i e", e=E),
                                        eoff[:, :].unsqueeze(1).to_broadcast([P, QT, E]), ALU.add), b)
                for i in range(TOPK):
                    ins = dve.tensor_tensor(prod[:, 0:QT, i, :], hb[:, :, i, :], pree[:, :, :], ALU.mult)
                chain(ins, b)
                chain(dve.tensor_reduce(posf[:, bass.ds(QT * b, QT), :], prod[:, 0:QT, :, :], X, ALU.add), b)
                dve.tensor_copy(posu[:, bass.ds(QT * b, QT), :], posf[:, bass.ds(QT * b, QT), :]).then_inc(pos_rdy, 1)
                dve.wait_ge(gexp, b + 1)
                chain(dve.tensor_scalar(gtmp[:, 0, :], gtmp[:, 1, :], 1.0, None, ALU.add), b)
                chain(dve.reciprocal(gate[:, bass.ds(QT * b, QT), 0], gtmp[:, 0, :]), b)
                dve.tensor_tensor(gate[:, bass.ds(QT * b, QT), 1], gate[:, bass.ds(QT * b, QT), 0], gtmp[:, 1, :],
                                  ALU.mult).then_inc(gate_done, 1)
                assert k[0] == CH, k[0]

            kk = [0]

            def step(ins):
                kk[0] += 1
                ins.then_inc(plan, 1)
                dve.wait_ge(plan, kk[0])

            J = MOE_TILES + 1
            dve.wait_ge(cnt_rdy, 1)
            step(dve.tensor_copy(cnt[:, :], ps[:, 6, 0:E]))
            cmp = big[:, 0:E * E].rearrange("p (e m) -> p e m", m=E)
            step(dve.tensor_tensor(cmp, cnt[:, :].unsqueeze(2).to_broadcast([P, E, E]),
                                   e128[:, :].unsqueeze(1).to_broadcast([P, E, E]), ALU.is_gt))
            step(dve.tensor_reduce(nt[:, :], cmp, X, ALU.add))
            step(dve.tensor_tensor_scan(binc[:, :], ones_f[:, :], nt[:, :], 0.0, ALU.mult, ALU.add))
            step(dve.tensor_scalar(lep[:, :], binc[:, :], pcol[:, 0:1], None, ALU.is_le))
            dve.tensor_reduce(colf[:, 0:1], lep[:, :], X, ALU.add).then_inc(plan, 1)
            kk[0] += 1
            step(dve.tensor_tensor(used[:, :], lep[:, :], nt[:, :], ALU.mult))
            step(dve.tensor_reduce(colf[:, 1:2], used[:, :], X, ALU.add))
            step(dve.tensor_scalar(colf[:, 2:3], colf[:, 0:1], float(E - 1), float(SLOT_TILES), ALU.min, ALU.mult))
            step(dve.tensor_tensor(colf[:, 3:4], pcol[:, :], colf[:, 1:2], ALU.subtract))
            step(dve.tensor_scalar(colf[:, 3:4], colf[:, 3:4], float(SLOT_TILES - 1), None, ALU.min))
            dve.tensor_tensor(rowu[:, :], colf[:, 2:3], colf[:, 3:4], ALU.add).then_inc(row_rdy, 1)
            le = big[:, :].rearrange("p (j e) -> p j e", e=E)
            step(dve.tensor_tensor(le, binc[:, :].unsqueeze(1).to_broadcast([P, J, E]),
                                   j_f[:, :].unsqueeze(2).to_broadcast([P, J, E]), ALU.is_le))
            step(dve.tensor_reduce(ef[:, :], le, X, ALU.add))
            dve.tensor_scalar(ei[:, :], ef[:, :], float(E - 1), None, ALU.min).then_inc(ei_rdy, 1)
            step(dve.tensor_tensor(base[:, :], binc[:, :], nt[:, :], ALU.subtract))
            step(dve.scalar_tensor_tensor(delta[:, :], base[:, :], float(P), eoff[:, :], ALU.mult, ALU.subtract))
            step(dve.tensor_tensor(prod[:, :, :, :].rearrange("p t k e -> p (t k) e"),
                                   hot[:, :, :, :].rearrange("p t k e -> p (t k) e"),
                                   delta[:, :].unsqueeze(1).to_broadcast([P, TT * TOPK, E]), ALU.mult))
            pd = prod[:, :, :, :].rearrange("p t k e -> p (t k e)")[:, 0:1]
            tmp = big[:, 0:TT * TOPK]
            step(dve.tensor_reduce(tmp, prod[:, :, :, :].rearrange("p t k e -> p (t k) e"), X, ALU.add))
            dve.wait_ge(scat, 16 * TT * TOPK)
            step(dve.tensor_tensor(posu[:, :, :].rearrange("p t k -> p (t k)"), posf[:, :, :].rearrange("p t k -> p (t k)"),
                                   tmp, ALU.add))
            dve.wait_ge(slot_in, 16)
            dve.tensor_copy(slotf[0:J, :], slots[0:J, :]).then_inc(slotT_in, 1)
            dve.wait_ge(slotT, 1)
            dve.tensor_copy(gidx[:, :], ps[:, 7, 0:J]).then_inc(gidx_rdy, 1)

            def tokens(j, k, free):
                dve.wait_ge(xgT_rdy, j + 1)
                if free:
                    dve.wait_ge(h_rdy, j - 1)
                dve.tensor_copy(xgT[:, k, :], ps[:, k, 0:256].bitcast(BF16)).then_inc(xgT_cp, 1)

            def hidden(j, k):
                dve.wait_ge(h_act, j + 1)
                dve.tensor_tensor(hlo[:, k, :], hf[:, k, :], hhi[:, k, :], ALU.subtract).then_inc(h_lo, 1)

            tokens(0, 0, False)
            tokens(1, 1, False)
            hidden(0, 0)
            tokens(2, 0, True)
            with dve.Fori(0, MOE_TILES // 2 - 1) as jj:
                hidden(2 * jj + 1, 1)
                tokens(2 * jj + 3, 1, True)
                hidden(2 * jj + 2, 0)
                tokens(2 * jj + 4, 0, True)
            hidden(MOE_TILES - 2, 1)
            hidden(MOE_TILES - 1, 0)

            for b in range(B):
                f = fin[:, b % 2, :, :]
                if b >= 2:
                    dve.wait_ge(fin_out[b % 2], 16)
                dve.wait_ge(yg_in[b % 2], 16 * TOPK * QT * (b // 2 + 1))
                s0 = 6 * QT * b
                for i in range(QT):
                    t = QT * b + i
                    dve.scalar_tensor_tensor(f[:, i, :], yg[:, b % 2, i, 0, :], gate[:, t, 0:1], x1[:, t, :],
                                             ALU.mult, ALU.add).then_inc(f_step, 1)
                for i in range(QT):
                    t = QT * b + i
                    dve.wait_ge(f_step, s0 + i + 1)
                    dve.scalar_tensor_tensor(f[:, i, :], yg[:, b % 2, i, 1, :], gate[:, t, 1:2], f[:, i, :],
                                             ALU.mult, ALU.add).then_inc(f_step, 1)
                for i in range(QT):
                    dve.wait_ge(f_step, s0 + QT + i + 1)
                    dve.bn_stats(st[:, i, :], f[:, i, :]).then_inc(f_step, 1)
                for i in range(QT):
                    dve.wait_ge(f_step, s0 + 2 * QT + i + 1)
                    dve.bn_aggr(mv[:, i, :], st[:, i, :]).then_inc(f_step, 1)
                dve.wait_ge(f_step, s0 + 4 * QT)
                dve.tensor_scalar(ve[:, :], mv[:, :, 1], EPS, None, ALU.add).then_inc(fvar, 1)
                dve.wait_ge(fstd, b + 1)
                dve.reciprocal(rstd[:, :], rstd[:, :]).then_inc(f_step, QT)
                dve.wait_ge(f_step, s0 + 5 * QT)
                for i in range(QT):
                    ins = dve.tensor_scalar(f[:, i, :], f[:, i, :], mv[:, i, 0:1], rstd[:, i:i + 1],
                                            ALU.subtract, ALU.mult).then_inc(f_step, 1)
                dve.wait_ge(f_step, s0 + 6 * QT)
                dve.sem_inc(fin_rdy, 1)

        @block.tensor
        def _(pe):
            def three(dst, lhsT, rhs, first=True, last=True):
                terms = [(a, r, c) for c in range(KC) for a, r in ((0, 0), (0, 1), (1, 0))]
                for n, (a, r, c) in enumerate(terms):
                    ins = pe.matmul(dst, lhsT(a, c), rhs(r, c), start=(n == 0), stop=(n == len(terms) - 1))
                return ins

            pe.wait_ge(w_lo, 1)
            def project(b, first):
                pe.wait_ge(x_lo, b + 1)
                cols = bass.ds(b * S, S)
                for m in range(4):
                    if not first:
                        pe.wait_ge(qkv_lo, 6 * b + m - 5)
                    three(ps[:, m, :], lambda a, c: wqkv[:, a, c, m * P:(m + 1) * P],
                          lambda r, c: xTs[:, r, c, cols]).then_inc(qkv_rdy, 1)
                for v in range(2):
                    if not first:
                        pe.wait_ge(qkv_lo, 6 * b + 4 + v - 5)
                    for i in range(2):
                        ins = three(ps[:, 4 + v, i * H:(i + 1) * H],
                                    lambda a, c: xTs[:, a, c, bass.ds(b * S + (2 * v + i) * P, P)],
                                    lambda r, c: wqkv[:, r, c, 2 * H:3 * H])
                    ins.then_inc(qkv_rdy, 1)

            project(0, True)
            with pe.Fori(1, B) as b:
                project(b, False)

            pe.wait_ge(cst, 17)
            pe.wait_ge(qkv_lo, 6 * B)

            def first_pass(g, k, n, loaded):
                if loaded is not None and n == 0:
                    pe.wait_ge(stk_in[k], loaded)
                if not (isinstance(g, int) and g < 2):
                    pe.wait_ge(s1_max, g - 1)
                bank = ps[:, S1B + (UNITS * k + n) % 2, :]
                for h, i, c in FIRST[n]:
                    w = (i + 1) * P
                    pe.matmul(bank[:, c:c + w], qstk[0:ROWS, k, h, i * P:w], kstk[0:ROWS, k, h, 0:w], start=True, stop=False)
                    ins = pe.matmul(bank[:, c + i * P:c + w], identb[:, :], maskb[:, 0:P], start=False, stop=True)
                ins.then_inc(s1_rdy, 1)

            def second_pass(g, k, n):
                if not (isinstance(g, int) and g < SRING):
                    pe.wait_ge(exp_done, g - SRING + 1)
                bank = ps[:, S2B + (UNITS * k + n) % SRING, :]
                for h, kt, q, c in SECOND[n]:
                    ins = pe.matmul(bank[:, c:c + S - q], kstk[0:ROWS + 2, k, h, kt * P:(kt + 1) * P],
                                    qstk[0:ROWS + 2, k, h, q:S], start=True, stop=True)
                ins.then_inc(s2_rdy, 1)

            def transpose_maxima(pair, k):
                pe.wait_ge(s1_max, UNITS * (pair + 1))
                if not (isinstance(pair, int) and pair < 1):
                    pe.wait_ge(m_lo, pair)
                pe.transpose(ps[0:2 * QT, MB, 0:P], m8[:, k % 2, :], ident[:, :]).then_inc(mT_rdy, 1)

            def times_v(g, u, k, n):
                pe.wait_ge(lo_done, g + 1)
                if n == 0 and not (isinstance(g, int) and g == 0):
                    pe.wait_ge(pv_cp, PAIRS * u + k)
                slot = (UNITS * k + n) % PRING
                blocks = [(h, kt, q + c2 * P, c + c2 * P) for h, kt, q, c in SECOND[n] for c2 in range((S - q) // P)]
                for e, (h, kt, q, c) in enumerate(blocks):
                    o = (q // P * 2 + h) * VW
                    for p in (phi, plo):
                        ins = pe.matmul(ps[:, PVB, o:o + VW], p[:, slot, c:c + P],
                                        vst[:, bass.ds(u, 1), kt, 2 * k + h, :].rearrange("p o c -> p (o c)"),
                                        start=(n == 0 and e == 0 and p is phi),
                                        stop=(n == UNITS - 1 and e == len(blocks) - 1 and p is plo),
                                        skip_group_check=True)
                ins.then_inc(pv_done, 1)

            for n in range(UNITS):
                first_pass(n, 0, n, 32)
            transpose_maxima(0, 0)
            for n in range(UNITS):
                first_pass(UNITS + n, 1, n, 32)

            def turn(u, first, last):
                for k in range(PAIRS):
                    pair = PAIRS * u + k
                    for n in range(UNITS):
                        g = TU * u + UNITS * k + n
                        if n == 0:
                            pe.wait_ge(mrow_in[k], 32 * (u + 1))
                        second_pass(g, k, n)
                        if not (last and k >= 2):
                            first_pass(g + 2 * UNITS, (k + 2) % PAIRS, n, 32 * (u + (1 if k < 2 else 2)))
                        if n == 1 and not (last and k == PAIRS - 1):
                            transpose_maxima(pair + 1, (k + 1) % PAIRS)
                        back = UNITS * k + n - LAG
                        if back >= 0:
                            times_v(TU * u + back, u, back // UNITS, back % UNITS)
                        elif not first:
                            times_v(TU * u + back, u - 1, PAIRS - 1, back % UNITS)

            turn(0, True, False)
            with pe.Fori(1, TURNS - 1) as u:
                turn(u, False, False)
            turn(TURNS - 1, False, True)
            for back in range(TU - LAG, TU):
                times_v(TU * (TURNS - 1) + back, TURNS - 1, PAIRS - 1, back % UNITS)

            pe.wait_ge(nrm_done, PAIRS * TURNS)
            pe.wait_ge(ld_r, 16)
            pe.wait_ge(w_lo, 2)

            for b in range(B):
                for c in range(KC):
                    if b > 0:
                        pe.wait_ge(aT_lo, KC * b)
                    for i in range(QT):
                        ins = pe.transpose(ps[:, c, i * P:(i + 1) * P],
                                           at[:, 2 * b + c, i, :], ident[:, :])
                    ins.then_inc(aT_rdy, 1)
                pe.wait_ge(aT_lo, KC * (b + 1))
                pe.wait_ge(res_done, 2 * b)
                for g in range(2):
                    for i in range(2 * g, 2 * g + 2):
                        ins = three(ps[:, 2 + g, (i % 2) * H:(i % 2 + 1) * H],
                                    lambda a, c: aT[:, a, c, i * P:(i + 1) * P], lambda r, c: wo[:, r, c, :])
                    ins.then_inc(op_rdy, 1)
                pe.wait_ge(x1T_cp, KC * b)
                pe.wait_ge(x1_rdy, QT * (b + 1))
                for c in range(KC):
                    for i in range(QT):
                        ins = pe.transpose(ps[:, 4 + c, i * P:(i + 1) * P],
                                           x1[:, QT * b + i, c * P:(c + 1) * P],
                                           ident[:, :])
                    ins.then_inc(x1T_rdy, 1)
                pe.wait_ge(x1T_cp, KC * (b + 1))
                pe.wait_ge(gate_done, b)
                for i in range(QT):
                    for c in range(KC):
                        ins = pe.matmul(ps[:, 6, i * E:(i + 1) * E], x1T[:, c, i * P:(i + 1) * P], rout[:, c, :],
                                        start=(c == 0), stop=(c == KC - 1))
                ins.then_inc(lg_rdy, 1)
                pe.wait_ge(any_rdy, b + 1)
                pe.matmul(ps[:, 7, 0:QT * E], before[:, :], anyb[:, :, :].rearrange("p i e -> p (i e)"), start=True, stop=False)
                pe.matmul(ps[:, 7, 0:QT * E], onesb[:, :], excl[:, :, :].rearrange("p i e -> p (i e)"),
                          start=False, stop=True).then_inc(pre_rdy, 1)

            pe.wait_ge(gate_done, B)
            pe.matmul(ps[:, 6, 0:E], onesb[:, :], total[:, :], start=True, stop=True).then_inc(cnt_rdy, 1)
            J = MOE_TILES + 1
            pe.wait_ge(slotT_in, 1)
            pe.transpose(ps[:, 7, 0:J], slotf[0:J, :], ident[0:J, 0:J]).then_inc(slotT, 1)

            pe.wait_ge(wch_lo, ALL_CHUNKS)
            pe.wait_ge(ei_rdy, 1)

            def turn_tokens(j, k, free):
                pe.wait_ge(xg_in[k], 8 * (j - k) + 16)
                if free:
                    pe.wait_ge(xgT_cp, j - 1)
                for c in range(4):
                    ins = pe.transpose(ps[:, k, c * P // 2:(c + 1) * P // 2].bitcast(BF16), xg[:, k, c * P:(c + 1) * P], identb[:, :])
                ins.then_inc(xgT_rdy, 1)

            def through_w1(j, k, free):
                e = pe.value_load(ei[0:1, bass.ds(j, 1)], min_val=0, max_val=E - 1)
                pe.wait_ge(xgT_cp, j + 1)
                if free:
                    pe.wait_ge(h_act, j - 1)
                terms = [(a, r, c) for c in range(KC) for a, r in ((0, 0), (0, 1), (1, 0))]
                for f in range(FC):
                    for n, (a, r, c) in enumerate(terms):
                        o = (2 * c + a) * F + f * P
                        ins = pe.matmul(ps[:, 2 + k, f * P:(f + 1) * P],
                                        w1[:, bass.ds(e, 1), o:o + P].rearrange("p o n -> p (o n)"),
                                        xgT[:, k, (r * KC + c) * P:(r * KC + c + 1) * P],
                                        start=(n == 0), stop=(n == len(terms) - 1))
                ins.then_inc(h_rdy, 1)

            def through_w2(j, k, free):
                e = pe.value_load(ei[0:1, bass.ds(j, 1)], min_val=0, max_val=E - 1)
                pe.wait_ge(h_lo, j + 1)
                if free:
                    pe.wait_ge(y_cp, j - 1)
                terms = [(c, h, r) for c in range(FC) for h, r in ((hhi, 0), (hhi, 1), (hlo, 0))]
                for n, (c, h, r) in enumerate(terms):
                    o = (2 * c + r) * H
                    ins = pe.matmul(ps[:, 4 + k, 0:H], h[:, k, c * P:(c + 1) * P],
                                    w2[:, bass.ds(e, 1), o:o + H].rearrange("p o n -> p (o n)"),
                                    start=(n == 0), stop=(n == len(terms) - 1))
                ins.then_inc(y_rdy, 1)

            turn_tokens(0, 0, False)
            turn_tokens(1, 1, False)
            through_w1(0, 0, False)
            turn_tokens(2, 0, True)
            through_w1(1, 1, False)
            through_w2(0, 0, False)
            turn_tokens(3, 1, True)
            through_w1(2, 0, True)
            through_w2(1, 1, False)
            with pe.Fori(1, MOE_TILES // 2 - 1) as jj:
                turn_tokens(2 * jj + 2, 0, True)
                through_w1(2 * jj + 1, 1, True)
                through_w2(2 * jj, 0, True)
                turn_tokens(2 * jj + 3, 1, True)
                through_w1(2 * jj + 2, 0, True)
                through_w2(2 * jj + 1, 1, True)
            turn_tokens(MOE_TILES - 1, 0, True)
            through_w1(MOE_TILES - 2, 1, True)
            through_w2(MOE_TILES - 3, 0, True)
            through_w1(MOE_TILES - 1, 0, True)
            through_w2(MOE_TILES - 2, 1, True)
            through_w2(MOE_TILES - 1, 0, True)


def kernel(L0_attn_hidden_states, L0_attn_w_qkv, L0_attn_w_o, L0_ffn_router_w, L0_ffn_W1, L0_ffn_W2):
    import numpy as np
    import concourse.bacc as bacc
    from concourse.bass_utils import run_bass_kernel_spmd

    x = np.ascontiguousarray(L0_attn_hidden_states).reshape(T, H)
    arrays = {
        "x_dram": x,
        "xT_dram": np.ascontiguousarray(x.T),
        "wqkvT_dram": np.ascontiguousarray(np.asarray(L0_attn_w_qkv).T),
        "woT_dram": np.ascontiguousarray(np.asarray(L0_attn_w_o).T),
        "router_dram": np.ascontiguousarray(L0_ffn_router_w),
        "W1_dram": np.ascontiguousarray(L0_ffn_W1),
        "W2_dram": np.ascontiguousarray(L0_ffn_W2),
    }
    nc = bacc.Bacc("TRN2", target_bir_lowering=False, num_devices=1)
    args = [nc.dram_tensor(n, a.shape, mybir.dt.from_np(a.dtype), kind="ExternalInput").ap() for n, a in arrays.items()]
    out = nc.dram_tensor("out_dram", (T, H), F32, kind="ExternalOutput").ap()
    post_norm_moe_layer(nc, *args, out)
    r = run_bass_kernel_spmd(nc, [arrays], core_ids=[0])
    return r.results[0]["out_dram"].reshape(B, S, H)
```

```python
from contextlib import ExitStack

import concourse.bass as bass
from concourse import mybir

P = 128
B, S, H = 4, 512, 256
NH, HD = 16, 16
T = B * S
TT = T // P
QT = S // P
KC = H // P
E, F = 16, 512
FC = F // P
TOPK = 2
MOE_TILES = (TOPK * T + E * (P - 1)) // P
SLOT_TILES = T // P + 1
EPS = 1e-5
NEG = -1.0e30

HALF = 8
TURNS = B * NH // HALF
PAIRS = HALF // 2
UNITS = 5
TU = PAIRS * UNITS
ROWS = 4 * HD
MROW = 96
VW = 2 * HD + 1
FULL = (1, 4)
POOL_LOW = (2,)
DVE_LOW = (0, 3)
V_TILES = (1, 3)
LAG = 4
AHEAD = 12
SPLIT_AT = (0, 4)
LOW_LAG = 1
STEPS = 4
PRING = 5
SRING = 2

F32 = mybir.dt.float32
BF16 = mybir.dt.bfloat16
I32 = mybir.dt.int32
U32 = mybir.dt.uint32
ALU = mybir.AluOpType
ACT = mybir.ActivationFunctionType
X = mybir.AxisListType.X

SECOND = [[(0, 0, 0, 0)], [(0, 1, 128, 0), (0, 3, 384, 384)], [(0, 2, 256, 0), (1, 2, 256, 256)],
          [(1, 0, 0, 0)], [(1, 1, 128, 0), (1, 3, 384, 384)]]
FIRST = [[(0, 3, 0)], [(0, 2, 0), (0, 0, 384)], [(0, 1, 0), (1, 1, 256)], [(1, 3, 0)], [(1, 2, 0), (1, 0, 384)]]
W_SLOTS = 3


def post_norm_moe_layer(nc, x, xT, wqkvT, woT, router, W1, W2, out):
    ctx = ExitStack()
    with ctx:
        def sb(name, shape, dt):
            return ctx.enter_context(nc.sbuf_tensor(name, shape, dt))

        def sem(name):
            return ctx.enter_context(nc.semaphore(name))

        q_scr = nc.dram_tensor("q_scr", [TURNS, HALF, ROWS, S], BF16, kind="Internal").ap()
        k_scr = nc.dram_tensor("k_scr", [TURNS, HALF, ROWS, S], BF16, kind="Internal").ap()
        x1_scr = nc.dram_tensor("x1_scr", [T, 2 * H], BF16, kind="Internal").ap()
        slot_scr = nc.dram_tensor("slot_scr", [E * SLOT_TILES * P, 1], I32, kind="Internal").ap()
        y_scr = nc.dram_tensor("y_scr", [MOE_TILES * P, H], F32, kind="Internal").ap()

        w1 = sb("w1", [P, E, KC * 2 * F], BF16)
        w2 = sb("w2", [P, E, FC * 2 * H], BF16)
        ax = sb("ax", [P, T // P * H], F32)
        hold_v = sb("hold_v", [P, TURNS * QT * HALF * VW * 2 // 4], F32)
        hold_q = sb("hold_q", [P, 2048], F32)
        hold_w = sb("hold_w", [P, 3 * KC * F], F32)
        wqkv = sb("wqkv", [P, 2, KC, 3 * H], BF16)
        wo = sb("wo", [P, 2, KC, H], BF16)
        rout = sb("rout", [P, KC, E], F32)
        ident = sb("ident", [P, P], F32)
        identb = sb("identb", [P, P], BF16)
        maskb = sb("maskb", [P, 2 * P], BF16)
        before = sb("before", [P, P], BF16)
        onesb = sb("onesb", [P, P], BF16)
        v32 = sb("v32", [P, TURNS, len(V_TILES), HALF, HD + 1], F32)
        pvs = sb("pvs", [P, 2, 2 * QT, VW], F32)
        onum = sb("onum", [P, 2 * QT, HD], F32)
        orec = sb("orec", [P, 2 * QT], F32)
        m8 = sb("m8", [P, 2, 2 * QT], F32)
        mrow = sb("mrow", [2 * QT, 2, 2, P], BF16)

        late = w2[:, E // 2:, :].rearrange("p e c -> p (e c)")
        xTs = late[:, 0:8192].rearrange("p (a c n) -> p a c n", a=2, c=KC)
        pf = late[:, 0:2 * PRING * 512].bitcast(F32).rearrange("p (r n) -> p r n", r=PRING)
        plo = late[:, 2 * PRING * 512:3 * PRING * 512].rearrange("p (r n) -> p r n", r=PRING)
        phi = late[:, 0:2 * PRING * 512].rearrange("p (r n two) -> p r n two", r=PRING, two=2)[:, :, :, 1]
        wstg = late[:, 8192:8192 + 4096].bitcast(F32)
        wqkv_f = wstg[:, 0:1536].rearrange("p (c n) -> p c n", c=KC)
        wo_f = wstg[:, 1536:2048].rearrange("p (c n) -> p c n", c=KC)
        kstk = late[:, 8192:8192 + 4096].rearrange("p (s h n) -> p s h n", s=PAIRS, h=2)
        ev = late[:, 12288:16384].rearrange("p (m a n) -> p m a n", m=4, a=2)
        qstk = hold_q[:, :].bitcast(BF16).rearrange("p (s h n) -> p s h n", s=PAIRS, h=2)
        xTf = ax[:, :].rearrange("p (c n) -> p c n", c=KC)
        at = ax[:, :].rearrange("p (u i n) -> p u i n", u=TURNS, i=QT)
        x1 = ax[:, :].rearrange("p (t n) -> p t n", t=TT)
        vst = hold_v[:, :].bitcast(BF16).rearrange("p (u k h c) -> p u k h c", u=TURNS, k=QT, h=HALF)
        wchunk = hold_w[:, :].rearrange("p (r n) -> p r n", r=3)

        aT = hold_v[:, 0:1024].bitcast(BF16).rearrange("p (a c n) -> p a c n", a=2, c=KC)
        xres = hold_v[:, 1024:2048].rearrange("p (i n) -> p i n", i=QT)
        r1 = hold_v[:, 2048:3072].rearrange("p (i n) -> p i n", i=QT)
        x1T = hold_v[:, 3072:4096].rearrange("p (c n) -> p c n", c=KC)
        x1hl = hold_q[:, 0:1024].bitcast(BF16).rearrange("p (i n) -> p i n", i=QT)
        xg = hold_q[:, 0:512].bitcast(BF16).rearrange("p (r n) -> p r n", r=2)
        xgT = hold_q[:, 512:1024].bitcast(BF16).rearrange("p (r n) -> p r n", r=2)
        ysb = hold_q[:, 1024:1536].rearrange("p (r n) -> p r n", r=2)
        hw = wqkv[:, :, :, :].rearrange("p a c n -> p (a c n)")
        hf = hw[:, 0:2048].bitcast(F32).rearrange("p (r n) -> p r n", r=2)
        hhi = hw[:, 0:2048].rearrange("p (r n two) -> p r n two", r=2, two=2)[:, :, :, 1]
        hlo = hw[:, 2048:3072].rearrange("p (r n) -> p r n", r=2)
        yg = hold_v[:, 0:4096].rearrange("p (r i k n) -> p r i k n", r=2, i=QT, k=2)
        fin = hold_w[:, 0:2048].rearrange("p (r i n) -> p r i n", r=2, i=QT)

        st = sb("st", [P, QT, 6], F32)
        mv = sb("mv", [P, QT, 2], F32)
        ve = sb("ve", [P, QT], F32)
        rstd = sb("rstd", [P, QT], F32)
        mhalf = sb("mhalf", [P, QT], F32)
        lg = sb("lg", [P, QT, E], F32)
        top = sb("top", [P, QT, 8], F32)
        topi = sb("topi", [P, QT, 8], U32)
        topf = sb("topf", [P, QT, 2], F32)
        hot = hold_q[:, 1024:1536].rearrange("p (t k e) -> p t k e", t=TT, k=TOPK)
        anyb = sb("anyb", [P, QT, E], BF16)
        excl = sb("excl", [P, QT, E], BF16)
        total = sb("total", [P, E], BF16)
        pree = sb("pree", [P, QT, E], F32)
        prod = hold_q[:, 1536:2048].rearrange("p (t k e) -> p t k e", t=TT, k=TOPK)
        posf = sb("posf", [P, TT, TOPK], F32)
        posu = sb("posu", [P, TT, TOPK], U32)
        gate = sb("gate", [P, TT, TOPK], F32)
        gtmp = sb("gtmp", [P, 2, QT], F32)
        e_i = sb("e_i", [P, E], I32)
        e_f = sb("e_f", [P, E], F32)
        eoff = sb("eoff", [P, E], F32)
        e128 = sb("e128", [P, E], F32)
        j_i = sb("j_i", [P, MOE_TILES + 1], I32)
        j_f = sb("j_f", [P, MOE_TILES + 1], F32)
        tok = sb("tok", [P, TT], I32)
        pcol_i = sb("pcol_i", [P, 1], I32)
        pcol = sb("pcol", [P, 1], F32)
        zero_i = sb("zero_i", [P, E * SLOT_TILES], I32)
        ones_f = sb("ones_f", [P, E], F32)
        cnt = sb("cnt", [P, E], F32)
        nt = sb("nt", [P, E], F32)
        binc = sb("binc", [P, E], F32)
        base = sb("base", [P, E], F32)
        delta = sb("delta", [P, E], F32)
        big = hold_v[:, 3072:3072 + (MOE_TILES + 1) * E]
        ef = sb("ef", [P, MOE_TILES + 1], F32)
        ei = sb("ei", [P, MOE_TILES + 3], I32)
        lep = sb("lep", [P, E], F32)
        used = sb("used", [P, E], F32)
        colf = sb("colf", [P, 4], F32)
        rowu = sb("rowu", [P, 1], U32)
        slots = hold_v[:, 3840:3968].bitcast(I32)
        slotf = hold_v[:, 3968:4096]
        gidx = sb("gidx", [P, MOE_TILES + 1], U32)
        idx1 = sb("idx1", [P, 2], U32)
        idx2 = sb("idx2", [P, 2], U32)

        ps = ctx.enter_context(nc.psum_tensor("ps", [P, 8, 512], F32))
        S1B, S2B, PVB, MB = 0, 4, 6, 7

        ld_w, ld_r, ld_x1 = [sem("ld_w0"), sem("ld_w1")], sem("ld_r"), sem("ld_x1")
        ld_x = [sem(f"ld_xT{b}") for b in range(B)]
        cst = sem("cst")
        cst_v = sem("cst_v")
        zero_out = sem("zero_out")
        w_hi, w_lo, x_hi, x_lo = sem("w_hi"), sem("w_lo"), sem("x_hi"), sem("x_lo")
        qkv_rdy, qkv_hi, qkv_lo = sem("qkv_rdy"), sem("qkv_hi"), sem("qkv_lo")
        ev_out = [sem(f"ev_out{m}") for m in range(4)]
        stk_in = [sem(f"stk_in{k}") for k in range(PAIRS)]
        mrow_in = [sem(f"mrow_in{k}") for k in range(PAIRS)]
        s1_rdy, s1_max = sem("s1_rdy"), sem("s1_max")
        mT_rdy, m_hi, m_lo = sem("mT_rdy"), sem("m_hi"), sem("m_lo")
        s2_rdy, exp_done, sel_done, lo_done, pv_done = (sem("s2_rdy"), sem("exp_done"), sem("sel_done"),
                                                         sem("lo_done"), sem("pv_done"))
        lo_pool = sem("lo_pool")
        pv_cp, nrm_step, nrm_done = sem("pv_cp"), sem("nrm_step"), sem("nrm_done")
        wch_in = [sem(f"wch_in{n}") for n in range(W_SLOTS)]
        wch_hi, wch_lo = sem("wch_hi"), sem("wch_lo")
        aT_rdy, aT_hi, aT_lo, op_rdy, res_done, ln_step = (sem("aT_rdy"), sem("aT_hi"), sem("aT_lo"),
                                                           sem("op_rdy"), sem("res_done"), sem("ln_step"))
        var_rdy, rstd_rdy, x1_rdy, x1_hi, x1_lo, x1_out = (sem("var_rdy"), sem("rstd_rdy"), sem("x1_rdy"),
                                                           sem("x1_hi"), sem("x1_lo"), sem("x1_out"))
        x1T_rdy, x1T_cp, lg_rdy, rt = sem("x1T_rdy"), sem("x1T_cp"), sem("lg_rdy"), sem("rt")
        any_rdy, pre_rdy, pos_rdy, gexp_in, gexp, gate_done = (sem("any_rdy"), sem("pre_rdy"), sem("pos_rdy"),
                                                               sem("gexp_in"), sem("gexp"), sem("gate_done"))
        scat = sem("scat")
        cnt_rdy, plan, row_rdy, slot_in, slotT_in, slotT, gidx_rdy, ei_rdy = (
            sem("cnt_rdy"), sem("plan"), sem("row_rdy"), sem("slot_in"), sem("slotT_in"), sem("slotT"),
            sem("gidx_rdy"), sem("ei_rdy"))
        i_cp, go = sem("i_cp"), sem("go")
        xg_in = [sem("xg_in0"), sem("xg_in1")]
        xgT_rdy, xgT_cp, h_rdy, h_act, h_lo, y_rdy, y_cp = (sem("xgT_rdy"), sem("xgT_cp"), sem("h_rdy"), sem("h_act"),
                                                            sem("h_lo"), sem("y_rdy"), sem("y_cp"))
        y_out = [sem("y_out0"), sem("y_out1")]
        i2_cp = sem("i2_cp")
        yg_in, f_step, fvar, fstd, fin_rdy, fin_out = ([sem("yg_in0"), sem("yg_in1")], sem("f_step"), sem("fvar"), sem("fstd"),
                                                       sem("fin_rdy"), [sem("fin_out0"), sem("fin_out1")])

        def ahead(u, k, n):
            f = UNITS * k + n + AHEAD
            return u + f // TU, f // UNITS % PAIRS, f % UNITS, TU * u + f

        def w1_views(e, buf):
            return (W1[bass.ds(e, 1)].rearrange("e (c p) n -> p (e c) n", p=P),
                    wchunk[:, buf, :].rearrange("p (c n) -> p c n", n=F),
                    [w1[:, bass.ds(e, 1), :].rearrange("p e (c a n) -> p (e c) a n", a=2, n=F)[:, :, a, :] for a in (0, 1)])

        def w2_views(e, buf):
            return (W2[bass.ds(e, 1)].rearrange("e (c p) n -> p (e c) n", p=P),
                    wchunk[:, buf, :].rearrange("p (c n) -> p c n", n=H),
                    [w2[:, bass.ds(e, 1), :].rearrange("p e (c a n) -> p (e c) a n", a=2, n=H)[:, :, a, :] for a in (0, 1)])

        def matrix(turn, n):
            return w1_views(2 * turn + n, n) if n < 2 else w2_views(turn, n)

        A_CHUNKS = W_SLOTS * TURNS
        ALL_CHUNKS = 2 * E
        assert A_CHUNKS == E + E // 2

        block = ctx.enter_context(nc.Block())

        @block.sync
        def _(sp):
            def fetch(turn, n):
                src, stage, _ = matrix(turn, n)
                sp.dma_start(stage, src).then_inc(wch_in[n], 16)

            sp.dma_start(wqkv_f, wqkvT.rearrange("(c p) n -> p c n", p=P)).then_inc(ld_w[0], 16)
            for b in range(B):
                sp.dma_start(xTf[:, :, b * S:(b + 1) * S],
                             xT.rearrange("(c p) n -> p c n", p=P)[:, :, b * S:(b + 1) * S]).then_inc(ld_x[b], 16)
            sp.dma_start(wo_f, woT.rearrange("(c p) n -> p c n", p=P)).then_inc(ld_w[1], 16)
            sp.dma_start(rout[:, :, :], router.rearrange("(c p) n -> p c n", p=P)).then_inc(ld_r, 16)
            for n in range(W_SLOTS):
                fetch(0, n)
            sp.wait_ge(cst, 1)
            sp.dma_start(slot_scr.rearrange("(p n) o -> p (n o)", p=P), zero_i[:, :]).then_inc(zero_out, 16)

            with sp.Fori(0, B) as b:
                for m in range(4):
                    scr = q_scr if m < 2 else k_scr
                    order = "u h (d e a) t -> a (u h d) e t" if m >= 2 else "u h (d a e) t -> a (u h d) e t"
                    dst = scr[bass.ds(2 * b + m % 2, 1)].rearrange(order, d=HD, a=2)
                    sp.wait_ge(qkv_lo, 6 * b + m + 1)
                    for part in range(2):
                        sp.dma_start(dst[part], ev[:, m, part, :].unsqueeze(1).to_broadcast([P, 2, S])).then_inc(ev_out[m], 16)

            def load_stack(u, k):
                sp.dma_start(qstk[0:ROWS, k, :, :],
                             q_scr[u, 2 * k:2 * k + 2].rearrange("h r t -> r h t")).then_inc(stk_in[k], 16)
                sp.dma_start(kstk[0:ROWS, k, :, :],
                             k_scr[u, 2 * k:2 * k + 2].rearrange("h r t -> r h t")).then_inc(stk_in[k], 16)

            def load_stack_dyn(u, k):
                for scr, stk in ((q_scr, qstk), (k_scr, kstk)):
                    sp.dma_start(stk[0:ROWS, k, :, :], scr[bass.ds(u, 1), 2 * k:2 * k + 2].rearrange(
                        "u h r t -> r (u h) t")).then_inc(stk_in[k], 16)

            def send_maxima(pair, k):
                sp.wait_ge(m_lo, pair + 1)
                for part in range(2):
                    sp.dma_start(qstk[MROW + part:MROW + part + 1, k, :, :].rearrange("o h (i q) -> o (h i) q", i=QT),
                                 mrow[:, k % 2, part, :]).then_inc(mrow_in[k], 16)

            for m in range(4):
                sp.wait_ge(ev_out[m], B * 32)
            for k in range(3):
                load_stack(0, k)
            send_maxima(0, 0)

            def turn(u, first, last):
                for k in range(PAIRS):
                    pair = PAIRS * u + k
                    if not (last and k > 0):
                        if k > 0:
                            sp.wait_ge(s2_rdy, UNITS * pair)
                            load_stack_dyn(u + 1, k - 1)
                        else:
                            if not isinstance(u, int) or u > 0:
                                sp.wait_ge(s2_rdy, UNITS * pair)
                            load_stack_dyn(u, PAIRS - 1)
                    if not (last and k == PAIRS - 1):
                        send_maxima(pair + 1, (k + 1) % PAIRS)
                    if k >= 2 and not last:
                        sp.wait_ge(wch_lo, W_SLOTS * u + k - 1)
                        fetch(u + 1, k - 2)
                    elif k == 0 and not first:
                        sp.wait_ge(wch_lo, W_SLOTS * u)
                        fetch(u, W_SLOTS - 1)

            turn(0, True, False)
            with sp.Fori(1, TURNS - 1) as u:
                turn(u, False, False)
            turn(TURNS - 1, False, True)

            def late_fetch(n):
                if n < W_SLOTS:
                    sp.wait_ge(wch_lo, A_CHUNKS - W_SLOTS + n + 1)
                else:
                    sp.wait_ge(wch_lo, A_CHUNKS + n - W_SLOTS + 1)
                src, stage, _ = w2_views(E // 2 + n, n % W_SLOTS)
                sp.dma_start(stage, src).then_inc(wch_in[n % W_SLOTS], 16)

            def residual(b):
                if b > 0:
                    sp.wait_ge(res_done, 2 * b)
                sp.dma_start(xres, x[b * S:(b + 1) * S, :].rearrange("(i p) n -> p i n", p=P)).then_inc(ld_x1, 16)

            late_fetch(0)
            late_fetch(1)
            late_fetch(2)
            sp.wait_ge(nrm_done, PAIRS * TURNS)
            residual(0)
            for b in range(B):
                sp.wait_ge(x1_lo, b + 1)
                sp.dma_start(x1_scr[b * S:(b + 1) * S, :].rearrange("(i p) n -> p i n", p=P), x1hl).then_inc(x1_out, 16)
                if b + 1 < B:
                    residual(b + 1)
                for n in range(W_SLOTS + 2 * b, min(W_SLOTS + 2 * b + 2, E // 2)):
                    late_fetch(n)

            with sp.Fori(0, MOE_TILES // 2) as jj:
                for k in range(2):
                    sp.wait_ge(y_cp, 2 * jj + k + 1)
                    sp.dma_start(y_scr[bass.ds((2 * jj + k) * P, P), :], ysb[:, k, :]).then_inc(y_out[k], 16)
            sp.wait_ge(y_cp, MOE_TILES)
            sp.dma_start(y_scr[(MOE_TILES - 1) * P:, :], ysb[:, 0, :]).then_inc(y_out[0], 16)

            for b in range(B):
                sp.wait_ge(fin_rdy, b + 1)
                sp.dma_start(out[b * S:(b + 1) * S, :].rearrange("(i p) n -> p i n", p=P),
                             fin[:, b % 2, :, :]).then_inc(fin_out[b % 2], 16)
            sp.wait_ge(fin_out[0], 32)
            sp.wait_ge(fin_out[1], 32)

        @block.gpsimd
        def _(pool):
            n = [0]

            def made(ins):
                ins.then_inc(cst, 1)
                n[0] += 1
                pool.wait_ge(cst, n[0])

            made(pool.memset(zero_i[:, :], 0))
            made(pool.memset(ident[:, :], 0.0))
            made(pool.affine_select(ident[:, :], ident[:, :], [[-1, P]], ALU.not_equal, 1.0, base=0, channel_multiplier=1))
            made(pool.tensor_copy(identb[:, :], ident[:, :]))
            made(pool.memset(onesb[:, :], 1.0))
            made(pool.memset(ones_f[:, :], 1.0))
            made(pool.memset(maskb[:, :], 0.0))
            made(pool.affine_select(maskb[:, :], maskb[:, :], [[0, 2], [-1, P]], ALU.is_ge, NEG, base=0, channel_multiplier=1))
            made(pool.affine_select(before[:, :], onesb[:, :], [[1, P]], ALU.is_gt, 0.0, base=0, channel_multiplier=-1))
            made(pool.iota(e_i[:, :], [[1, E]], base=0, channel_multiplier=0))
            made(pool.iota(j_i[:, :], [[1, MOE_TILES + 1]], base=0, channel_multiplier=0))
            made(pool.iota(tok[:, :], [[P, TT]], base=0, channel_multiplier=1))
            made(pool.iota(pcol_i[:, :], [[1, 1]], base=0, channel_multiplier=1))
            made(pool.memset(mhalf[:, :], -0.5))
            made(pool.memset(total[:, :], 0.0))
            made(pool.memset(vst.rearrange("p u k h c -> p (u k h) c")[:, :, HD:HD + 1], 1.0))
            made(pool.memset(v32[:, :, :, :, :].rearrange("p u k h c -> p (u k h) c")[:, :, HD:HD + 1], 1.0))
            pool.wait_ge(w_lo, 2)
            made(pool.memset(kstk[ROWS:P, :, :, :], 0.0))
            made(pool.memset(kstk[MROW:MROW + 2, :, :, :], 1.0))
            made(pool.memset(qstk[ROWS:P, :, :, :], 0.0))

            def diagonal(u, slot, unit):
                cols = [c for _, _, _, c in SECOND[unit]]
                pool.wait_ge(exp_done, u + 1)
                pool.sem_inc(go, 1)
                if len(cols) == 1:
                    v, pat = pf[:, slot, 0:P], [[1, P]]
                else:
                    v = pf[:, slot, :].rearrange("p (b q) -> p b q", q=P)[:, 0:cols[1] // P + 1:cols[1] // P, :]
                    pat = [[0, 2], [1, P]]
                ins = pool.affine_select(v, v, pat, ALU.is_ge, 0.0, base=0, channel_multiplier=-1)
                ins.then_inc(sel_done, 1)

            def probabilities_low(u, slot, half):
                if half == 0:
                    pool.wait_ge(sel_done, u + 1)
                s = slice(256 * half, 256 * half + 256)
                pool.tensor_tensor(plo[:, slot, s], pf[:, slot, s], phi[:, slot, s], ALU.subtract).then_inc(lo_pool, 1)

            def split_low(views, c, halves=(0, 1)):
                _, stage, (high, low) = views
                mid = stage.shape[1] // 2
                pool.wait_ge(wch_hi, c + 1)
                s = slice(mid * halves[0], mid * (halves[-1] + 1))
                ins = pool.tensor_tensor(low[:, s], stage[:, s], high[:, s], ALU.subtract)
                if halves[-1] == 1:
                    ins.then_inc(wch_lo, 1)

            with pool.Fori(0, TURNS) as u:
                for k in range(PAIRS):
                    for unit in range(UNITS):
                        g = TU * u + UNITS * k + unit
                        diagonal(g, (UNITS * k + unit) % PRING, unit)
                        if unit in POOL_LOW:
                            probabilities_low(g, (UNITS * k + unit) % PRING, 0)
                        if unit - 1 in POOL_LOW:
                            probabilities_low(g - 1, (UNITS * k + unit - 1) % PRING, 1)
                        if k > 0 and unit in SPLIT_AT:
                            split_low(matrix(u, k - 1), W_SLOTS * u + k - 1, (SPLIT_AT.index(unit),))

            def late_low(n):
                split_low(w2_views(E // 2 + n, n % W_SLOTS), A_CHUNKS + n)

            def norm_factor(b):
                pool.wait_ge(var_rdy, b + 1)
                pool.tensor_tensor(rstd[:, :], ve[:, :], mhalf[:, :], ALU.pow).then_inc(rstd_rdy, 1)

            def place_tokens(b):
                pool.wait_ge(pos_rdy, b + 1)
                for i in range(QT):
                    for k in range(TOPK):
                        t = QT * b + i
                        pool.indirect_dma_start(slot_scr, bass.IndirectOffsetOnAxis(ap=posu[:, t, k:k + 1], axis=0),
                                                tok[:, t:t + 1], None).then_inc(scat, 16)

            pool.wait_ge(zero_out, 16)
            norm_factor(0)
            for b in range(B):
                for n in (2 * b, 2 * b + 1):
                    late_low(n)
                if b + 1 < B:
                    norm_factor(b + 1)
                place_tokens(b)
            pool.wait_ge(row_rdy, 1)
            pool.wait_ge(scat, 16 * TT * TOPK)
            pool.indirect_dma_start(slots[0:MOE_TILES + 1, :], None, slot_scr.rearrange("(r n) o -> r (n o)", n=P),
                                    bass.IndirectOffsetOnAxis(ap=rowu[0:MOE_TILES + 1, 0:1], axis=0)).then_inc(slot_in, 16)
            pool.wait_ge(gidx_rdy, 1)
            pool.wait_ge(x1_out, 16 * B)

            def gather(j, k, first):
                if not first:
                    pool.wait_ge(xgT_rdy, j - 1)
                    pool.wait_ge(xg_in[k], 16 * (j // 2) if isinstance(j, int) else 8 * (j - k))
                pool.tensor_copy(idx1[:, k:k + 1], gidx[:, bass.ds(j, 1)]).then_inc(i_cp, 1)
                pool.wait_ge(i_cp, j + 1)
                pool.sem_inc(go, 1)
                pool.indirect_dma_start(xg[:, k, :], None, x1_scr,
                                        bass.IndirectOffsetOnAxis(ap=idx1[:, k:k + 1], axis=0)).then_inc(xg_in[k], 16)

            for k in range(2):
                gather(k, k, True)
            with pool.Fori(1, MOE_TILES // 2) as jj:
                for k in range(2):
                    gather(2 * jj + k, k, False)
            gather(MOE_TILES - 1, 0, False)

            pool.wait_ge(y_out[0], 16 * (MOE_TILES // 2 + 1))
            pool.wait_ge(y_out[1], 16 * (MOE_TILES // 2))
            for t in range(TT):
                if t == 2 * QT or t == 3 * QT:
                    pool.wait_ge(f_step, 6 * QT * (t // QT - 1))
                for k in range(TOPK):
                    pool.indirect_dma_start(yg[:, t // QT % 2, t % QT, k, :], None, y_scr,
                                            bass.IndirectOffsetOnAxis(ap=posu[:, t, k:k + 1], axis=0)).then_inc(yg_in[t // QT % 2], 16)

        @block.scalar
        def _(act):
            act.wait_ge(ld_w[0], 16)
            act.copy(wqkv[:, 0, :, :], wqkv_f).then_inc(w_hi, 1)
            for b in range(B):
                if b == 1:
                    act.wait_ge(ld_w[1], 16)
                    act.copy(wo[:, 0, :, :], wo_f).then_inc(w_hi, 1)
                act.wait_ge(ld_x[b], 16)
                act.copy(xTs[:, 0, :, b * S:(b + 1) * S], xTf[:, :, b * S:(b + 1) * S]).then_inc(x_hi, 1)
            with act.Fori(0, B) as b:
                for m in range(4):
                    act.wait_ge(qkv_rdy, 6 * b + m + 1)
                    act.wait_ge(ev_out[m], 32 * b)
                    act.copy(ev[:, m, 0, :], ps[:, m, :]).then_inc(qkv_hi, 1)
                for v in range(2):
                    act.wait_ge(qkv_rdy, 6 * b + 4 + v + 1)
                    for i in range(2):
                        if 2 * v + i in V_TILES:
                            act.copy(v32[:, bass.ds(2 * b, 2), V_TILES.index(2 * v + i), :, 0:HD],
                                     ps[:, 4 + v, i * H:(i + 1) * H].rearrange("p (f h d) -> p f h d", f=2, d=HD))
                    for i in range(2):
                        ins = act.copy(vst[:, bass.ds(2 * b, 2), 2 * v + i, :, 0:HD],
                                       ps[:, 4 + v, i * H:(i + 1) * H].rearrange("p (f h d) -> p f h d", f=2, d=HD))
                    ins.then_inc(qkv_hi, 1)

            def maxima_high(pair, k, free):
                act.wait_ge(mT_rdy, pair + 1)
                if free is not None:
                    act.wait_ge(mrow_in[(k - 2) % PAIRS], free)
                act.mul(mrow[:, k % 2, 0, :], ps[0:2 * QT, MB, 0:P], -1.0).then_inc(m_hi, 1)

            def pv_copy(pair, k):
                act.wait_ge(pv_done, UNITS * (pair + 1))
                if not (isinstance(pair, int) and pair < 2):
                    act.wait_ge(nrm_done, pair - 1)
                act.copy(pvs[:, k % 2, :, :], ps[:, PVB, 0:2 * QT * VW].rearrange("p (a c) -> p a c", c=VW)).then_inc(pv_cp, 1)

            maxima_high(0, 0, None)
            maxima_high(1, 1, None)

            def turn(u, first, last):
                for k in range(PAIRS):
                    pair = PAIRS * u + k
                    for n in range(UNITS):
                        g = TU * u + UNITS * k + n
                        if n == LAG and not (first and k == 0):
                            pv_copy(pair - 1, (k - 1) % PAIRS)
                        act.wait_ge(s2_rdy, g + 1)
                        if not (first and g < PRING):
                            act.wait_ge(pv_done, g - PRING + 1)
                        act.activation(pf[:, (UNITS * k + n) % PRING, :], ps[:, S2B + (UNITS * k + n) % SRING, :],
                                       ACT.Exp, scale=1.0 / HD ** 0.5).then_inc(exp_done, 1)
                        if n == UNITS - 1 and not (last and k >= PAIRS - 2):
                            maxima_high(pair + 2, (k + 2) % PAIRS, 32 * (u + 1))
                    if k < W_SLOTS:
                        act.wait_ge(wch_in[k], 16 * (u + 1))
                        _, stage, (high, _) = matrix(u, k)
                        act.copy(high, stage).then_inc(wch_hi, 1)

            turn(0, True, False)
            with act.Fori(1, TURNS - 1) as u:
                turn(u, False, False)
            turn(TURNS - 1, False, True)
            pv_copy(PAIRS * TURNS - 1, PAIRS - 1)

            def attention_high(b):
                for c in range(KC):
                    act.wait_ge(aT_rdy, KC * b + c + 1)
                    act.wait_ge(op_rdy, 2 * b)
                    act.copy(aT[:, 0, c, :], ps[:, c, :]).then_inc(aT_hi, 1)

            attention_high(0)
            for b in range(B):
                act.wait_ge(x1_rdy, QT * (b + 1))
                if b > 0:
                    act.wait_ge(x1_out, 16 * b)
                act.copy(x1hl[:, :, 0:H], x1[:, QT * b:QT * (b + 1), :]).then_inc(x1_hi, 1)
                for c in range(KC):
                    act.wait_ge(x1T_rdy, KC * b + c + 1)
                    act.copy(x1T[:, c, :], ps[:, 4 + c, :]).then_inc(x1T_cp, 1)
                if b + 1 < B:
                    attention_high(b + 1)
                act.wait_ge(gexp_in, b + 1)
                act.activation(gtmp[:, 1, :], gtmp[:, 0, :], ACT.Exp).then_inc(gexp, 1)
                for n in (2 * b, 2 * b + 1):
                    act.wait_ge(wch_in[n % W_SLOTS], 16 * (TURNS + n // W_SLOTS + 1))
                    act.wait_ge(pv_done, TU * TURNS)
                    _, stage, (high, _) = w2_views(E // 2 + n, n % W_SLOTS)
                    act.copy(high, stage).then_inc(wch_hi, 1)

            def expert_tile(j, k, free):
                act.wait_ge(h_rdy, j + 1)
                if free:
                    act.wait_ge(y_rdy, j - 1)
                act.activation(hf[:, k, :], ps[:, 2 + k, :], ACT.Silu).then_inc(h_act, 1)

            def result(j, k, free):
                act.wait_ge(y_rdy, j + 1)
                if free:
                    act.wait_ge(y_out[k], 8 * (j - k))
                act.copy(ysb[:, k, :], ps[:, 4 + k, 0:H]).then_inc(y_cp, 1)

            expert_tile(0, 0, False)
            expert_tile(1, 1, False)
            result(0, 0, False)
            expert_tile(2, 0, True)
            result(1, 1, False)
            with act.Fori(1, MOE_TILES // 2) as jj:
                expert_tile(2 * jj + 1, 1, True)
                result(2 * jj, 0, True)
                expert_tile(2 * jj + 2, 0, True)
                result(2 * jj + 1, 1, True)
            result(MOE_TILES - 1, 0, True)

            for b in range(B):
                act.wait_ge(fvar, b + 1)
                act.sqrt(rstd[:, :], ve[:, :]).then_inc(fstd, 1)

        @block.vector
        def _(dve):
            dve.wait_ge(w_hi, 1)
            dve.tensor_tensor(wqkv[:, 1, :, :], wqkv_f, wqkv[:, 0, :, :], ALU.subtract).then_inc(w_lo, 1)
            for b in range(B):
                if b == 1:
                    dve.wait_ge(w_hi, 2)
                    dve.tensor_tensor(wo[:, 1, :, :], wo_f, wo[:, 0, :, :], ALU.subtract).then_inc(w_lo, 1)
                dve.wait_ge(x_hi, b + 1)
                s = slice(b * S, (b + 1) * S)
                dve.tensor_tensor(xTs[:, 1, :, s], xTf[:, :, s], xTs[:, 0, :, s], ALU.subtract).then_inc(x_lo, 1)
            dve.wait_ge(cst, 16)
            dve.tensor_copy(e_f[:, :], e_i[:, :]).then_inc(cst_v, 1)
            dve.tensor_copy(j_f[:, :], j_i[:, :]).then_inc(cst_v, 1)
            dve.tensor_copy(pcol[:, :], pcol_i[:, :]).then_inc(cst_v, 1)
            dve.wait_ge(cst_v, 3)
            dve.tensor_scalar(eoff[:, :], e_f[:, :], float(SLOT_TILES * P), None, ALU.mult).then_inc(cst_v, 1)
            dve.tensor_scalar(e128[:, :], e_f[:, :], float(P), None, ALU.mult).then_inc(cst_v, 1)
            with dve.Fori(0, B) as b:
                for m in range(4):
                    dve.wait_ge(qkv_hi, 6 * b + m + 1)
                    dve.tensor_tensor(ev[:, m, 1, :], ps[:, m, :], ev[:, m, 0, :], ALU.subtract).then_inc(qkv_lo, 1)
                for v in range(2):
                    dve.wait_ge(qkv_hi, 6 * b + 4 + v + 1)
                    for i in range(2):
                        vs = vst[:, bass.ds(2 * b, 2), 2 * v + i, :, :]
                        ins = dve.tensor_tensor(vs[:, :, :, HD + 1:VW],
                                                ps[:, 4 + v, i * H:(i + 1) * H].rearrange("p (f h d) -> p f h d", f=2, d=HD),
                                                vs[:, :, :, 0:HD], ALU.subtract)
                    ins.then_inc(qkv_lo, 1)

            def unit_max(g, k, n, wait_m8):
                dve.wait_ge(s1_rdy, g + 1)
                if n == 0 and wait_m8 is not None:
                    dve.wait_ge(mT_rdy, wait_m8)
                bank = S1B + (UNITS * k + n) % 4
                m = m8[:, k % 2, :]
                if n == 2:
                    ins = dve.tensor_reduce(m.rearrange("p (h i) -> p h i", i=QT)[:, :, 1],
                                            ps[:, bank, :].rearrange("p (h n) -> p h n", h=2), X, ALU.max)
                else:
                    for h, i, c in FIRST[n]:
                        ins = dve.tensor_reduce(m[:, h * QT + i:h * QT + i + 1], ps[:, bank, c:c + (i + 1) * P], X, ALU.max)
                ins.then_inc(s1_max, 1)

            def maxima_low(pair, k):
                dve.wait_ge(m_hi, pair + 1)
                dve.scalar_tensor_tensor(mrow[:, k % 2, 1, :], ps[0:2 * QT, MB, 0:P], -1.0, mrow[:, k % 2, 0, :],
                                         ALU.mult, ALU.subtract).then_inc(m_lo, 1)

            def low_part(g, slot):
                dve.wait_ge(sel_done, g + 1)
                dve.tensor_tensor(plo[:, slot, :], pf[:, slot, :], phi[:, slot, :], ALU.subtract).then_inc(lo_done, 1)

            def normalise(pair, u, k):
                dve.wait_ge(pv_cp, pair + 1)
                if not (isinstance(pair, int) and pair == 0):
                    dve.wait_ge(nrm_done, pair)
                v = pvs[:, k % 2, :, :]
                dve.reciprocal(orec[:, :], v[:, :, HD]).then_inc(nrm_step, 1)
                dve.tensor_tensor(onum[:, :, :], v[:, :, 0:HD], v[:, :, HD + 1:VW], ALU.add).then_inc(nrm_step, 1)
                dve.wait_ge(nrm_step, 2 * pair + 2)
                dst = at[:, bass.ds(u, 1), :, 2 * k * HD:2 * (k + 1) * HD].rearrange("p u i (h d) -> p (u i) h d", d=HD)
                dve.tensor_tensor(dst, onum[:, :, :].rearrange("p (i h) d -> p i h d", h=2),
                                  orec[:, :].rearrange("p (i h) -> p i h", h=2).unsqueeze(3).to_broadcast([P, QT, 2, HD]),
                                  ALU.mult).then_inc(nrm_done, 1)

            for f in range(AHEAD):
                unit_max(f, f // UNITS, f % UNITS, f // UNITS - 1 if f >= 2 * UNITS else None)
                if f == UNITS - 1:
                    maxima_low(0, 0)

            def turn(u, first, last):
                for k in range(PAIRS):
                    pair = PAIRS * u + k
                    for n in range(UNITS):
                        g = TU * u + UNITS * k + n
                        _, k1, n1, f = ahead(u, k, n)
                        if not (last and UNITS * k + n + AHEAD >= TU):
                            unit_max(f, k1, n1, pair + (n + AHEAD) // UNITS - 1)
                        if n == 0 and not (last and k == PAIRS - 1):
                            maxima_low(pair + 1, (k + 1) % PAIRS)
                        back = UNITS * k + n - LOW_LAG
                        if back % UNITS in DVE_LOW and not (first and back < 0):
                            low_part(TU * u + back, back % PRING)
                        if n == UNITS - 1 and not (first and k == 0):
                            normalise(pair - 1, u if k > 0 else u - 1, (k - 1) % PAIRS)

            turn(0, True, False)
            with dve.Fori(1, TURNS - 1) as u:
                turn(u, False, False)
            turn(TURNS - 1, False, True)
            for back in range(TU - LOW_LAG, TU):
                if back % UNITS in DVE_LOW:
                    low_part(TU * (TURNS - 1) + back, back % PRING)
            normalise(PAIRS * TURNS - 1, TURNS - 1, PAIRS - 1)

            kr = [0]

            def chain(ins):
                kr[0] += 1
                ins.then_inc(rt, 1)
                dve.wait_ge(rt, kr[0])

            def attention_low(b):
                for c in range(KC):
                    dve.wait_ge(aT_hi, KC * b + c + 1)
                    dve.tensor_tensor(aT[:, 1, c, :], ps[:, c, :], aT[:, 0, c, :], ALU.subtract).then_inc(aT_lo, 1)

            def residual(b):
                dve.wait_ge(ld_x1, 16 * (b + 1))
                for g in range(2):
                    dve.wait_ge(op_rdy, 2 * b + g + 1)
                    dve.tensor_tensor(r1[:, 2 * g:2 * g + 2, :], ps[:, 2 + g, :].rearrange("p (i n) -> p i n", i=2),
                                      xres[:, 2 * g:2 * g + 2, :], ALU.add).then_inc(res_done, 1)
                for i in range(QT):
                    if i % 2 == 0:
                        dve.wait_ge(res_done, 2 * b + i // 2 + 1)
                    dve.bn_stats(st[:, i, :], r1[:, i, :]).then_inc(ln_step, 1)
                for i in range(QT):
                    dve.wait_ge(ln_step, 2 * QT * b + i + 1)
                    dve.bn_aggr(mv[:, i, :], st[:, i, :]).then_inc(ln_step, 1)
                dve.wait_ge(ln_step, 2 * QT * (b + 1))
                dve.tensor_scalar(ve[:, :], mv[:, :, 1], EPS, None, ALU.add).then_inc(var_rdy, 1)

            attention_low(0)
            residual(0)
            for b in range(B):
                tiles = slice(QT * b, QT * (b + 1))
                dve.wait_ge(rstd_rdy, b + 1)
                for i in range(QT):
                    dve.tensor_scalar(x1[:, QT * b + i, :], r1[:, i, :], mv[:, i, 0:1], rstd[:, i:i + 1],
                                      ALU.subtract, ALU.mult).then_inc(x1_rdy, 1)
                dve.wait_ge(x1_hi, b + 1)
                dve.tensor_tensor(x1hl[:, :, H:2 * H], x1[:, tiles, :], x1hl[:, :, 0:H], ALU.subtract).then_inc(x1_lo, 1)
                if b + 1 < B:
                    attention_low(b + 1)
                dve.wait_ge(lg_rdy, b + 1)
                chain(dve.tensor_copy(lg[:, :, :], ps[:, 6, 0:QT * E].rearrange("p (i e) -> p i e", e=E)))
                for i in range(QT):
                    ins = dve.max(top[:, i, :], lg[:, i, :])
                chain(ins)
                if b > 0:
                    dve.wait_ge(gexp, b)
                dve.tensor_tensor(gtmp[:, 0, :], top[:, :, 1], top[:, :, 0], ALU.subtract).then_inc(gexp_in, 1)
                for i in range(QT):
                    ins = dve.max_index(topi[:, i, :], top[:, i, :], lg[:, i, :])
                chain(ins)
                chain(dve.tensor_copy(topf[:, :, :], topi[:, :, 0:2]))
                hb = hot[:, tiles, :, :]
                for i in range(TOPK):
                    ins = dve.tensor_tensor(hb[:, :, i, :], e_f[:, :].unsqueeze(1).to_broadcast([P, QT, E]),
                                            topf[:, :, i:i + 1].to_broadcast([P, QT, E]), ALU.is_equal)
                chain(ins)
                chain(dve.tensor_tensor(anyb[:, :, :], hb[:, :, 0, :], hb[:, :, 1, :], ALU.add))
                chain(dve.tensor_copy(excl[:, 0, :], total[:, :]))
                for i in range(1, QT):
                    chain(dve.tensor_tensor(excl[:, i, :], excl[:, i - 1, :], anyb[:, i - 1, :], ALU.add))
                dve.tensor_tensor(total[:, :], excl[:, QT - 1, :], anyb[:, QT - 1, :], ALU.add).then_inc(any_rdy, 1)
                if b + 1 < B:
                    residual(b + 1)
                dve.wait_ge(gexp, b + 1)
                chain(dve.tensor_scalar(gtmp[:, 0, :], gtmp[:, 1, :], 1.0, None, ALU.add))
                chain(dve.reciprocal(gate[:, tiles, 0], gtmp[:, 0, :]))
                dve.tensor_tensor(gate[:, tiles, 1], gate[:, tiles, 0], gtmp[:, 1, :], ALU.mult).then_inc(gate_done, 1)
                dve.wait_ge(pre_rdy, b + 1)
                chain(dve.tensor_tensor(pree[:, :, :], ps[:, 7, 0:QT * E].rearrange("p (i e) -> p i e", e=E),
                                        eoff[:, :].unsqueeze(1).to_broadcast([P, QT, E]), ALU.add))
                for i in range(TOPK):
                    ins = dve.tensor_tensor(prod[:, 0:QT, i, :], hb[:, :, i, :], pree[:, :, :], ALU.mult)
                chain(ins)
                chain(dve.tensor_reduce(posf[:, tiles, :], prod[:, 0:QT, :, :], X, ALU.add))
                dve.tensor_copy(posu[:, tiles, :], posf[:, tiles, :]).then_inc(pos_rdy, 1)

            kk = [0]

            def step(ins):
                kk[0] += 1
                ins.then_inc(plan, 1)
                dve.wait_ge(plan, kk[0])

            J = MOE_TILES + 1
            dve.wait_ge(cnt_rdy, 1)
            step(dve.tensor_copy(cnt[:, :], ps[:, 6, 0:E]))
            cmp = big[:, 0:E * E].rearrange("p (e m) -> p e m", m=E)
            step(dve.tensor_tensor(cmp, cnt[:, :].unsqueeze(2).to_broadcast([P, E, E]),
                                   e128[:, :].unsqueeze(1).to_broadcast([P, E, E]), ALU.is_gt))
            step(dve.tensor_reduce(nt[:, :], cmp, X, ALU.add))
            step(dve.tensor_tensor_scan(binc[:, :], ones_f[:, :], nt[:, :], 0.0, ALU.mult, ALU.add))
            step(dve.tensor_scalar(lep[:, :], binc[:, :], pcol[:, 0:1], None, ALU.is_le))
            dve.tensor_reduce(colf[:, 0:1], lep[:, :], X, ALU.add).then_inc(plan, 1)
            kk[0] += 1
            step(dve.tensor_tensor(used[:, :], lep[:, :], nt[:, :], ALU.mult))
            step(dve.tensor_reduce(colf[:, 1:2], used[:, :], X, ALU.add))
            step(dve.tensor_scalar(colf[:, 2:3], colf[:, 0:1], float(E - 1), float(SLOT_TILES), ALU.min, ALU.mult))
            step(dve.tensor_tensor(colf[:, 3:4], pcol[:, :], colf[:, 1:2], ALU.subtract))
            step(dve.tensor_scalar(colf[:, 3:4], colf[:, 3:4], float(SLOT_TILES - 1), None, ALU.min))
            dve.tensor_tensor(rowu[:, :], colf[:, 2:3], colf[:, 3:4], ALU.add).then_inc(row_rdy, 1)
            le = big[:, :].rearrange("p (j e) -> p j e", e=E)
            step(dve.tensor_tensor(le, binc[:, :].unsqueeze(1).to_broadcast([P, J, E]),
                                   j_f[:, :].unsqueeze(2).to_broadcast([P, J, E]), ALU.is_le))
            step(dve.tensor_reduce(ef[:, :], le, X, ALU.add))
            dve.tensor_scalar(ei[:, 2:], ef[:, :], float(E - 1), None, ALU.min).then_inc(ei_rdy, 1)
            step(dve.tensor_tensor(base[:, :], binc[:, :], nt[:, :], ALU.subtract))
            step(dve.scalar_tensor_tensor(delta[:, :], base[:, :], float(P), eoff[:, :], ALU.mult, ALU.subtract))
            step(dve.tensor_tensor(prod[:, :, :, :].rearrange("p t k e -> p (t k) e"),
                                   hot[:, :, :, :].rearrange("p t k e -> p (t k) e"),
                                   delta[:, :].unsqueeze(1).to_broadcast([P, TT * TOPK, E]), ALU.mult))
            pd = prod[:, :, :, :].rearrange("p t k e -> p (t k e)")[:, 0:1]
            tmp = big[:, 0:TT * TOPK]
            step(dve.tensor_reduce(tmp, prod[:, :, :, :].rearrange("p t k e -> p (t k) e"), X, ALU.add))
            dve.wait_ge(scat, 16 * TT * TOPK)
            step(dve.tensor_tensor(posu[:, :, :].rearrange("p t k -> p (t k)"), posf[:, :, :].rearrange("p t k -> p (t k)"),
                                   tmp, ALU.add))
            dve.wait_ge(slot_in, 16)
            dve.tensor_copy(slotf[0:J, :], slots[0:J, :]).then_inc(slotT_in, 1)
            dve.wait_ge(slotT, 1)
            dve.tensor_copy(gidx[:, :], ps[:, 7, 0:J]).then_inc(gidx_rdy, 1)

            def tokens(j, k, free):
                dve.wait_ge(xgT_rdy, j + 1)
                if free:
                    dve.wait_ge(h_rdy, j - 1)
                dve.tensor_copy(xgT[:, k, :], ps[:, k, 0:256].bitcast(BF16)).then_inc(xgT_cp, 1)

            def hidden(j, k):
                dve.wait_ge(h_act, j + 1)
                dve.tensor_tensor(hlo[:, k, :], hf[:, k, :], hhi[:, k, :], ALU.subtract).then_inc(h_lo, 1)

            tokens(0, 0, False)
            tokens(1, 1, False)
            hidden(0, 0)
            tokens(2, 0, True)
            with dve.Fori(0, MOE_TILES // 2 - 1) as jj:
                hidden(2 * jj + 1, 1)
                tokens(2 * jj + 3, 1, True)
                hidden(2 * jj + 2, 0)
                tokens(2 * jj + 4, 0, True)
            hidden(MOE_TILES - 2, 1)
            hidden(MOE_TILES - 1, 0)

            for b in range(B):
                f = fin[:, b % 2, :, :]
                if b >= 2:
                    dve.wait_ge(fin_out[b % 2], 16)
                dve.wait_ge(yg_in[b % 2], 16 * TOPK * QT * (b // 2 + 1))
                s0 = 6 * QT * b
                for i in range(QT):
                    t = QT * b + i
                    dve.scalar_tensor_tensor(f[:, i, :], yg[:, b % 2, i, 0, :], gate[:, t, 0:1], x1[:, t, :],
                                             ALU.mult, ALU.add).then_inc(f_step, 1)
                for i in range(QT):
                    t = QT * b + i
                    dve.wait_ge(f_step, s0 + i + 1)
                    dve.scalar_tensor_tensor(f[:, i, :], yg[:, b % 2, i, 1, :], gate[:, t, 1:2], f[:, i, :],
                                             ALU.mult, ALU.add).then_inc(f_step, 1)
                for i in range(QT):
                    dve.wait_ge(f_step, s0 + QT + i + 1)
                    dve.bn_stats(st[:, i, :], f[:, i, :]).then_inc(f_step, 1)
                for i in range(QT):
                    dve.wait_ge(f_step, s0 + 2 * QT + i + 1)
                    dve.bn_aggr(mv[:, i, :], st[:, i, :]).then_inc(f_step, 1)
                dve.wait_ge(f_step, s0 + 4 * QT)
                dve.tensor_scalar(ve[:, :], mv[:, :, 1], EPS, None, ALU.add).then_inc(fvar, 1)
                dve.wait_ge(fstd, b + 1)
                dve.reciprocal(rstd[:, :], rstd[:, :]).then_inc(f_step, QT)
                dve.wait_ge(f_step, s0 + 5 * QT)
                for i in range(QT):
                    ins = dve.tensor_scalar(f[:, i, :], f[:, i, :], mv[:, i, 0:1], rstd[:, i:i + 1],
                                            ALU.subtract, ALU.mult).then_inc(f_step, 1)
                dve.wait_ge(f_step, s0 + 6 * QT)
                dve.sem_inc(fin_rdy, 1)

        @block.tensor
        def _(pe):
            def three(dst, lhsT, rhs, first=True, last=True):
                terms = [(a, r, c) for c in range(KC) for a, r in ((0, 0), (0, 1), (1, 0))]
                for n, (a, r, c) in enumerate(terms):
                    ins = pe.matmul(dst, lhsT(a, c), rhs(r, c), start=(n == 0), stop=(n == len(terms) - 1))
                return ins

            pe.wait_ge(w_lo, 1)
            def project(b, first):
                pe.wait_ge(x_lo, b + 1)
                cols = bass.ds(b * S, S)
                for m in range(4):
                    if not first:
                        pe.wait_ge(qkv_lo, 6 * b + m - 5)
                    three(ps[:, m, :], lambda a, c: wqkv[:, a, c, m * P:(m + 1) * P],
                          lambda r, c: xTs[:, r, c, cols]).then_inc(qkv_rdy, 1)
                for v in range(2):
                    if not first:
                        pe.wait_ge(qkv_lo, 6 * b + 4 + v - 5)
                    for i in range(2):
                        ins = three(ps[:, 4 + v, i * H:(i + 1) * H],
                                    lambda a, c: xTs[:, a, c, bass.ds(b * S + (2 * v + i) * P, P)],
                                    lambda r, c: wqkv[:, r, c, 2 * H:3 * H])
                    ins.then_inc(qkv_rdy, 1)

            project(0, True)
            with pe.Fori(1, B) as b:
                project(b, False)

            pe.wait_ge(cst, 20)
            pe.wait_ge(qkv_lo, 6 * B)

            def first_pass(g, k, n, loaded):
                if loaded is not None and n == 0:
                    pe.wait_ge(stk_in[k], loaded)
                if not (isinstance(g, int) and g < 4):
                    pe.wait_ge(s1_max, g - 3)
                bank = ps[:, S1B + (UNITS * k + n) % 4, :]
                for h, i, c in FIRST[n]:
                    w = (i + 1) * P
                    pe.matmul(bank[:, c:c + w], qstk[0:MROW, k, h, i * P:w], kstk[0:MROW, k, h, 0:w], start=True, stop=False)
                    ins = pe.matmul(bank[:, c + i * P:c + w], identb[:, :], maskb[:, 0:P], start=False, stop=True)
                ins.then_inc(s1_rdy, 1)

            def second_pass(g, k, n):
                if not (isinstance(g, int) and g < SRING):
                    pe.wait_ge(exp_done, g - SRING + 1)
                bank = ps[:, S2B + (UNITS * k + n) % SRING, :]
                for h, kt, q, c in SECOND[n]:
                    ins = pe.matmul(bank[:, c:c + S - q], kstk[:, k, h, kt * P:(kt + 1) * P],
                                    qstk[:, k, h, q:S], start=True, stop=True)
                ins.then_inc(s2_rdy, 1)

            def transpose_maxima(pair, k):
                pe.wait_ge(s1_max, UNITS * (pair + 1))
                if not (isinstance(pair, int) and pair < 1):
                    pe.wait_ge(m_lo, pair)
                pe.transpose(ps[0:2 * QT, MB, 0:P], m8[:, k % 2, :], ident[:, :]).then_inc(mT_rdy, 1)

            def times_v(g, u, k, n):
                pair = PAIRS * u + k
                if n in FULL:
                    pe.wait_ge(sel_done, g + 1)
                elif n in POOL_LOW:
                    pe.wait_ge(lo_pool, 2 * (len(POOL_LOW) * pair + POOL_LOW.index(n) + 1))
                else:
                    pe.wait_ge(lo_done, len(DVE_LOW) * pair + DVE_LOW.index(n) + 1)
                if n == 0 and not (isinstance(g, int) and g == 0):
                    pe.wait_ge(pv_cp, PAIRS * u + k)
                slot = (UNITS * k + n) % PRING
                blocks = [(h, kt, q + c2 * P, c + c2 * P) for h, kt, q, c in SECOND[n] for c2 in range((S - q) // P)]
                for e, (h, kt, q, c) in enumerate(blocks):
                    o = (q // P * 2 + h) * VW
                    if n in FULL:
                        ins = pe.matmul(ps[:, PVB, o:o + HD + 1], pf[:, slot, c:c + P],
                                        v32[:, bass.ds(u, 1), V_TILES.index(kt), 2 * k + h, :].rearrange("p o c -> p (o c)"),
                                        start=False, stop=(n == UNITS - 1 and e == len(blocks) - 1), skip_group_check=True)
                        continue
                    for p in (phi, plo):
                        ins = pe.matmul(ps[:, PVB, o:o + VW], p[:, slot, c:c + P],
                                        vst[:, bass.ds(u, 1), kt, 2 * k + h, :].rearrange("p o c -> p (o c)"),
                                        start=(n == 0 and e == 0 and p is phi),
                                        stop=(n == UNITS - 1 and e == len(blocks) - 1 and p is plo),
                                        skip_group_check=True)
                ins.then_inc(pv_done, 1)

            for f in range(AHEAD):
                first_pass(f, f // UNITS, f % UNITS, 32)
                if f in (UNITS - 1, 2 * UNITS - 1):
                    transpose_maxima(f // UNITS, f // UNITS)

            def turn(u, first, last):
                for k in range(PAIRS):
                    pair = PAIRS * u + k
                    for n in range(UNITS):
                        g = TU * u + UNITS * k + n
                        if n == 0:
                            pe.wait_ge(mrow_in[k], 32 * (u + 1))
                        second_pass(g, k, n)
                        u1, k1, n1, f = ahead(u, k, n)
                        if not (last and UNITS * k + n + AHEAD >= TU):
                            first_pass(f, k1, n1, 32 * (u1 + 1))
                        if n == UNITS - 1 and not (last and k >= PAIRS - 2):
                            transpose_maxima(pair + 2, (k + 2) % PAIRS)
                        back = UNITS * k + n - LAG
                        if back >= 0:
                            times_v(TU * u + back, u, back // UNITS, back % UNITS)
                        elif not first:
                            times_v(TU * u + back, u - 1, PAIRS - 1, back % UNITS)

            turn(0, True, False)
            with pe.Fori(1, TURNS - 1) as u:
                turn(u, False, False)
            turn(TURNS - 1, False, True)
            for back in range(TU - LAG, TU):
                times_v(TU * (TURNS - 1) + back, TURNS - 1, PAIRS - 1, back % UNITS)

            pe.wait_ge(nrm_done, PAIRS * TURNS)
            pe.wait_ge(ld_r, 16)
            pe.wait_ge(w_lo, 2)

            def turn_attention(b):
                for c in range(KC):
                    if b > 0:
                        pe.wait_ge(aT_lo, KC * b)
                    for i in range(QT):
                        ins = pe.transpose(ps[:, c, i * P:(i + 1) * P], at[:, 2 * b + c, i, :], ident[:, :])
                    ins.then_inc(aT_rdy, 1)

            def project_out(b):
                pe.wait_ge(aT_lo, KC * (b + 1))
                if b > 0:
                    pe.wait_ge(res_done, 2 * b)
                for g in range(2):
                    for i in range(2 * g, 2 * g + 2):
                        ins = three(ps[:, 2 + g, (i % 2) * H:(i % 2 + 1) * H],
                                    lambda a, c: aT[:, a, c, i * P:(i + 1) * P], lambda r, c: wo[:, r, c, :])
                    ins.then_inc(op_rdy, 1)

            turn_attention(0)
            project_out(0)
            for b in range(B):
                pe.wait_ge(x1_rdy, QT * (b + 1))
                for c in range(KC):
                    if b > 0:
                        pe.wait_ge(x1T_cp, KC * (b - 1) + c + 1)
                    for i in range(QT):
                        ins = pe.transpose(ps[:, 4 + c, i * P:(i + 1) * P], x1[:, QT * b + i, c * P:(c + 1) * P], ident[:, :])
                    ins.then_inc(x1T_rdy, 1)
                if b + 1 < B:
                    turn_attention(b + 1)
                pe.wait_ge(x1T_cp, KC * (b + 1))
                for i in range(QT):
                    for c in range(KC):
                        ins = pe.matmul(ps[:, 6, i * E:(i + 1) * E], x1T[:, c, i * P:(i + 1) * P], rout[:, c, :],
                                        start=(c == 0), stop=(c == KC - 1))
                ins.then_inc(lg_rdy, 1)
                if b + 1 < B:
                    project_out(b + 1)
                pe.wait_ge(any_rdy, b + 1)
                pe.matmul(ps[:, 7, 0:QT * E], before[:, :], anyb[:, :, :].rearrange("p i e -> p (i e)"), start=True, stop=False)
                pe.matmul(ps[:, 7, 0:QT * E], onesb[:, :], excl[:, :, :].rearrange("p i e -> p (i e)"),
                          start=False, stop=True).then_inc(pre_rdy, 1)

            pe.wait_ge(gate_done, B)
            pe.matmul(ps[:, 6, 0:E], onesb[:, :], total[:, :], start=True, stop=True).then_inc(cnt_rdy, 1)
            J = MOE_TILES + 1
            pe.wait_ge(slotT_in, 1)
            pe.transpose(ps[:, 7, 0:J], slotf[0:J, :], ident[0:J, 0:J]).then_inc(slotT, 1)

            pe.wait_ge(wch_lo, ALL_CHUNKS)
            pe.wait_ge(ei_rdy, 1)

            def turn_tokens(j, k, free):
                pe.wait_ge(xg_in[k], 8 * (j - k) + 16)
                if free:
                    pe.wait_ge(xgT_cp, j - 1)
                for c in range(4):
                    ins = pe.transpose(ps[:, k, c * P // 2:(c + 1) * P // 2].bitcast(BF16), xg[:, k, c * P:(c + 1) * P], identb[:, :])
                ins.then_inc(xgT_rdy, 1)

            def through_w1(j, k, e, free):
                pe.wait_ge(xgT_cp, j + 1)
                if free:
                    pe.wait_ge(h_act, j - 1)
                terms = [(a, r, c) for c in range(KC) for a, r in ((0, 0), (0, 1), (1, 0))]
                for f in range(FC):
                    for n, (a, r, c) in enumerate(terms):
                        o = (2 * c + a) * F + f * P
                        ins = pe.matmul(ps[:, 2 + k, f * P:(f + 1) * P],
                                        w1[:, bass.ds(e, 1), o:o + P].rearrange("p o n -> p (o n)"),
                                        xgT[:, k, (r * KC + c) * P:(r * KC + c + 1) * P],
                                        start=(n == 0), stop=(n == len(terms) - 1))
                ins.then_inc(h_rdy, 1)

            def through_w2(j, k, e, free):
                pe.wait_ge(h_lo, j + 1)
                if free:
                    pe.wait_ge(y_cp, j - 1)
                terms = [(c, h, r) for c in range(FC) for h, r in ((hhi, 0), (hhi, 1), (hlo, 0))]
                for n, (c, h, r) in enumerate(terms):
                    o = (2 * c + r) * H
                    ins = pe.matmul(ps[:, 4 + k, 0:H], h[:, k, c * P:(c + 1) * P],
                                    w2[:, bass.ds(e, 1), o:o + H].rearrange("p o n -> p (o n)"),
                                    start=(n == 0), stop=(n == len(terms) - 1))
                ins.then_inc(y_rdy, 1)

            def tile_step(j, k, e0, e1):
                known = isinstance(j, int)
                if not (known and j + 2 >= MOE_TILES):
                    turn_tokens(j + 2, k, True)
                if not (known and j + 1 >= MOE_TILES):
                    through_w1(j + 1, 1 - k, e1, not (known and j < 1))
                through_w2(j, k, e0, not (known and j < 2))

            number = [pe.alloc_register(f"expert{n}") for n in range(STEPS + 1)]

            def experts(j, count):
                pe.load(number[:count], ei[0:1, bass.ds(j + 2, count)])
                return [pe.snap(reg, min_val=0, max_val=E - 1) for reg in number[:count]]

            e = experts(0, 3)
            turn_tokens(0, 0, False)
            turn_tokens(1, 1, False)
            through_w1(0, 0, e[0], False)
            tile_step(0, 0, e[0], e[1])
            tile_step(1, 1, e[1], e[2])
            with pe.Fori(0, (MOE_TILES - 4) // STEPS) as jj:
                e = experts(STEPS * jj + 2, STEPS + 1)
                for n in range(STEPS):
                    tile_step(STEPS * jj + 2 + n, n % 2, e[n], e[n + 1])
            done = 2 + (MOE_TILES - 4) // STEPS * STEPS
            e = experts(done, MOE_TILES - done)
            for n in range(MOE_TILES - done):
                tile_step(done + n, n % 2, e[n], e[min(n + 1, len(e) - 1)])


def kernel(L0_attn_hidden_states, L0_attn_w_qkv, L0_attn_w_o, L0_ffn_router_w, L0_ffn_W1, L0_ffn_W2):
    import numpy as np
    import concourse.bacc as bacc
    from concourse.bass_utils import run_bass_kernel_spmd

    x = np.ascontiguousarray(L0_attn_hidden_states).reshape(T, H)
    arrays = {
        "x_dram": x,
        "xT_dram": np.ascontiguousarray(x.T),
        "wqkvT_dram": np.ascontiguousarray(np.asarray(L0_attn_w_qkv).T),
        "woT_dram": np.ascontiguousarray(np.asarray(L0_attn_w_o).T),
        "router_dram": np.ascontiguousarray(L0_ffn_router_w),
        "W1_dram": np.ascontiguousarray(L0_ffn_W1),
        "W2_dram": np.ascontiguousarray(L0_ffn_W2),
    }
    nc = bacc.Bacc("TRN2", target_bir_lowering=False, num_devices=1)
    args = [nc.dram_tensor(n, a.shape, mybir.dt.from_np(a.dtype), kind="ExternalInput").ap() for n, a in arrays.items()]
    out = nc.dram_tensor("out_dram", (T, H), F32, kind="ExternalOutput").ap()
    post_norm_moe_layer(nc, *args, out)
    r = run_bass_kernel_spmd(nc, [arrays], core_ids=[0])
    return r.results[0]["out_dram"].reshape(B, S, H)
```

```python
from contextlib import ExitStack

import concourse.bass as bass
from concourse import mybir

P = 128
B, S, H = 4, 512, 256
NH, HD = 16, 16
T = B * S
TT = T // P
QT = S // P
KC = H // P
E, F = 16, 512
FC = F // P
TOPK = 2
MOE_TILES = (TOPK * T + E * (P - 1)) // P
SLOT_TILES = T // P + 1
EPS = 1e-5
NEG = -1.0e30

HALF = 8
TURNS = B * NH // HALF
PAIRS = HALF // 2
UNITS = 5
TU = PAIRS * UNITS
ROWS = 4 * HD
MROW = 96
VW = 2 * HD + 1
FULL = (1, 4)
POOL_LOW = (2,)
DVE_LOW = (0, 3)
V_TILES = (1, 3)
LAG = 4
AHEAD = 12
SPLIT_AT = (0, 4)
LOW_LAG = 2
BEHIND = 4
STEPS = 14
PRING = 5
SRING = 2

F32 = mybir.dt.float32
BF16 = mybir.dt.bfloat16
I32 = mybir.dt.int32
U32 = mybir.dt.uint32
ALU = mybir.AluOpType
ACT = mybir.ActivationFunctionType
X = mybir.AxisListType.X

SECOND = [[(0, 0, 0, 0)], [(0, 1, 128, 0), (0, 3, 384, 384)], [(0, 2, 256, 0), (1, 2, 256, 256)],
          [(1, 0, 0, 0)], [(1, 1, 128, 0), (1, 3, 384, 384)]]
FIRST = [[(0, 3, 0)], [(0, 2, 0), (0, 0, 384)], [(0, 1, 0), (1, 1, 256)], [(1, 3, 0)], [(1, 2, 0), (1, 0, 384)]]
W_SLOTS = 3


def post_norm_moe_layer(nc, x, xT, wqkvT, woT, router, W1, W2, out):
    ctx = ExitStack()
    with ctx:
        def sb(name, shape, dt):
            return ctx.enter_context(nc.sbuf_tensor(name, shape, dt))

        def sem(name):
            return ctx.enter_context(nc.semaphore(name))

        q_scr = nc.dram_tensor("q_scr", [TURNS, HALF, ROWS, S], BF16, kind="Internal").ap()
        k_scr = nc.dram_tensor("k_scr", [TURNS, HALF, ROWS, S], BF16, kind="Internal").ap()
        x1_scr = nc.dram_tensor("x1_scr", [T, 2 * H], BF16, kind="Internal").ap()
        slot_scr = nc.dram_tensor("slot_scr", [E * SLOT_TILES * P, 1], I32, kind="Internal").ap()
        y_scr = nc.dram_tensor("y_scr", [TOPK * T + (MOE_TILES + 1) * P, H], F32, kind="Internal").ap()

        w1 = sb("w1", [P, E, KC * 2 * F], BF16)
        w2 = sb("w2", [P, E, FC * 2 * H], BF16)
        ax = sb("ax", [P, T // P * H], F32)
        hold_v = sb("hold_v", [P, TURNS * QT * HALF * VW * 2 // 4], F32)
        hold_q = sb("hold_q", [P, 2048], F32)
        hold_w = sb("hold_w", [P, 3 * KC * F], F32)
        wqkv = sb("wqkv", [P, 2, KC, 3 * H], BF16)
        wo = sb("wo", [P, 2, KC, H], BF16)
        rout = sb("rout", [P, KC, E], F32)
        ident = sb("ident", [P, P], F32)
        identb = sb("identb", [P, P], BF16)
        maskb = sb("maskb", [P, 2 * P], BF16)
        before = sb("before", [P, P], BF16)
        onesb = sb("onesb", [P, P], BF16)
        v32 = sb("v32", [P, TURNS, len(V_TILES), HALF, HD + 1], F32)
        pvs = sb("pvs", [P, 2, 2 * QT, VW], F32)
        onum = sb("onum", [P, 2 * QT, HD], F32)
        orec = sb("orec", [P, 2 * QT], F32)
        m8 = sb("m8", [P, 2, 2 * QT], F32)
        mrow = sb("mrow", [2 * QT, 2, 2, P], BF16)

        late = w2[:, E // 2:, :].rearrange("p e c -> p (e c)")
        xTs = late[:, 0:8192].rearrange("p (a c n) -> p a c n", a=2, c=KC)
        pf = late[:, 0:2 * PRING * 512].bitcast(F32).rearrange("p (r n) -> p r n", r=PRING)
        plo = late[:, 2 * PRING * 512:3 * PRING * 512].rearrange("p (r n) -> p r n", r=PRING)
        phi = late[:, 0:2 * PRING * 512].rearrange("p (r n two) -> p r n two", r=PRING, two=2)[:, :, :, 1]
        wstg = late[:, 8192:8192 + 4096].bitcast(F32)
        wqkv_f = wstg[:, 0:1536].rearrange("p (c n) -> p c n", c=KC)
        wo_f = wstg[:, 1536:2048].rearrange("p (c n) -> p c n", c=KC)
        kstk = late[:, 8192:8192 + 4096].rearrange("p (s h n) -> p s h n", s=PAIRS, h=2)
        ev = late[:, 12288:16384].rearrange("p (m a n) -> p m a n", m=4, a=2)
        qstk = hold_q[:, :].bitcast(BF16).rearrange("p (s h n) -> p s h n", s=PAIRS, h=2)
        xTf = ax[:, :].rearrange("p (c n) -> p c n", c=KC)
        at = ax[:, :].rearrange("p (u i n) -> p u i n", u=TURNS, i=QT)
        x1 = ax[:, :].rearrange("p (t n) -> p t n", t=TT)
        vst = hold_v[:, :].bitcast(BF16).rearrange("p (u k h c) -> p u k h c", u=TURNS, k=QT, h=HALF)
        wchunk = hold_w[:, :].rearrange("p (r n) -> p r n", r=3)

        xres = [v.rearrange("p (i n) -> p i n", i=QT) for v in
                (hold_v[:, 1024:2048], v32[:, :, :, :, :].rearrange("p u k h c -> p (u k h c)")[:, 0:QT * H])]
        aT = hold_v[:, 0:1024].bitcast(BF16).rearrange("p (a c n) -> p a c n", a=2, c=KC)
        r1 = hold_v[:, 2048:3072].rearrange("p (i n) -> p i n", i=QT)
        x1T = hold_v[:, 3072:4096].rearrange("p (c n) -> p c n", c=KC)
        x1hl = hold_q[:, 0:1024].bitcast(BF16).rearrange("p (i n) -> p i n", i=QT)
        xg = hold_q[:, 0:512].bitcast(BF16).rearrange("p (r n) -> p r n", r=2)
        xgT = hold_q[:, 512:1024].bitcast(BF16).rearrange("p (r n) -> p r n", r=2)
        ysb = hold_q[:, 1024:1536].rearrange("p (r n) -> p r n", r=2)
        hw = wqkv[:, :, :, :].rearrange("p a c n -> p (a c n)")
        hf = hw[:, 0:2048].bitcast(F32).rearrange("p (r n) -> p r n", r=2)
        hhi = hw[:, 0:2048].rearrange("p (r n two) -> p r n two", r=2, two=2)[:, :, :, 1]
        hlo = hw[:, 2048:3072].rearrange("p (r n) -> p r n", r=2)
        yg = w1[:, 0:E // 2, :].rearrange("p e c -> p (e c)").bitcast(F32).rearrange(
            "p (b i k n) -> p b i k n", b=B, i=QT, k=TOPK)
        fin = w2[:, 0:E // 4, :].rearrange("p e c -> p (e c)").bitcast(F32).rearrange("p (b i n) -> p b i n", b=B, i=QT)
        fst = hold_w[:, 0:96].rearrange("p (b i c) -> p b i c", b=B, i=QT)
        fmv = hold_w[:, 96:128].rearrange("p (b i c) -> p b i c", b=B, i=QT)
        fve, fsd, frs, fnb = [hold_w[:, 128 + 16 * n:144 + 16 * n].rearrange("p (b i) -> p b i", b=B) for n in range(4)]

        st = sb("st", [P, QT, 6], F32)
        mv = sb("mv", [P, QT, 2], F32)
        ve = sb("ve", [P, QT], F32)
        rstd = sb("rstd", [P, QT], F32)
        warm = sb("warm", [P, 1], F32)
        mhalf = sb("mhalf", [P, QT], F32)
        lg = sb("lg", [P, QT, E], F32)
        top = sb("top", [P, QT, 8], F32)
        topi = sb("topi", [P, QT, 8], U32)
        topf = sb("topf", [P, QT, 2], F32)
        hot = hold_q[:, 1024:1536].rearrange("p (t k e) -> p t k e", t=TT, k=TOPK)
        anyb = sb("anyb", [P, QT, E], BF16)
        excl = sb("excl", [P, QT, E], BF16)
        total = sb("total", [P, E], BF16)
        pree = sb("pree", [P, QT, E], F32)
        prod = hold_q[:, 1536:2048].rearrange("p (t k e) -> p t k e", t=TT, k=TOPK)
        posf = sb("posf", [P, TT, TOPK], F32)
        posu = sb("posu", [P, TT, TOPK], U32)
        gate = sb("gate", [P, TT, TOPK], F32)
        gtmp = sb("gtmp", [P, 2, QT], F32)
        e_i = sb("e_i", [P, E], I32)
        e_f = sb("e_f", [P, E], F32)
        eoff = sb("eoff", [P, E], F32)
        e128 = sb("e128", [P, E], F32)
        j_i = sb("j_i", [P, MOE_TILES + 1], I32)
        j_f = sb("j_f", [P, MOE_TILES + 1], F32)
        tok = sb("tok", [P, TT, TOPK], I32)
        pcol_i = sb("pcol_i", [P, 1], I32)
        pcol = sb("pcol", [P, 1], F32)
        empty_i = sb("empty_i", [P, E * SLOT_TILES], I32)
        ones_f = sb("ones_f", [P, E], F32)
        cnt = sb("cnt", [P, E], F32)
        nt = sb("nt", [P, E], F32)
        binc = sb("binc", [P, E], F32)
        spare = sb("spare", [P, MOE_TILES + 1], F32)
        big = hold_v[:, 3072:3072 + (MOE_TILES + 1) * E]
        ef = sb("ef", [P, MOE_TILES + 1], F32)
        ei = sb("ei", [P, MOE_TILES + 3], I32)
        lep = sb("lep", [P, E], F32)
        used = sb("used", [P, E], F32)
        colf = sb("colf", [P, 4], F32)
        ei_tmp = sb("ei_tmp", [P, MOE_TILES + 1], U32)
        rowu = sb("rowu", [P, 1], U32)
        slots = hold_v[:, 3840:3968].bitcast(I32)
        slotf = hold_v[:, 3968:4096]
        gidx = sb("gidx", [P, MOE_TILES + 1], U32)
        yidx = sb("yidx", [P, MOE_TILES + 1], U32)
        idx1 = sb("idx1", [P, 2], U32)
        idx2 = sb("idx2", [P, 2], U32)

        ps = ctx.enter_context(nc.psum_tensor("ps", [P, 8, 512], F32))
        S1B, S2B, PVB, MB = 0, 4, 6, 7

        ld_w, ld_r, ld_x1 = [sem("ld_w0"), sem("ld_w1")], sem("ld_r"), [sem("ld_x0"), sem("ld_x1")]
        ld_x = [sem(f"ld_xT{b}") for b in range(B)]
        cst = sem("cst")
        cst_v = sem("cst_v")
        empty_out = sem("empty_out")
        w_hi, w_lo, x_hi, x_lo = sem("w_hi"), sem("w_lo"), sem("x_hi"), sem("x_lo")
        qkv_rdy, qkv_hi, qkv_lo = sem("qkv_rdy"), sem("qkv_hi"), sem("qkv_lo")
        ev_out = [sem(f"ev_out{m}") for m in range(4)]
        stk_in = [sem(f"stk_in{k}") for k in range(PAIRS)]
        mrow_in = [sem(f"mrow_in{k}") for k in range(PAIRS)]
        s1_rdy, s1_max = sem("s1_rdy"), sem("s1_max")
        mT_rdy, m_hi, m_lo = sem("mT_rdy"), sem("m_hi"), sem("m_lo")
        s2_rdy, exp_done, sel_done, lo_done, pv_done = (sem("s2_rdy"), sem("exp_done"), sem("sel_done"),
                                                         sem("lo_done"), sem("pv_done"))
        lo_pool = sem("lo_pool")
        pv_cp, nrm_step, nrm_done = sem("pv_cp"), sem("nrm_step"), sem("nrm_done")
        wch_in = [sem(f"wch_in{n}") for n in range(W_SLOTS)]
        wch_hi, wch_lo, late_lo = sem("wch_hi"), sem("wch_lo"), sem("late_lo")
        aT_rdy, aT_hi, aT_lo, op_rdy, res_done, ln_step = (sem("aT_rdy"), sem("aT_hi"), sem("aT_lo"),
                                                           sem("op_rdy"), sem("res_done"), sem("ln_step"))
        var_rdy, rstd_rdy, x1_rdy, x1_hi, x1_lo, x1_out = (sem("var_rdy"), sem("rstd_rdy"), sem("x1_rdy"),
                                                           sem("x1_hi"), sem("x1_lo"), sem("x1_out"))
        x1T_rdy, x1T_cp, lg_rdy, rt = sem("x1T_rdy"), sem("x1T_cp"), sem("lg_rdy"), sem("rt")
        any_rdy, pre_rdy, pos_rdy, gexp_in, gexp, gate_done = (sem("any_rdy"), sem("pre_rdy"), sem("pos_rdy"),
                                                               sem("gexp_in"), sem("gexp"), sem("gate_done"))
        scat = sem("scat")
        cnt_rdy, plan, row_rdy, slot_in, slotT_in, slotT, gidx_rdy, ei_rdy = (
            sem("cnt_rdy"), sem("plan"), sem("row_rdy"), sem("slot_in"), sem("slotT_in"), sem("slotT"),
            sem("gidx_rdy"), sem("ei_rdy"))
        i_cp, go = sem("i_cp"), sem("go")
        xg_in = [sem("xg_in0"), sem("xg_in1")]
        xgT_rdy, xgT_cp, h_rdy, h_act, h_lo, y_rdy, y_cp = (sem("xgT_rdy"), sem("xgT_cp"), sem("h_rdy"), sem("h_act"),
                                                            sem("h_lo"), sem("y_rdy"), sem("y_cp"))
        y_out = [sem("y_out0"), sem("y_out1")]
        i2_cp = sem("i2_cp")
        yg_in = [sem(f"yg_in{b}") for b in range(B)]
        f_rec = sem("f_rec")
        f_scaled, f_sum, f_step, fvar, fstd, fnb_rdy, fin_rdy, fin_out = (
            sem("f_scaled"), sem("f_sum"), sem("f_step"), sem("fvar"), sem("fstd"), sem("fnb_rdy"), sem("fin_rdy"),
            sem("fin_out"))
        yidx_rdy, f_first, fwarm = sem("yidx_rdy"), sem("f_first"), sem("fwarm")

        def ahead(u, k, n):
            f = UNITS * k + n + AHEAD
            return u + f // TU, f // UNITS % PAIRS, f % UNITS, TU * u + f

        ALONE = PAIRS * TURNS - AHEAD // UNITS

        def dve_lows(pair):
            return tuple(sorted(DVE_LOW + FULL)) if isinstance(pair, int) and pair >= ALONE else DVE_LOW

        def lows_done(pair, n):
            more = len(FULL) * (pair - ALONE) if isinstance(pair, int) and pair > ALONE else 0
            return len(DVE_LOW) * pair + more + dve_lows(pair).index(n) + 1

        def w1_views(e, buf):
            return (W1[bass.ds(e, 1)].rearrange("e (c p) n -> p (e c) n", p=P),
                    wchunk[:, buf, :].rearrange("p (c n) -> p c n", n=F),
                    [w1[:, bass.ds(e, 1), :].rearrange("p e (c a n) -> p (e c) a n", a=2, n=F)[:, :, a, :] for a in (0, 1)])

        def w2_views(e, buf):
            return (W2[bass.ds(e, 1)].rearrange("e (c p) n -> p (e c) n", p=P),
                    wchunk[:, buf, :].rearrange("p (c n) -> p c n", n=H),
                    [w2[:, bass.ds(e, 1), :].rearrange("p e (c a n) -> p (e c) a n", a=2, n=H)[:, :, a, :] for a in (0, 1)])

        def matrix(turn, n):
            return w1_views(2 * turn + n, n) if n < 2 else w2_views(turn, n)

        A_CHUNKS = W_SLOTS * TURNS
        assert A_CHUNKS == E + E // 2

        block = ctx.enter_context(nc.Block())

        @block.sync
        def _(sp):
            def fetch(turn, n):
                src, stage, _ = matrix(turn, n)
                sp.dma_start(stage, src).then_inc(wch_in[n], 16)

            sp.dma_start(wqkv_f, wqkvT.rearrange("(c p) n -> p c n", p=P)).then_inc(ld_w[0], 16)
            for b in range(B):
                sp.dma_start(xTf[:, :, b * S:(b + 1) * S],
                             xT.rearrange("(c p) n -> p c n", p=P)[:, :, b * S:(b + 1) * S]).then_inc(ld_x[b], 16)
            sp.dma_start(wo_f, woT.rearrange("(c p) n -> p c n", p=P)).then_inc(ld_w[1], 16)
            sp.dma_start(rout[:, :, :], router.rearrange("(c p) n -> p c n", p=P)).then_inc(ld_r, 16)
            for n in range(W_SLOTS):
                fetch(0, n)
            sp.wait_ge(cst, 1)
            sp.dma_start(slot_scr.rearrange("(p n) o -> p (n o)", p=P), empty_i[:, :]).then_inc(empty_out, 16)

            def store_qk(b):
                for m in range(4):
                    scr = q_scr if m < 2 else k_scr
                    order = "u h (d e a) t -> a (u h d) e t" if m >= 2 else "u h (d a e) t -> a (u h d) e t"
                    dst = scr[bass.ds(2 * b + m % 2, 1)].rearrange(order, d=HD, a=2)
                    sp.wait_ge(qkv_lo, 6 * b + m + 1)
                    for part in range(2):
                        sp.dma_start(dst[part], ev[:, m, part, :].unsqueeze(1).to_broadcast([P, 2, S])).then_inc(ev_out[m], 16)

            with sp.Fori(0, B - 1) as b:
                store_qk(b)

            def load_stack(u, k):
                sp.dma_start(qstk[0:ROWS, k, :, :],
                             q_scr[u, 2 * k:2 * k + 2].rearrange("h r t -> r h t")).then_inc(stk_in[k], 16)
                sp.dma_start(kstk[0:ROWS, k, :, :],
                             k_scr[u, 2 * k:2 * k + 2].rearrange("h r t -> r h t")).then_inc(stk_in[k], 16)

            def load_stack_dyn(u, k):
                for scr, stk in ((q_scr, qstk), (k_scr, kstk)):
                    sp.dma_start(stk[0:ROWS, k, :, :], scr[bass.ds(u, 1), 2 * k:2 * k + 2].rearrange(
                        "u h r t -> r (u h) t")).then_inc(stk_in[k], 16)

            def send_maxima(pair, k):
                sp.wait_ge(m_lo, pair + 1)
                for part in range(2):
                    sp.dma_start(qstk[MROW + part:MROW + part + 1, k, :, :].rearrange("o h (i q) -> o (h i) q", i=QT),
                                 mrow[:, k % 2, part, :]).then_inc(mrow_in[k], 16)

            for m in range(4):
                sp.wait_ge(ev_out[m], 32)
            sp.wait_ge(w_lo, 2)
            for k in range(3):
                load_stack(0, k)
            store_qk(B - 1)
            send_maxima(0, 0)
            for m in range(4):
                sp.wait_ge(ev_out[m], B * 32)

            def turn(u, first, last):
                for k in range(PAIRS):
                    pair = PAIRS * u + k
                    if not (last and k > 0):
                        if k > 0:
                            sp.wait_ge(s2_rdy, UNITS * pair)
                            load_stack_dyn(u + 1, k - 1)
                        else:
                            if not isinstance(u, int) or u > 0:
                                sp.wait_ge(s2_rdy, UNITS * pair)
                            load_stack_dyn(u, PAIRS - 1)
                    if not (last and k == PAIRS - 1):
                        send_maxima(pair + 1, (k + 1) % PAIRS)
                    if k >= 2 and not last:
                        sp.wait_ge(wch_lo, W_SLOTS * u + k - 1)
                        fetch(u + 1, k - 2)
                    elif k == 0 and not first:
                        sp.wait_ge(wch_lo, W_SLOTS * u)
                        fetch(u, W_SLOTS - 1)

            turn(0, True, False)
            with sp.Fori(1, TURNS - 1) as u:
                turn(u, False, False)
            turn(TURNS - 1, False, True)

            def late_fetch(n):
                if n < W_SLOTS:
                    sp.wait_ge(wch_lo, A_CHUNKS - W_SLOTS + n + 1)
                else:
                    m = n - W_SLOTS
                    if m % 2 == 0:
                        sp.wait_ge(wch_lo, A_CHUNKS + m // 2 + 1)
                    else:
                        sp.wait_ge(late_lo, m // 2 + 1)
                src, stage, _ = w2_views(E // 2 + n, n % W_SLOTS)
                sp.dma_start(stage, src).then_inc(wch_in[n % W_SLOTS], 16)

            def residual(b):
                if b > 1:
                    sp.wait_ge(res_done, 2 * (b - 1))
                sp.dma_start(xres[b % 2], x[b * S:(b + 1) * S, :].rearrange("(i p) n -> p i n", p=P)).then_inc(ld_x1[b % 2], 16)

            late_fetch(0)
            late_fetch(1)
            late_fetch(2)
            sp.wait_ge(nrm_done, PAIRS * TURNS)
            residual(0)
            residual(1)
            for b in range(B):
                if b + 2 < B:
                    residual(b + 2)
                sp.wait_ge(x1_lo, b + 1)
                sp.dma_start(x1_scr[b * S:(b + 1) * S, :].rearrange("(i p) n -> p i n", p=P), x1hl).then_inc(x1_out, 16)
                for n in range(W_SLOTS + 2 * b, min(W_SLOTS + 2 * b + 2, E // 2)):
                    late_fetch(n)

            sp.wait_ge(y_out[0], 16 * (MOE_TILES // 2 + 1))
            sp.wait_ge(y_out[1], 16 * (MOE_TILES // 2))
            for b in range(B):
                sp.dma_start(yg[:, b, :, :, :].rearrange("p i k n -> p i (k n)"),
                             y_scr[TOPK * b * S:TOPK * (b + 1) * S, :].rearrange("(i p k) n -> p i (k n)", p=P, k=TOPK)
                             ).then_inc(yg_in[b], 16)
            for b in range(B):
                sp.wait_ge(fin_rdy, b + 1)
                sp.dma_start(out[b * S:(b + 1) * S, :].rearrange("(i p) n -> p i n", p=P),
                             fin[:, b, :, :]).then_inc(fin_out, 16)
            sp.wait_ge(fin_out, 16 * B)

        @block.gpsimd
        def _(pool):
            n = [0]

            def made(ins):
                ins.then_inc(cst, 1)
                n[0] += 1
                pool.wait_ge(cst, n[0])

            made(pool.memset(empty_i[:, :], TOPK * T))
            made(pool.memset(ident[:, :], 0.0))
            made(pool.affine_select(ident[:, :], ident[:, :], [[-1, P]], ALU.not_equal, 1.0, base=0, channel_multiplier=1))
            made(pool.tensor_copy(identb[:, :], ident[:, :]))
            made(pool.memset(onesb[:, :], 1.0))
            made(pool.memset(ones_f[:, :], 1.0))
            made(pool.memset(maskb[:, :], 0.0))
            made(pool.affine_select(maskb[:, :], maskb[:, :], [[0, 2], [-1, P]], ALU.is_ge, NEG, base=0, channel_multiplier=1))
            made(pool.affine_select(before[:, :], onesb[:, :], [[1, P]], ALU.is_gt, 0.0, base=0, channel_multiplier=-1))
            made(pool.iota(e_i[:, :], [[1, E]], base=0, channel_multiplier=0))
            made(pool.iota(j_i[:, :], [[1, MOE_TILES + 1]], base=0, channel_multiplier=0))
            made(pool.iota(tok[:, :, :], [[TOPK * P, TT], [1, TOPK]], base=0, channel_multiplier=TOPK))
            made(pool.iota(pcol_i[:, :], [[1, 1]], base=0, channel_multiplier=1))
            made(pool.memset(mhalf[:, :], -0.5))
            made(pool.memset(total[:, :], 0.0))
            made(pool.memset(vst.rearrange("p u k h c -> p (u k h) c")[:, :, HD:HD + 1], 1.0))
            made(pool.memset(v32[:, :, :, :, :].rearrange("p u k h c -> p (u k h) c")[:, :, HD:HD + 1], 1.0))
            pool.wait_ge(w_lo, 2)
            made(pool.memset(kstk[ROWS:P, :, :, :], 0.0))
            made(pool.memset(kstk[MROW:MROW + 2, :, :, :], 1.0))
            made(pool.memset(qstk[ROWS:P, :, :, :], 0.0))

            def diagonal(u, slot, unit):
                cols = [c for _, _, _, c in SECOND[unit]]
                pool.wait_ge(exp_done, u + 1)
                pool.sem_inc(go, 1)
                if len(cols) == 1:
                    v, pat = pf[:, slot, 0:P], [[1, P]]
                else:
                    v = pf[:, slot, :].rearrange("p (b q) -> p b q", q=P)[:, 0:cols[1] // P + 1:cols[1] // P, :]
                    pat = [[0, 2], [1, P]]
                ins = pool.affine_select(v, v, pat, ALU.is_ge, 0.0, base=0, channel_multiplier=-1)
                ins.then_inc(sel_done, 1)

            def probabilities_low(u, slot, half):
                if half == 0:
                    pool.wait_ge(sel_done, u + 1)
                s = slice(256 * half, 256 * half + 256)
                pool.tensor_tensor(plo[:, slot, s], pf[:, slot, s], phi[:, slot, s], ALU.subtract).then_inc(lo_pool, 1)

            def split_low(views, c, halves=(0, 1)):
                _, stage, (high, low) = views
                mid = stage.shape[1] // 2
                pool.wait_ge(wch_hi, c + 1)
                s = slice(mid * halves[0], mid * (halves[-1] + 1))
                ins = pool.tensor_tensor(low[:, s], stage[:, s], high[:, s], ALU.subtract)
                if halves[-1] == 1:
                    ins.then_inc(wch_lo, 1)

            with pool.Fori(0, TURNS) as u:
                for k in range(PAIRS):
                    for unit in range(UNITS):
                        g = TU * u + UNITS * k + unit
                        diagonal(g, (UNITS * k + unit) % PRING, unit)
                        if unit in POOL_LOW:
                            probabilities_low(g, (UNITS * k + unit) % PRING, 0)
                        if unit - 1 in POOL_LOW:
                            probabilities_low(g - 1, (UNITS * k + unit - 1) % PRING, 1)
                        if k > 0 and unit in SPLIT_AT:
                            split_low(matrix(u, k - 1), W_SLOTS * u + k - 1, (SPLIT_AT.index(unit),))

            def late_low(n):
                split_low(w2_views(E // 2 + n, n % W_SLOTS), A_CHUNKS + n)

            def norm_factor(b):
                pool.wait_ge(var_rdy, b + 1)
                pool.tensor_tensor(rstd[:, :], ve[:, :], mhalf[:, :], ALU.pow).then_inc(rstd_rdy, 1)

            def place_tokens(b):
                pool.wait_ge(pos_rdy, b + 1)
                for i in range(QT):
                    for k in range(TOPK):
                        t = QT * b + i
                        pool.indirect_dma_start(slot_scr, bass.IndirectOffsetOnAxis(ap=posu[:, t, k:k + 1], axis=0),
                                                tok[:, t, k:k + 1], None).then_inc(scat, 16)

            pool.wait_ge(empty_out, 16)
            norm_factor(0)
            for b in range(B):
                if b + 1 < B:
                    norm_factor(b + 1)
                late_low(2 * b)
                place_tokens(b)
            pool.wait_ge(row_rdy, 1)
            pool.wait_ge(scat, 16 * TT * TOPK)
            pool.indirect_dma_start(slots[0:MOE_TILES + 1, :], None, slot_scr.rearrange("(r n) o -> r (n o)", n=P),
                                    bass.IndirectOffsetOnAxis(ap=rowu[0:MOE_TILES + 1, 0:1], axis=0)).then_inc(slot_in, 16)
            pool.wait_ge(gidx_rdy, 1)
            pool.wait_ge(yidx_rdy, 1)
            pool.wait_ge(x1_out, 16 * B)

            def gather(j, k, first):
                if not first:
                    pool.wait_ge(xgT_rdy, j - 1)
                    pool.wait_ge(xg_in[k], 16 * (j // 2) if isinstance(j, int) else 8 * (j - k))
                pool.tensor_copy(idx1[:, k:k + 1], gidx[:, bass.ds(j, 1)]).then_inc(i_cp, 1)
                pool.wait_ge(i_cp, j + 1)
                pool.sem_inc(go, 1)
                pool.indirect_dma_start(xg[:, k, :], None, x1_scr,
                                        bass.IndirectOffsetOnAxis(ap=idx1[:, k:k + 1], axis=0)).then_inc(xg_in[k], 16)

            def scatter(j, k):
                if not (isinstance(j, int) and j < 2):
                    pool.wait_ge(y_out[k], 8 * (j - k))
                pool.tensor_copy(idx2[:, k:k + 1], yidx[:, bass.ds(j, 1)]).then_inc(i2_cp, 1)
                pool.wait_ge(i2_cp, j + 1)
                pool.wait_ge(y_cp, j + 1)
                pool.sem_inc(go, 1)
                pool.indirect_dma_start(y_scr, bass.IndirectOffsetOnAxis(ap=idx2[:, k:k + 1], axis=0),
                                        ysb[:, k, :], None).then_inc(y_out[k], 16)

            for j in range(6):
                gather(j, j % 2, j < 2)
                if j >= BEHIND:
                    scatter(j - BEHIND, j % 2)
            with pool.Fori(3, MOE_TILES // 2) as jj:
                for k in range(2):
                    gather(2 * jj + k, k, False)
                    scatter(2 * jj + k - BEHIND, k)
            gather(MOE_TILES - 1, 0, False)
            for j in range(MOE_TILES - 1 - BEHIND, MOE_TILES):
                scatter(j, j % 2)

            for b in range(1, B):
                pool.wait_ge(f_scaled, b)
                pool.tensor_tensor(yg[:, b, :, 0, :], yg[:, b, :, 0, :], x1[:, QT * b:QT * (b + 1), :],
                                   ALU.add).then_inc(f_sum, 1)

        @block.scalar
        def _(act):
            act.wait_ge(ld_w[0], 16)
            act.copy(wqkv[:, 0, :, :], wqkv_f).then_inc(w_hi, 1)
            for b in range(B):
                if b == 1:
                    act.wait_ge(ld_w[1], 16)
                    act.copy(wo[:, 0, :, :], wo_f).then_inc(w_hi, 1)
                act.wait_ge(ld_x[b], 16)
                act.copy(xTs[:, 0, :, b * S:(b + 1) * S], xTf[:, :, b * S:(b + 1) * S]).then_inc(x_hi, 1)
            def high_parts(b, first):
                for m in range(4):
                    act.wait_ge(qkv_rdy, 6 * b + m + 1)
                    if not first:
                        act.wait_ge(ev_out[m], 32 * b)
                    act.copy(ev[:, m, 0, :], ps[:, m, :]).then_inc(qkv_hi, 1)
                for v in range(2):
                    act.wait_ge(qkv_rdy, 6 * b + 4 + v + 1)
                    for i in range(2):
                        if 2 * v + i in V_TILES:
                            act.copy(v32[:, bass.ds(2 * b, 2), V_TILES.index(2 * v + i), :, 0:HD],
                                     ps[:, 4 + v, i * H:(i + 1) * H].rearrange("p (f h d) -> p f h d", f=2, d=HD))
                    for i in range(2):
                        ins = act.copy(vst[:, bass.ds(2 * b, 2), 2 * v + i, :, 0:HD],
                                       ps[:, 4 + v, i * H:(i + 1) * H].rearrange("p (f h d) -> p f h d", f=2, d=HD))
                    ins.then_inc(qkv_hi, 1)

            high_parts(0, True)
            with act.Fori(1, B) as b:
                high_parts(b, False)

            def maxima_high(pair, k, free):
                act.wait_ge(mT_rdy, pair + 1)
                if free is not None:
                    act.wait_ge(mrow_in[(k - 2) % PAIRS], free)
                act.mul(mrow[:, k % 2, 0, :], ps[0:2 * QT, MB, 0:P], -1.0).then_inc(m_hi, 1)

            def pv_copy(pair, k):
                act.wait_ge(pv_done, UNITS * (pair + 1))
                if not (isinstance(pair, int) and pair < 2):
                    act.wait_ge(nrm_done, pair - 1)
                act.copy(pvs[:, k % 2, :, :], ps[:, PVB, 0:2 * QT * VW].rearrange("p (a c) -> p a c", c=VW)).then_inc(pv_cp, 1)

            maxima_high(0, 0, None)
            maxima_high(1, 1, None)

            def turn(u, first, last):
                for k in range(PAIRS):
                    pair = PAIRS * u + k
                    for n in range(UNITS):
                        g = TU * u + UNITS * k + n
                        if n == LAG and not (first and k == 0):
                            pv_copy(pair - 1, (k - 1) % PAIRS)
                        act.wait_ge(s2_rdy, g + 1)
                        if not (first and g < PRING):
                            act.wait_ge(pv_done, g - PRING + 1)
                        act.activation(pf[:, (UNITS * k + n) % PRING, :], ps[:, S2B + (UNITS * k + n) % SRING, :],
                                       ACT.Exp, scale=1.0 / HD ** 0.5).then_inc(exp_done, 1)
                        if n == UNITS - 1 and not (last and k >= PAIRS - 2):
                            maxima_high(pair + 2, (k + 2) % PAIRS, 32 * (u + 1))
                    if k < W_SLOTS:
                        act.wait_ge(wch_in[k], 16 * (u + 1))
                        _, stage, (high, _) = matrix(u, k)
                        act.copy(high, stage).then_inc(wch_hi, 1)

            turn(0, True, False)
            with act.Fori(1, TURNS - 1) as u:
                turn(u, False, False)
            turn(TURNS - 1, False, True)
            pv_copy(PAIRS * TURNS - 1, PAIRS - 1)

            def attention_high(b):
                for c in range(KC):
                    act.wait_ge(aT_rdy, KC * b + c + 1)
                    act.wait_ge(op_rdy, 2 * b)
                    act.copy(aT[:, 0, c, :], ps[:, c, :]).then_inc(aT_hi, 1)

            attention_high(0)
            attention_high(1)
            for b in range(B):
                act.wait_ge(x1_rdy, QT * (b + 1))
                if b > 0:
                    act.wait_ge(x1_out, 16 * b)
                act.copy(x1hl[:, :, 0:H], x1[:, QT * b:QT * (b + 1), :]).then_inc(x1_hi, 1)
                for c in range(KC):
                    act.wait_ge(x1T_rdy, KC * b + c + 1)
                    act.copy(x1T[:, c, :], ps[:, 4 + c, :]).then_inc(x1T_cp, 1)
                if b + 2 < B:
                    attention_high(b + 2)
                act.wait_ge(gexp_in, b + 1)
                act.activation(gtmp[:, 1, :], gtmp[:, 0, :], ACT.Exp).then_inc(gexp, 1)
                for n in (2 * b, 2 * b + 1):
                    act.wait_ge(wch_in[n % W_SLOTS], 16 * (TURNS + n // W_SLOTS + 1))
                    act.wait_ge(pv_done, TU * TURNS)
                    _, stage, (high, _) = w2_views(E // 2 + n, n % W_SLOTS)
                    act.copy(high, stage).then_inc(wch_hi, 1)

            def expert_tile(j, k, free):
                act.wait_ge(h_rdy, j + 1)
                if free:
                    act.wait_ge(y_rdy, j - 1)
                act.activation(hf[:, k, :], ps[:, 2 + k, :], ACT.Silu).then_inc(h_act, 1)

            def result(j, k, free):
                act.wait_ge(y_rdy, j + 1)
                if free:
                    act.wait_ge(y_out[k], 8 * (j - k))
                act.copy(ysb[:, k, :], ps[:, 4 + k, 0:H]).then_inc(y_cp, 1)

            expert_tile(0, 0, False)
            expert_tile(1, 1, False)
            result(0, 0, False)
            expert_tile(2, 0, True)
            result(1, 1, False)
            with act.Fori(1, MOE_TILES // 2) as jj:
                expert_tile(2 * jj + 1, 1, True)
                result(2 * jj, 0, True)
                expert_tile(2 * jj + 2, 0, True)
                result(2 * jj + 1, 1, True)
            result(MOE_TILES - 1, 0, True)

            def scale_first(b):
                act.wait_ge(yg_in[b], 16)
                for i in range(QT):
                    ins = act.activation(yg[:, b, i, 0, :], yg[:, b, i, 0, :], ACT.Copy, scale=gate[:, QT * b + i, 0:1])
                ins.then_inc(f_scaled, 1)

            act.sqrt(warm[:, :], ones_f[:, 0:1]).then_inc(fwarm, 1)
            for b in range(1, 3):
                scale_first(b)
            def deviation(b):
                act.wait_ge(fvar, b + 1)
                act.sqrt(fsd[:, b, :], fve[:, b, :]).then_inc(fstd, 1)

            deviation(0)
            scale_first(3)
            for b in range(B):
                if b + 1 < B:
                    deviation(b + 1)
                act.wait_ge(fnb_rdy, b + 1)
                for i in range(QT):
                    ins = act.activation(fin[:, b, i, :], fin[:, b, i, :], ACT.Identity, scale=frs[:, b, i:i + 1],
                                         bias=fnb[:, b, i:i + 1])
                ins.then_inc(fin_rdy, 1)

        @block.vector
        def _(dve):
            dve.wait_ge(w_hi, 1)
            dve.tensor_tensor(wqkv[:, 1, :, :], wqkv_f, wqkv[:, 0, :, :], ALU.subtract).then_inc(w_lo, 1)
            for b in range(B):
                if b == 1:
                    dve.wait_ge(w_hi, 2)
                    dve.tensor_tensor(wo[:, 1, :, :], wo_f, wo[:, 0, :, :], ALU.subtract).then_inc(w_lo, 1)
                dve.wait_ge(x_hi, b + 1)
                s = slice(b * S, (b + 1) * S)
                dve.tensor_tensor(xTs[:, 1, :, s], xTf[:, :, s], xTs[:, 0, :, s], ALU.subtract).then_inc(x_lo, 1)
            dve.wait_ge(cst, 16)
            dve.tensor_copy(e_f[:, :], e_i[:, :]).then_inc(cst_v, 1)
            dve.tensor_copy(j_f[:, :], j_i[:, :]).then_inc(cst_v, 1)
            dve.tensor_copy(pcol[:, :], pcol_i[:, :]).then_inc(cst_v, 1)
            dve.wait_ge(cst_v, 3)
            dve.tensor_scalar(eoff[:, :], e_f[:, :], float(SLOT_TILES * P), None, ALU.mult).then_inc(cst_v, 1)
            dve.tensor_scalar(e128[:, :], e_f[:, :], float(P), None, ALU.mult).then_inc(cst_v, 1)
            dve.scalar_tensor_tensor(spare[:, :], j_f[:, :], float(P), pcol[:, 0:1].to_broadcast([P, MOE_TILES + 1]),
                                     ALU.mult, ALU.add).then_inc(cst_v, 1)
            with dve.Fori(0, B) as b:
                for m in range(4):
                    dve.wait_ge(qkv_hi, 6 * b + m + 1)
                    dve.tensor_tensor(ev[:, m, 1, :], ps[:, m, :], ev[:, m, 0, :], ALU.subtract).then_inc(qkv_lo, 1)
                for v in range(2):
                    dve.wait_ge(qkv_hi, 6 * b + 4 + v + 1)
                    for i in range(2):
                        vs = vst[:, bass.ds(2 * b, 2), 2 * v + i, :, :]
                        ins = dve.tensor_tensor(vs[:, :, :, HD + 1:VW],
                                                ps[:, 4 + v, i * H:(i + 1) * H].rearrange("p (f h d) -> p f h d", f=2, d=HD),
                                                vs[:, :, :, 0:HD], ALU.subtract)
                    ins.then_inc(qkv_lo, 1)

            def unit_max(g, k, n, wait_m8):
                dve.wait_ge(s1_rdy, g + 1)
                if n == 0 and wait_m8 is not None:
                    dve.wait_ge(mT_rdy, wait_m8)
                bank = S1B + (UNITS * k + n) % 4
                m = m8[:, k % 2, :]
                if n == 2:
                    ins = dve.tensor_reduce(m.rearrange("p (h i) -> p h i", i=QT)[:, :, 1],
                                            ps[:, bank, :].rearrange("p (h n) -> p h n", h=2), X, ALU.max)
                else:
                    for h, i, c in FIRST[n]:
                        ins = dve.tensor_reduce(m[:, h * QT + i:h * QT + i + 1], ps[:, bank, c:c + (i + 1) * P], X, ALU.max)
                ins.then_inc(s1_max, 1)

            def maxima_low(pair, k):
                dve.wait_ge(m_hi, pair + 1)
                dve.scalar_tensor_tensor(mrow[:, k % 2, 1, :], ps[0:2 * QT, MB, 0:P], -1.0, mrow[:, k % 2, 0, :],
                                         ALU.mult, ALU.subtract).then_inc(m_lo, 1)

            def low_part(g, slot):
                dve.wait_ge(sel_done, g + 1)
                dve.tensor_tensor(plo[:, slot, :], pf[:, slot, :], phi[:, slot, :], ALU.subtract).then_inc(lo_done, 1)

            def normalise(pair, u, k):
                dve.wait_ge(pv_cp, pair + 1)
                if not (isinstance(pair, int) and pair == 0):
                    dve.wait_ge(nrm_done, pair)
                v = pvs[:, k % 2, :, :]
                dve.reciprocal(orec[:, :], v[:, :, HD]).then_inc(nrm_step, 1)
                dve.tensor_tensor(onum[:, :, :], v[:, :, 0:HD], v[:, :, HD + 1:VW], ALU.add).then_inc(nrm_step, 1)
                dve.wait_ge(nrm_step, 2 * pair + 2)
                dst = at[:, bass.ds(u, 1), :, 2 * k * HD:2 * (k + 1) * HD].rearrange("p u i (h d) -> p (u i) h d", d=HD)
                dve.tensor_tensor(dst, onum[:, :, :].rearrange("p (i h) d -> p i h d", h=2),
                                  orec[:, :].rearrange("p (i h) -> p i h", h=2).unsqueeze(3).to_broadcast([P, QT, 2, HD]),
                                  ALU.mult).then_inc(nrm_done, 1)

            for f in range(AHEAD):
                unit_max(f, f // UNITS, f % UNITS, f // UNITS - 1 if f >= 2 * UNITS else None)
                if f == UNITS - 1:
                    maxima_low(0, 0)

            def turn(u, first, last):
                for k in range(PAIRS):
                    pair = PAIRS * u + k
                    for n in range(UNITS):
                        g = TU * u + UNITS * k + n
                        _, k1, n1, f = ahead(u, k, n)
                        if not (last and UNITS * k + n + AHEAD >= TU):
                            unit_max(f, k1, n1, pair + (n + AHEAD) // UNITS - 1)
                        if n == 0 and not (last and k == PAIRS - 1):
                            maxima_low(pair + 1, (k + 1) % PAIRS)
                        back = UNITS * k + n - LOW_LAG
                        if back % UNITS in dve_lows(PAIRS * u + back // UNITS) and not (first and back < 0):
                            low_part(TU * u + back, back % PRING)
                        if n == UNITS - 1 and not (first and k == 0):
                            normalise(pair - 1, u if k > 0 else u - 1, (k - 1) % PAIRS)

            turn(0, True, False)
            with dve.Fori(1, TURNS - 1) as u:
                turn(u, False, False)
            turn(TURNS - 1, False, True)
            for back in range(TU - LOW_LAG, TU):
                if back % UNITS in dve_lows(PAIRS * TURNS - 1):
                    low_part(TU * (TURNS - 1) + back, back % PRING)
            normalise(PAIRS * TURNS - 1, TURNS - 1, PAIRS - 1)

            kr = [0]

            def chain(ins):
                kr[0] += 1
                ins.then_inc(rt, 1)
                dve.wait_ge(rt, kr[0])

            def attention_low(b):
                for c in range(KC):
                    dve.wait_ge(aT_hi, KC * b + c + 1)
                    dve.tensor_tensor(aT[:, 1, c, :], ps[:, c, :], aT[:, 0, c, :], ALU.subtract).then_inc(aT_lo, 1)

            def residual(b):
                dve.wait_ge(ld_x1[b % 2], 16 * (b // 2 + 1))
                for g in range(2):
                    dve.wait_ge(op_rdy, 2 * b + g + 1)
                    dve.tensor_tensor(r1[:, 2 * g:2 * g + 2, :], ps[:, 2 + g, :].rearrange("p (i n) -> p i n", i=2),
                                      xres[b % 2][:, 2 * g:2 * g + 2, :], ALU.add).then_inc(res_done, 1)
                for i in range(QT):
                    if i % 2 == 0:
                        dve.wait_ge(res_done, 2 * b + i // 2 + 1)
                    dve.bn_stats(st[:, i, :], r1[:, i, :]).then_inc(ln_step, 1)
                for i in range(QT):
                    dve.wait_ge(ln_step, 2 * QT * b + i + 1)
                    dve.bn_aggr(mv[:, i, :], st[:, i, :]).then_inc(ln_step, 1)
                dve.wait_ge(ln_step, 2 * QT * (b + 1))
                dve.tensor_scalar(ve[:, :], mv[:, :, 1], EPS, None, ALU.add).then_inc(var_rdy, 1)

            def late_low(n):
                dve.wait_ge(wch_hi, A_CHUNKS + n + 1)
                _, stage, (high, low) = w2_views(E // 2 + n, n % W_SLOTS)
                dve.tensor_tensor(low, stage, high, ALU.subtract).then_inc(late_lo, 1)

            attention_low(0)
            residual(0)
            attention_low(1)
            for b in range(B):
                tiles = slice(QT * b, QT * (b + 1))
                dve.wait_ge(rstd_rdy, b + 1)
                for i in range(QT):
                    dve.tensor_scalar(x1[:, QT * b + i, :], r1[:, i, :], mv[:, i, 0:1], rstd[:, i:i + 1],
                                      ALU.subtract, ALU.mult).then_inc(x1_rdy, 1)
                if b + 1 < B:
                    dve.wait_ge(x1_rdy, QT * (b + 1))
                    residual(b + 1)
                dve.wait_ge(x1_hi, b + 1)
                dve.tensor_tensor(x1hl[:, :, H:2 * H], x1[:, tiles, :], x1hl[:, :, 0:H], ALU.subtract).then_inc(x1_lo, 1)
                if b + 2 < B:
                    attention_low(b + 2)
                dve.wait_ge(lg_rdy, b + 1)
                chain(dve.tensor_copy(lg[:, :, :], ps[:, 6, 0:QT * E].rearrange("p (i e) -> p i e", e=E)))
                for i in range(QT):
                    ins = dve.max(top[:, i, :], lg[:, i, :])
                chain(ins)
                if b > 0:
                    dve.wait_ge(gexp, b)
                dve.tensor_tensor(gtmp[:, 0, :], top[:, :, 1], top[:, :, 0], ALU.subtract).then_inc(gexp_in, 1)
                for i in range(QT):
                    ins = dve.max_index(topi[:, i, :], top[:, i, :], lg[:, i, :])
                chain(ins)
                chain(dve.tensor_copy(topf[:, :, :], topi[:, :, 0:2]))
                hb = hot[:, tiles, :, :]
                for i in range(TOPK):
                    ins = dve.tensor_tensor(hb[:, :, i, :], e_f[:, :].unsqueeze(1).to_broadcast([P, QT, E]),
                                            topf[:, :, i:i + 1].to_broadcast([P, QT, E]), ALU.is_equal)
                chain(ins)
                chain(dve.tensor_tensor(anyb[:, :, :], hb[:, :, 0, :], hb[:, :, 1, :], ALU.add))
                chain(dve.tensor_copy(excl[:, 0, :], total[:, :]))
                for i in range(1, QT):
                    chain(dve.tensor_tensor(excl[:, i, :], excl[:, i - 1, :], anyb[:, i - 1, :], ALU.add))
                dve.tensor_tensor(total[:, :], excl[:, QT - 1, :], anyb[:, QT - 1, :], ALU.add).then_inc(any_rdy, 1)
                dve.wait_ge(gexp, b + 1)
                chain(dve.tensor_scalar(gtmp[:, 0, :], gtmp[:, 1, :], 1.0, None, ALU.add))
                chain(dve.reciprocal(gate[:, tiles, 0], gtmp[:, 0, :]))
                dve.tensor_tensor(gate[:, tiles, 1], gate[:, tiles, 0], gtmp[:, 1, :], ALU.mult).then_inc(gate_done, 1)
                dve.wait_ge(pre_rdy, b + 1)
                chain(dve.tensor_tensor(pree[:, :, :], ps[:, 7, 0:QT * E].rearrange("p (i e) -> p i e", e=E),
                                        eoff[:, :].unsqueeze(1).to_broadcast([P, QT, E]), ALU.add))
                for i in range(TOPK):
                    ins = dve.tensor_tensor(prod[:, 0:QT, i, :], hb[:, :, i, :], pree[:, :, :], ALU.mult)
                chain(ins)
                chain(dve.tensor_reduce(posf[:, tiles, :], prod[:, 0:QT, :, :], X, ALU.add))
                dve.tensor_copy(posu[:, tiles, :], posf[:, tiles, :]).then_inc(pos_rdy, 1)
                if b + 1 < B:
                    late_low(2 * b + 1)

            kk = [0]

            def step(ins):
                kk[0] += 1
                ins.then_inc(plan, 1)
                dve.wait_ge(plan, kk[0])

            J = MOE_TILES + 1
            dve.wait_ge(cnt_rdy, 1)
            step(dve.tensor_copy(cnt[:, :], ps[:, 6, 0:E]))
            cmp = big[:, 0:E * E].rearrange("p (e m) -> p e m", m=E)
            step(dve.tensor_tensor(cmp, cnt[:, :].unsqueeze(2).to_broadcast([P, E, E]),
                                   e128[:, :].unsqueeze(1).to_broadcast([P, E, E]), ALU.is_gt))
            step(dve.tensor_reduce(nt[:, :], cmp, X, ALU.add))
            step(dve.tensor_tensor_scan(binc[:, :], ones_f[:, :], nt[:, :], 0.0, ALU.mult, ALU.add))
            step(dve.tensor_scalar(lep[:, :], binc[:, :], pcol[:, 0:1], None, ALU.is_le))
            dve.tensor_reduce(colf[:, 0:1], lep[:, :], X, ALU.add).then_inc(plan, 1)
            kk[0] += 1
            step(dve.tensor_tensor(used[:, :], lep[:, :], nt[:, :], ALU.mult))
            step(dve.tensor_reduce(colf[:, 1:2], used[:, :], X, ALU.add))
            step(dve.tensor_scalar(colf[:, 2:3], colf[:, 0:1], float(E - 1), float(SLOT_TILES), ALU.min, ALU.mult))
            step(dve.tensor_tensor(colf[:, 3:4], pcol[:, :], colf[:, 1:2], ALU.subtract))
            step(dve.tensor_scalar(colf[:, 3:4], colf[:, 3:4], float(SLOT_TILES - 1), None, ALU.min))
            dve.tensor_tensor(rowu[:, :], colf[:, 2:3], colf[:, 3:4], ALU.add).then_inc(row_rdy, 1)
            le = big[:, :].rearrange("p (j e) -> p j e", e=E)
            step(dve.tensor_tensor(le, binc[:, :].unsqueeze(1).to_broadcast([P, J, E]),
                                   j_f[:, :].unsqueeze(2).to_broadcast([P, J, E]), ALU.is_le))
            step(dve.tensor_reduce(ef[:, :], le, X, ALU.add))
            dve.tensor_scalar(ei[:, 2:], ef[:, :], float(E - 1), None, ALU.min).then_inc(ei_rdy, 1)
            late_low(E // 2 - 1)
            dve.wait_ge(slot_in, 16)
            dve.tensor_copy(slotf[0:J, :], slots[0:J, :]).then_inc(slotT_in, 1)
            dve.wait_ge(slotT, 1)
            step(dve.tensor_scalar(ei_tmp[:, :], ps[:, 7, 0:J], float(TOPK * T - 1), None, ALU.min))
            dve.tensor_scalar(gidx[:, :], ei_tmp[:, :], 1, None, ALU.logical_shift_right).then_inc(gidx_rdy, 1)
            step(dve.scalar_tensor_tensor(ef[:, :], ps[:, 7, 0:J], float(TOPK * T), spare[:, :], ALU.is_ge, ALU.mult))
            dve.tensor_tensor(yidx[:, :], ef[:, :], ps[:, 7, 0:J], ALU.add).then_inc(yidx_rdy, 1)

            def tokens(j, k, free):
                dve.wait_ge(xgT_rdy, j + 1)
                if free:
                    dve.wait_ge(h_rdy, j - 1)
                dve.tensor_copy(xgT[:, k, :], ps[:, k, 0:256].bitcast(BF16)).then_inc(xgT_cp, 1)

            def hidden(j, k):
                dve.wait_ge(h_act, j + 1)
                dve.tensor_tensor(hlo[:, k, :], hf[:, k, :], hhi[:, k, :], ALU.subtract).then_inc(h_lo, 1)

            tokens(0, 0, False)
            tokens(1, 1, False)
            hidden(0, 0)
            tokens(2, 0, True)
            with dve.Fori(0, MOE_TILES // 2 - 1) as jj:
                hidden(2 * jj + 1, 1)
                tokens(2 * jj + 3, 1, True)
                hidden(2 * jj + 2, 0)
                tokens(2 * jj + 4, 0, True)
            hidden(MOE_TILES - 2, 1)
            hidden(MOE_TILES - 1, 0)

            def scale_and_shift(b):
                dve.wait_ge(fstd, b + 1)
                dve.reciprocal(frs[:, b, :], fsd[:, b, :]).then_inc(f_rec, 1)
                dve.wait_ge(f_rec, b + 1)
                dve.scalar_tensor_tensor(fnb[:, b, :], fmv[:, b, :, 0], -1.0, frs[:, b, :],
                                         ALU.mult, ALU.mult).then_inc(fnb_rdy, 1)

            for b in range(B):
                f = fin[:, b, :, :]
                s0 = 3 * QT * b
                if b == 0:
                    dve.wait_ge(yg_in[b], 16)
                    for i in range(QT):
                        dve.scalar_tensor_tensor(yg[:, b, i, 0, :], yg[:, b, i, 0, :], gate[:, i, 0:1], x1[:, i, :],
                                                 ALU.mult, ALU.add).then_inc(f_first, 1)
                    dve.wait_ge(f_first, QT)
                else:
                    dve.wait_ge(f_sum, b)
                for i in range(QT):
                    dve.scalar_tensor_tensor(f[:, i, :], yg[:, b, i, 1, :], gate[:, QT * b + i, 1:2], yg[:, b, i, 0, :],
                                             ALU.mult, ALU.add).then_inc(f_step, 1)
                for i in range(QT):
                    dve.wait_ge(f_step, s0 + i + 1)
                    dve.bn_stats(fst[:, b, i, :], f[:, i, :]).then_inc(f_step, 1)
                for i in range(QT):
                    dve.wait_ge(f_step, s0 + QT + i + 1)
                    dve.bn_aggr(fmv[:, b, i, :], fst[:, b, i, :]).then_inc(f_step, 1)
                dve.wait_ge(f_step, s0 + 3 * QT)
                dve.tensor_scalar(fve[:, b, :], fmv[:, b, :, 1], EPS, None, ALU.add).then_inc(fvar, 1)
                if b > 0:
                    scale_and_shift(b - 1)
            scale_and_shift(B - 1)

        @block.tensor
        def _(pe):
            def three(dst, lhsT, rhs, first=True, last=True):
                terms = [(a, r, c) for c in range(KC) for a, r in ((0, 0), (0, 1), (1, 0))]
                for n, (a, r, c) in enumerate(terms):
                    ins = pe.matmul(dst, lhsT(a, c), rhs(r, c), start=(n == 0), stop=(n == len(terms) - 1))
                return ins

            pe.wait_ge(w_lo, 1)
            def project(b, first):
                pe.wait_ge(x_lo, b + 1)
                cols = bass.ds(b * S, S)
                for m in range(4):
                    if not first:
                        pe.wait_ge(qkv_lo, 6 * b + m - 5)
                    three(ps[:, m, :], lambda a, c: wqkv[:, a, c, m * P:(m + 1) * P],
                          lambda r, c: xTs[:, r, c, cols]).then_inc(qkv_rdy, 1)
                for v in range(2):
                    if not first:
                        pe.wait_ge(qkv_lo, 6 * b + 4 + v - 5)
                    for i in range(2):
                        ins = three(ps[:, 4 + v, i * H:(i + 1) * H],
                                    lambda a, c: xTs[:, a, c, bass.ds(b * S + (2 * v + i) * P, P)],
                                    lambda r, c: wqkv[:, r, c, 2 * H:3 * H])
                    ins.then_inc(qkv_rdy, 1)

            project(0, True)
            with pe.Fori(1, B) as b:
                project(b, False)

            pe.wait_ge(cst, 20)
            pe.wait_ge(qkv_lo, 6 * B)

            def first_pass(g, k, n, loaded):
                if loaded is not None and n == 0:
                    pe.wait_ge(stk_in[k], loaded)
                if not (isinstance(g, int) and g < 4):
                    pe.wait_ge(s1_max, g - 3)
                bank = ps[:, S1B + (UNITS * k + n) % 4, :]
                for h, i, c in FIRST[n]:
                    w = (i + 1) * P
                    pe.matmul(bank[:, c:c + w], qstk[0:MROW, k, h, i * P:w], kstk[0:MROW, k, h, 0:w], start=True, stop=False)
                    ins = pe.matmul(bank[:, c + i * P:c + w], identb[:, :], maskb[:, 0:P], start=False, stop=True)
                ins.then_inc(s1_rdy, 1)

            def second_pass(g, k, n):
                if not (isinstance(g, int) and g < SRING):
                    pe.wait_ge(exp_done, g - SRING + 1)
                bank = ps[:, S2B + (UNITS * k + n) % SRING, :]
                for h, kt, q, c in SECOND[n]:
                    ins = pe.matmul(bank[:, c:c + S - q], kstk[:, k, h, kt * P:(kt + 1) * P],
                                    qstk[:, k, h, q:S], start=True, stop=True)
                ins.then_inc(s2_rdy, 1)

            def transpose_maxima(pair, k):
                pe.wait_ge(s1_max, UNITS * (pair + 1))
                if not (isinstance(pair, int) and pair < 1):
                    pe.wait_ge(m_lo, pair)
                pe.transpose(ps[0:2 * QT, MB, 0:P], m8[:, k % 2, :], ident[:, :]).then_inc(mT_rdy, 1)

            def times_v(g, u, k, n):
                pair = PAIRS * u + k
                full = n in FULL and n not in dve_lows(pair)
                if full:
                    pe.wait_ge(sel_done, g + 1)
                elif n in POOL_LOW:
                    pe.wait_ge(lo_pool, 2 * (len(POOL_LOW) * pair + POOL_LOW.index(n) + 1))
                else:
                    pe.wait_ge(lo_done, lows_done(pair, n))
                if n == 0 and not (isinstance(g, int) and g == 0):
                    pe.wait_ge(pv_cp, PAIRS * u + k)
                slot = (UNITS * k + n) % PRING
                blocks = [(h, kt, q + c2 * P, c + c2 * P) for h, kt, q, c in SECOND[n] for c2 in range((S - q) // P)]
                for e, (h, kt, q, c) in enumerate(blocks):
                    o = (q // P * 2 + h) * VW
                    if full:
                        ins = pe.matmul(ps[:, PVB, o:o + HD + 1], pf[:, slot, c:c + P],
                                        v32[:, bass.ds(u, 1), V_TILES.index(kt), 2 * k + h, :].rearrange("p o c -> p (o c)"),
                                        start=False, stop=(n == UNITS - 1 and e == len(blocks) - 1), skip_group_check=True)
                        continue
                    for p in (phi, plo):
                        ins = pe.matmul(ps[:, PVB, o:o + VW], p[:, slot, c:c + P],
                                        vst[:, bass.ds(u, 1), kt, 2 * k + h, :].rearrange("p o c -> p (o c)"),
                                        start=(n == 0 and e == 0 and p is phi),
                                        stop=(n == UNITS - 1 and e == len(blocks) - 1 and p is plo),
                                        skip_group_check=True)
                ins.then_inc(pv_done, 1)

            for f in range(AHEAD):
                first_pass(f, f // UNITS, f % UNITS, 32)
                if f in (UNITS - 1, 2 * UNITS - 1):
                    transpose_maxima(f // UNITS, f // UNITS)

            def turn(u, first, last):
                for k in range(PAIRS):
                    pair = PAIRS * u + k
                    for n in range(UNITS):
                        g = TU * u + UNITS * k + n
                        if n == 0:
                            pe.wait_ge(mrow_in[k], 32 * (u + 1))
                        second_pass(g, k, n)
                        u1, k1, n1, f = ahead(u, k, n)
                        if not (last and UNITS * k + n + AHEAD >= TU):
                            first_pass(f, k1, n1, 32 * (u1 + 1))
                        if n == UNITS - 1 and not (last and k >= PAIRS - 2):
                            transpose_maxima(pair + 2, (k + 2) % PAIRS)
                        back = UNITS * k + n - LAG
                        if back >= 0:
                            times_v(TU * u + back, u, back // UNITS, back % UNITS)
                        elif not first:
                            times_v(TU * u + back, u - 1, PAIRS - 1, back % UNITS)

            turn(0, True, False)
            with pe.Fori(1, TURNS - 1) as u:
                turn(u, False, False)
            turn(TURNS - 1, False, True)
            for back in range(TU - LAG, TU):
                times_v(TU * (TURNS - 1) + back, TURNS - 1, PAIRS - 1, back % UNITS)

            pe.wait_ge(nrm_done, PAIRS * TURNS)
            pe.wait_ge(ld_r, 16)
            pe.wait_ge(w_lo, 2)

            def turn_attention(b):
                for c in range(KC):
                    if b > 0:
                        pe.wait_ge(aT_lo, KC * b)
                    for i in range(QT):
                        ins = pe.transpose(ps[:, c, i * P:(i + 1) * P], at[:, 2 * b + c, i, :], ident[:, :])
                    ins.then_inc(aT_rdy, 1)

            def project_out(b):
                pe.wait_ge(aT_lo, KC * (b + 1))
                if b > 0:
                    pe.wait_ge(res_done, 2 * b)
                for g in range(2):
                    for i in range(2 * g, 2 * g + 2):
                        ins = three(ps[:, 2 + g, (i % 2) * H:(i % 2 + 1) * H],
                                    lambda a, c: aT[:, a, c, i * P:(i + 1) * P], lambda r, c: wo[:, r, c, :])
                    ins.then_inc(op_rdy, 1)

            turn_attention(0)
            project_out(0)
            turn_attention(1)
            project_out(1)
            for b in range(B):
                pe.wait_ge(x1_rdy, QT * (b + 1))
                for c in range(KC):
                    if b > 0:
                        pe.wait_ge(x1T_cp, KC * (b - 1) + c + 1)
                    for i in range(QT):
                        ins = pe.transpose(ps[:, 4 + c, i * P:(i + 1) * P], x1[:, QT * b + i, c * P:(c + 1) * P], ident[:, :])
                    ins.then_inc(x1T_rdy, 1)
                if b + 2 < B:
                    turn_attention(b + 2)
                pe.wait_ge(x1T_cp, KC * (b + 1))
                for i in range(QT):
                    for c in range(KC):
                        ins = pe.matmul(ps[:, 6, i * E:(i + 1) * E], x1T[:, c, i * P:(i + 1) * P], rout[:, c, :],
                                        start=(c == 0), stop=(c == KC - 1))
                ins.then_inc(lg_rdy, 1)
                if b + 2 < B:
                    project_out(b + 2)
                pe.wait_ge(any_rdy, b + 1)
                pe.matmul(ps[:, 7, 0:QT * E], before[:, :], anyb[:, :, :].rearrange("p i e -> p (i e)"), start=True, stop=False)
                pe.matmul(ps[:, 7, 0:QT * E], onesb[:, :], excl[:, :, :].rearrange("p i e -> p (i e)"),
                          start=False, stop=True).then_inc(pre_rdy, 1)

            pe.wait_ge(gate_done, B)
            pe.matmul(ps[:, 6, 0:E], onesb[:, :], total[:, :], start=True, stop=True).then_inc(cnt_rdy, 1)
            J = MOE_TILES + 1
            pe.wait_ge(slotT_in, 1)
            pe.transpose(ps[:, 7, 0:J], slotf[0:J, :], ident[0:J, 0:J]).then_inc(slotT, 1)

            pe.wait_ge(wch_lo, A_CHUNKS + E // 4)
            pe.wait_ge(late_lo, E // 4)
            pe.wait_ge(ei_rdy, 1)

            def turn_tokens(j, k, free):
                pe.wait_ge(xg_in[k], 8 * (j - k) + 16)
                if free:
                    pe.wait_ge(xgT_cp, j - 1)
                for c in range(4):
                    ins = pe.transpose(ps[:, k, c * P // 2:(c + 1) * P // 2].bitcast(BF16),
                                       xg[:, k, c * P:(c + 1) * P], identb[:, :])
                ins.then_inc(xgT_rdy, 1)

            def through_w1(j, k, e, free):
                pe.wait_ge(xgT_cp, j + 1)
                if free:
                    pe.wait_ge(h_act, j - 1)
                terms = [(a, r, c) for c in range(KC) for a, r in ((0, 0), (0, 1), (1, 0))]
                for f in range(FC):
                    for n, (a, r, c) in enumerate(terms):
                        o = (2 * c + a) * F + f * P
                        ins = pe.matmul(ps[:, 2 + k, f * P:(f + 1) * P],
                                        w1[:, bass.ds(e, 1), o:o + P].rearrange("p o n -> p (o n)"),
                                        xgT[:, k, (r * KC + c) * P:(r * KC + c + 1) * P],
                                        start=(n == 0), stop=(n == len(terms) - 1))
                ins.then_inc(h_rdy, 1)

            def through_w2(j, k, e, free):
                pe.wait_ge(h_lo, j + 1)
                if free:
                    pe.wait_ge(y_cp, j - 1)
                terms = [(c, h, r) for c in range(FC) for h, r in ((hhi, 0), (hhi, 1), (hlo, 0))]
                for n, (c, h, r) in enumerate(terms):
                    o = (2 * c + r) * H
                    ins = pe.matmul(ps[:, 4 + k, 0:H], h[:, k, c * P:(c + 1) * P],
                                    w2[:, bass.ds(e, 1), o:o + H].rearrange("p o n -> p (o n)"),
                                    start=(n == 0), stop=(n == len(terms) - 1))
                ins.then_inc(y_rdy, 1)

            def tile_step(j, k, e0, e1):
                known = isinstance(j, int)
                if not (known and j + 2 >= MOE_TILES):
                    turn_tokens(j + 2, k, True)
                if not (known and j + 1 >= MOE_TILES):
                    through_w1(j + 1, 1 - k, e1, not (known and j < 1))
                through_w2(j, k, e0, not (known and j < 2))

            number = [pe.alloc_register(f"expert{n}") for n in range(STEPS + 1)]

            def experts(j, count):
                pe.load(number[:count], ei[0:1, bass.ds(j + 2, count)])
                return [pe.snap(reg, min_val=0, max_val=E - 1) for reg in number[:count]]

            e = experts(0, 3)
            turn_tokens(0, 0, False)
            turn_tokens(1, 1, False)
            through_w1(0, 0, e[0], False)
            tile_step(0, 0, e[0], e[1])
            tile_step(1, 1, e[1], e[2])
            with pe.Fori(0, (MOE_TILES - 4) // STEPS) as jj:
                e = experts(STEPS * jj + 2, STEPS + 1)
                for n in range(STEPS):
                    tile_step(STEPS * jj + 2 + n, n % 2, e[n], e[n + 1])
            done = 2 + (MOE_TILES - 4) // STEPS * STEPS
            e = experts(done, MOE_TILES - done)
            for n in range(MOE_TILES - done):
                tile_step(done + n, n % 2, e[n], e[min(n + 1, len(e) - 1)])


def kernel(L0_attn_hidden_states, L0_attn_w_qkv, L0_attn_w_o, L0_ffn_router_w, L0_ffn_W1, L0_ffn_W2):
    import numpy as np
    import concourse.bacc as bacc
    from concourse.bass_utils import run_bass_kernel_spmd

    x = np.ascontiguousarray(L0_attn_hidden_states).reshape(T, H)
    arrays = {
        "x_dram": x,
        "xT_dram": np.ascontiguousarray(x.T),
        "wqkvT_dram": np.ascontiguousarray(np.asarray(L0_attn_w_qkv).T),
        "woT_dram": np.ascontiguousarray(np.asarray(L0_attn_w_o).T),
        "router_dram": np.ascontiguousarray(L0_ffn_router_w),
        "W1_dram": np.ascontiguousarray(L0_ffn_W1),
        "W2_dram": np.ascontiguousarray(L0_ffn_W2),
    }
    nc = bacc.Bacc("TRN2", target_bir_lowering=False, num_devices=1)
    args = [nc.dram_tensor(n, a.shape, mybir.dt.from_np(a.dtype), kind="ExternalInput").ap() for n, a in arrays.items()]
    out = nc.dram_tensor("out_dram", (T, H), F32, kind="ExternalOutput").ap()
    post_norm_moe_layer(nc, *args, out)
    r = run_bass_kernel_spmd(nc, [arrays], core_ids=[0])
    return r.results[0]["out_dram"].reshape(B, S, H)
```
